# Optimizing a Trainium2 kernel written in Bass

```python
import numpy as np
import jax
import jax.numpy as jnp

def _softmax(x, axis=-1):
    return jax.nn.softmax(x, axis=axis)

def _gelu(x):
    return jax.nn.gelu(x, approximate=True)

def _silu(x):
    return jax.nn.silu(x)

def _sigmoid(x):
    return jax.nn.sigmoid(x)

def _layernorm(x, axis=-1, eps=1e-05):
    m = jnp.mean(x, axis=axis, keepdims=True)
    v = jnp.var(x, axis=axis, keepdims=True)
    return (x - m) / jnp.sqrt(v + eps)

def _scatter_add(tgt, idx, src, axis=0):
    return tgt.at[idx].add(src)

def _segment_sum(src, seg, n):
    return jax.ops.segment_sum(src, seg, n)
kernel_name = 'mk_lm_tower_d2_tok_ids2048_r4_947042'

def setup_inputs(seed: int=0):
    np.random.seed(seed)
    _w = jnp.asarray

    def _rec_inputs():
        import jax
        import jax.numpy as jnp
        _rk = jax.random.key(seed)
        x = jax.random.randint(jax.random.fold_in(_rk, 1), (16, 128), 0, 128, jnp.int32)
        return x
    x = _rec_inputs()

    def _L0_tok_setup():
        import jax, jax.numpy as jnp
        import numpy as np
        VOCAB = 128
        D_VIS = 512
        D_TXT = 512
        EPS = 1e-06
        VOCAB_OFFSET = 0

        def rms_norm(x, weight, eps):
            xf = x.astype(jnp.float32)
            var = jnp.mean(xf * xf, axis=-1, keepdims=True)
            normed = xf * jax.lax.rsqrt(var + eps)
            if weight is not None:
                normed = normed * weight.astype(jnp.float32)
            return normed.astype(x.dtype)
        key = jax.random.key(seed)
        k_ids, k_emb, k_w, k_proj = jax.random.split(key, 4)
        input_ids = jax.random.randint(k_ids, (8, 1024), 0, VOCAB, dtype=jnp.int64)
        emb_table = jax.random.normal(k_emb, (VOCAB, D_VIS), dtype=jnp.float32) * 0.02
        norm_weight = jnp.ones((D_VIS,), dtype=jnp.float32) + 0.01 * jax.random.normal(k_w, (D_VIS,), dtype=jnp.float32)
        proj_weight = jax.random.normal(k_proj, (D_TXT, D_VIS), dtype=jnp.float32) * 0.02
        return {'input_ids': input_ids, 'emb_table': emb_table, 'norm_weight': norm_weight, 'proj_weight': proj_weight}
    _L0_tok_all = _L0_tok_setup()
    _L0_tok_in = {k: v for k, v in _L0_tok_all.items() if k in ('emb_table', 'norm_weight', 'proj_weight')}
    del _L0_tok_all

    def _L0_attn_setup():
        import jax, jax.numpy as jnp
        import numpy as np
        D_MODEL, N_HEADS, D_STATE, N_GROUPS, CHUNK = (512, 32, 64, 1, 64)
        BATCH, SEQLEN = (2, 1024)

        def segsum(v):
            cs = jnp.cumsum(v, axis=-1)
            seg = cs[..., :, None] - cs[..., None, :]
            T = v.shape[-1]
            mask = jnp.tril(jnp.ones((T, T), bool))
            return jnp.where(mask, seg, -jnp.inf)

        def _ssd(x, A_log, D, B_w, B_b, C_w, C_b, dt_w, dt_b, out_w, out_b):
            b, t, d = x.shape
            h = A_log.shape[0]
            n = B_w.shape[0] // N_GROUPS
            p = d // h
            l = CHUNK
            c = t // l
            A = -jnp.exp(A_log.astype(jnp.float32))
            B = (x @ B_w.T + B_b).reshape(b, t, N_GROUPS, n)
            C = (x @ C_w.T + C_b).reshape(b, t, N_GROUPS, n)
            B = jnp.broadcast_to(B, (b, t, h, n))
            C = jnp.broadcast_to(C, (b, t, h, n))
            dt = jax.nn.softplus(x @ dt_w.T + dt_b)
            xh = x.reshape(b, t, h, p)
            xc = xh.reshape(b, c, l, h, p)
            Bc = B.reshape(b, c, l, h, n)
            Cc = C.reshape(b, c, l, h, n)
            dtc = dt.reshape(b, c, l, h)
            dA = jnp.transpose(dtc * A, (0, 3, 1, 2))
            A_cumsum = jnp.cumsum(dA, axis=-1)
            L = jnp.exp(segsum(dA))
            xdt = xc * dtc[..., None]
            Y_diag = jnp.einsum('bclhn,bcshn,bhcls,bcshp->bclhp', Cc, Bc, L, xdt)
            decay_states = jnp.exp(A_cumsum[..., -1:] - A_cumsum)
            states = jnp.einsum('bclhn,bhcl,bclhp->bchpn', Bc, decay_states, xdt)
            states = jnp.concatenate([jnp.zeros_like(states[:, :1]), states], axis=1)
            dA_last = jnp.pad(A_cumsum[..., -1], ((0, 0), (0, 0), (1, 0)))
            decay_chunk = jnp.exp(segsum(dA_last))
            new_states = jnp.einsum('bhzc,bchpn->bzhpn', decay_chunk, states)
            prev_states = new_states[:, :-1]
            state_decay_out = jnp.exp(A_cumsum)
            Y_off = jnp.einsum('bclhn,bchpn,bhcl->bclhp', Cc, prev_states, state_decay_out)
            Y = (Y_diag + Y_off).reshape(b, t, h, p) + D[None, None, :, None] * xh
            return Y.reshape(b, t, d) @ out_w.T + out_b
        key = jax.random.key(seed)
        ks = jax.random.split(key, 8)
        s = 0.02
        d, h, n, g = (D_MODEL, N_HEADS, D_STATE, N_GROUPS)
        return {'x': jax.random.normal(ks[0], (BATCH, SEQLEN, d), jnp.float32), 'A_log': jnp.log(jnp.arange(1, h + 1, dtype=jnp.float32)), 'D': jnp.ones((h,), jnp.float32), 'B_w': jax.random.normal(ks[1], (g * n, d), jnp.float32) * s, 'B_b': jnp.zeros((g * n,), jnp.float32), 'C_w': jax.random.normal(ks[2], (g * n, d), jnp.float32) * s, 'C_b': jnp.zeros((g * n,), jnp.float32), 'dt_w': jax.random.normal(ks[3], (h, d), jnp.float32) * s, 'dt_b': jnp.zeros((h,), jnp.float32), 'out_w': jax.random.normal(ks[4], (d, d), jnp.float32) * s, 'out_b': jnp.zeros((d,), jnp.float32)}
    _L0_attn_all = _L0_attn_setup()
    _L0_attn_in = {k: v for k, v in _L0_attn_all.items() if k in ('A_log', 'D', 'B_w', 'B_b', 'C_w', 'C_b', 'dt_w', 'dt_b', 'out_w', 'out_b')}
    del _L0_attn_all

    def _L0_ffn_setup():
        import jax, jax.numpy as jnp
        import numpy as np
        HIDDEN = 512
        INTER = 1376
        LUT_SIZE = 16

        def _ghost_linear(x, idx, lut):
            w = lut[idx]
            return jnp.einsum('bsh,oh->bso', x, w)
        key = jax.random.key(seed)
        k_x, k_lut, k_g, k_u, k_d = jax.random.split(key, 5)
        x = jax.random.normal(k_x, (2, 1024, HIDDEN), dtype=jnp.float32)
        lut = jax.random.normal(k_lut, (LUT_SIZE,), dtype=jnp.float32) * 0.02
        gate_idx = jax.random.randint(k_g, (INTER, HIDDEN), 0, LUT_SIZE, dtype=jnp.int32)
        up_idx = jax.random.randint(k_u, (INTER, HIDDEN), 0, LUT_SIZE, dtype=jnp.int32)
        down_idx = jax.random.randint(k_d, (HIDDEN, INTER), 0, LUT_SIZE, dtype=jnp.int32)
        return {'x': x, 'lut': lut, 'gate_idx': gate_idx, 'up_idx': up_idx, 'down_idx': down_idx}
    _L0_ffn_all = _L0_ffn_setup()
    _L0_ffn_in = {k: v for k, v in _L0_ffn_all.items() if k in ('lut', 'gate_idx', 'up_idx', 'down_idx')}
    del _L0_ffn_all

    def _L1_attn_setup():
        import jax, jax.numpy as jnp
        import numpy as np
        D_MODEL = 512
        N_HEADS = 16
        HEAD_DIM = D_MODEL // N_HEADS
        KV_LORA = 128
        Q_LORA = 192
        ROPE_DIM = 64
        EPS = 1e-06

        def _rmsnorm(x, g):
            var = jnp.mean(x * x, axis=-1, keepdims=True)
            return x * jax.lax.rsqrt(var + EPS) * g

        def _rope(t):
            d = t.shape[-1]
            s = t.shape[-2]
            inv_freq = 1.0 / 10000.0 ** (jnp.arange(0, d, 2, dtype=jnp.float32) / d)
            ang = jnp.arange(s, dtype=jnp.float32)[:, None] * inv_freq[None, :]
            cos = jnp.concatenate([jnp.cos(ang), jnp.cos(ang)], axis=-1)
            sin = jnp.concatenate([jnp.sin(ang), jnp.sin(ang)], axis=-1)
            t1, t2 = (t[..., :d // 2], t[..., d // 2:])
            rot = jnp.concatenate([-t2, t1], axis=-1)
            return t * cos + rot * sin
        key = jax.random.key(seed)
        ks = jax.random.split(key, 12)
        sc = 0.02
        inp = {'x': jax.random.normal(ks[0], (2, 512, D_MODEL), dtype=jnp.float32), 'Wcq': jax.random.normal(ks[1], (D_MODEL, Q_LORA), dtype=jnp.float32) * sc, 'g_q': jnp.ones((Q_LORA,), dtype=jnp.float32), 'Wdq': jax.random.normal(ks[2], (Q_LORA, N_HEADS * HEAD_DIM), dtype=jnp.float32) * sc, 'Wdqr': jax.random.normal(ks[3], (Q_LORA, N_HEADS * ROPE_DIM), dtype=jnp.float32) * sc, 'Wckv': jax.random.normal(ks[4], (D_MODEL, KV_LORA), dtype=jnp.float32) * sc, 'g_kv': jnp.ones((KV_LORA,), dtype=jnp.float32), 'Wdk': jax.random.normal(ks[5], (KV_LORA, N_HEADS * HEAD_DIM), dtype=jnp.float32) * sc, 'Wdv': jax.random.normal(ks[6], (KV_LORA, N_HEADS * HEAD_DIM), dtype=jnp.float32) * sc, 'Wkr': jax.random.normal(ks[7], (D_MODEL, ROPE_DIM), dtype=jnp.float32) * sc, 'Wo': jax.random.normal(ks[8], (N_HEADS * HEAD_DIM, D_MODEL), dtype=jnp.float32) * sc}
        return inp
    _L1_attn_all = _L1_attn_setup()
    _L1_attn_in = {k: v for k, v in _L1_attn_all.items() if k in ('Wcq', 'g_q', 'Wdq', 'Wdqr', 'Wckv', 'g_kv', 'Wdk', 'Wdv', 'Wkr', 'Wo')}
    del _L1_attn_all

    def _L1_ffn_setup():
        import jax, jax.numpy as jnp
        import numpy as np
        B, T, D = (1, 512, 512)
        E, K, F = (64, 4, 128)
        S, SF = (2, 128 * 4)
        CAP = 64

        def _moe_forward(x, router_w, router_bias, gate_w, up_w, down_w, sh_gate_w, sh_up_w, sh_down_w):
            b, t, d = x.shape
            flat = x.reshape(b * t, d)
            N = flat.shape[0]
            logits = flat @ router_w.T
            scores = jax.nn.softmax(logits, axis=-1)
            _, topk_idx = jax.lax.top_k(logits + router_bias, K)
            topk_w = jnp.take_along_axis(scores, topk_idx, axis=-1)
            topk_w = topk_w / topk_w.sum(axis=-1, keepdims=True)
            P = N * K
            e_flat = topk_idx.reshape(-1)
            t_flat = jnp.repeat(jnp.arange(N), K)
            w_flat = topk_w.reshape(-1)
            order = jnp.argsort(e_flat)
            e_s, t_s, w_s = (e_flat[order], t_flat[order], w_flat[order])
            counts = jnp.bincount(e_s, length=E)
            starts = jnp.concatenate([jnp.zeros((1,), counts.dtype), jnp.cumsum(counts)[:-1]])
            pos = jnp.arange(P) - starts[e_s]
            slot = jnp.where(pos < CAP, pos, CAP)
            tok_table = jnp.zeros((E, CAP + 1), jnp.int32).at[e_s, slot].set(t_s)[:, :CAP]
            w_table = jnp.zeros((E, CAP + 1), w_s.dtype).at[e_s, slot].set(w_s)[:, :CAP]
            xg = flat[tok_table]
            g = jnp.einsum('ecd,efd->ecf', xg, gate_w)
            u = jnp.einsum('ecd,efd->ecf', xg, up_w)
            y = jnp.einsum('ecf,edf->ecd', jax.nn.silu(g) * u, down_w)
            out = jnp.zeros_like(flat).at[tok_table.reshape(-1)].add((y * w_table[..., None]).reshape(-1, d))
            sg = jnp.einsum('nd,sfd->nsf', flat, sh_gate_w)
            su = jnp.einsum('nd,sfd->nsf', flat, sh_up_w)
            out = out + jnp.einsum('nsf,sdf->nd', jax.nn.silu(sg) * su, sh_down_w)
            return out.reshape(b, t, d)
        key = jax.random.key(seed)
        ks = jax.random.split(key, 9)
        s = 0.02
        return {'x': jax.random.normal(ks[0], (B, T, D), jnp.float32), 'router_w': jax.random.normal(ks[1], (E, D), jnp.float32) * s, 'router_bias': jnp.zeros((E,), jnp.float32), 'gate_w': jax.random.normal(ks[2], (E, F, D), jnp.float32) * s, 'up_w': jax.random.normal(ks[3], (E, F, D), jnp.float32) * s, 'down_w': jax.random.normal(ks[4], (E, D, F), jnp.float32) * s, 'sh_gate_w': jax.random.normal(ks[5], (S, SF, D), jnp.float32) * s, 'sh_up_w': jax.random.normal(ks[6], (S, SF, D), jnp.float32) * s, 'sh_down_w': jax.random.normal(ks[7], (S, D, SF), jnp.float32) * s}
    _L1_ffn_all = _L1_ffn_setup()
    _L1_ffn_in = {k: v for k, v in _L1_ffn_all.items() if k in ('router_w', 'router_bias', 'gate_w', 'up_w', 'down_w', 'sh_gate_w', 'sh_up_w', 'sh_down_w')}
    del _L1_ffn_all
    return {'x': x, 'L0_tok_emb_table': _L0_tok_in['emb_table'], 'L0_tok_norm_weight': _L0_tok_in['norm_weight'], 'L0_tok_proj_weight': _L0_tok_in['proj_weight'], 'L0_attn_A_log': _L0_attn_in['A_log'], 'L0_attn_D': _L0_attn_in['D'], 'L0_attn_B_w': _L0_attn_in['B_w'], 'L0_attn_B_b': _L0_attn_in['B_b'], 'L0_attn_C_w': _L0_attn_in['C_w'], 'L0_attn_C_b': _L0_attn_in['C_b'], 'L0_attn_dt_w': _L0_attn_in['dt_w'], 'L0_attn_dt_b': _L0_attn_in['dt_b'], 'L0_attn_out_w': _L0_attn_in['out_w'], 'L0_attn_out_b': _L0_attn_in['out_b'], 'L0_ffn_lut': _L0_ffn_in['lut'], 'L0_ffn_gate_idx': _L0_ffn_in['gate_idx'], 'L0_ffn_up_idx': _L0_ffn_in['up_idx'], 'L0_ffn_down_idx': _L0_ffn_in['down_idx'], 'L1_attn_Wcq': _L1_attn_in['Wcq'], 'L1_attn_g_q': _L1_attn_in['g_q'], 'L1_attn_Wdq': _L1_attn_in['Wdq'], 'L1_attn_Wdqr': _L1_attn_in['Wdqr'], 'L1_attn_Wckv': _L1_attn_in['Wckv'], 'L1_attn_g_kv': _L1_attn_in['g_kv'], 'L1_attn_Wdk': _L1_attn_in['Wdk'], 'L1_attn_Wdv': _L1_attn_in['Wdv'], 'L1_attn_Wkr': _L1_attn_in['Wkr'], 'L1_attn_Wo': _L1_attn_in['Wo'], 'L1_ffn_router_w': _L1_ffn_in['router_w'], 'L1_ffn_router_bias': _L1_ffn_in['router_bias'], 'L1_ffn_gate_w': _L1_ffn_in['gate_w'], 'L1_ffn_up_w': _L1_ffn_in['up_w'], 'L1_ffn_down_w': _L1_ffn_in['down_w'], 'L1_ffn_sh_gate_w': _L1_ffn_in['sh_gate_w'], 'L1_ffn_sh_up_w': _L1_ffn_in['sh_up_w'], 'L1_ffn_sh_down_w': _L1_ffn_in['sh_down_w']}

def reference(x, L0_tok_emb_table, L0_tok_norm_weight, L0_tok_proj_weight, L0_attn_A_log, L0_attn_D, L0_attn_B_w, L0_attn_B_b, L0_attn_C_w, L0_attn_C_b, L0_attn_dt_w, L0_attn_dt_b, L0_attn_out_w, L0_attn_out_b, L0_ffn_lut, L0_ffn_gate_idx, L0_ffn_up_idx, L0_ffn_down_idx, L1_attn_Wcq, L1_attn_g_q, L1_attn_Wdq, L1_attn_Wdqr, L1_attn_Wckv, L1_attn_g_kv, L1_attn_Wdk, L1_attn_Wdv, L1_attn_Wkr, L1_attn_Wo, L1_ffn_router_w, L1_ffn_router_bias, L1_ffn_gate_w, L1_ffn_up_w, L1_ffn_down_w, L1_ffn_sh_gate_w, L1_ffn_sh_up_w, L1_ffn_sh_down_w):
    import jax
    import jax.numpy as jnp

    def _L0_tok_ref(input_ids, emb_table, norm_weight, proj_weight):
        import jax, jax.numpy as jnp
        import numpy as np
        VOCAB = 128
        D_VIS = 512
        D_TXT = 512
        EPS = 1e-06
        VOCAB_OFFSET = 0

        def rms_norm(x, weight, eps):
            xf = x.astype(jnp.float32)
            var = jnp.mean(xf * xf, axis=-1, keepdims=True)
            normed = xf * jax.lax.rsqrt(var + eps)
            if weight is not None:
                normed = normed * weight.astype(jnp.float32)
            return normed.astype(x.dtype)
        hard_emb = emb_table[input_ids - VOCAB_OFFSET]
        hard_emb_norm = rms_norm(hard_emb, norm_weight, EPS)
        proj = jnp.einsum('bsd,ed->bse', hard_emb_norm, proj_weight)
        return rms_norm(proj, None, EPS)

    def _L0_attn_ref(x, A_log, D, B_w, B_b, C_w, C_b, dt_w, dt_b, out_w, out_b):
        import jax, jax.numpy as jnp
        import numpy as np
        D_MODEL, N_HEADS, D_STATE, N_GROUPS, CHUNK = (512, 32, 64, 1, 64)
        BATCH, SEQLEN = (2, 1024)

        def segsum(v):
            cs = jnp.cumsum(v, axis=-1)
            seg = cs[..., :, None] - cs[..., None, :]
            T = v.shape[-1]
            mask = jnp.tril(jnp.ones((T, T), bool))
            return jnp.where(mask, seg, -jnp.inf)

        def _ssd(x, A_log, D, B_w, B_b, C_w, C_b, dt_w, dt_b, out_w, out_b):
            b, t, d = x.shape
            h = A_log.shape[0]
            n = B_w.shape[0] // N_GROUPS
            p = d // h
            l = CHUNK
            c = t // l
            A = -jnp.exp(A_log.astype(jnp.float32))
            B = (x @ B_w.T + B_b).reshape(b, t, N_GROUPS, n)
            C = (x @ C_w.T + C_b).reshape(b, t, N_GROUPS, n)
            B = jnp.broadcast_to(B, (b, t, h, n))
            C = jnp.broadcast_to(C, (b, t, h, n))
            dt = jax.nn.softplus(x @ dt_w.T + dt_b)
            xh = x.reshape(b, t, h, p)
            xc = xh.reshape(b, c, l, h, p)
            Bc = B.reshape(b, c, l, h, n)
            Cc = C.reshape(b, c, l, h, n)
            dtc = dt.reshape(b, c, l, h)
            dA = jnp.transpose(dtc * A, (0, 3, 1, 2))
            A_cumsum = jnp.cumsum(dA, axis=-1)
            L = jnp.exp(segsum(dA))
            xdt = xc * dtc[..., None]
            Y_diag = jnp.einsum('bclhn,bcshn,bhcls,bcshp->bclhp', Cc, Bc, L, xdt)
            decay_states = jnp.exp(A_cumsum[..., -1:] - A_cumsum)
            states = jnp.einsum('bclhn,bhcl,bclhp->bchpn', Bc, decay_states, xdt)
            states = jnp.concatenate([jnp.zeros_like(states[:, :1]), states], axis=1)
            dA_last = jnp.pad(A_cumsum[..., -1], ((0, 0), (0, 0), (1, 0)))
            decay_chunk = jnp.exp(segsum(dA_last))
            new_states = jnp.einsum('bhzc,bchpn->bzhpn', decay_chunk, states)
            prev_states = new_states[:, :-1]
            state_decay_out = jnp.exp(A_cumsum)
            Y_off = jnp.einsum('bclhn,bchpn,bhcl->bclhp', Cc, prev_states, state_decay_out)
            Y = (Y_diag + Y_off).reshape(b, t, h, p) + D[None, None, :, None] * xh
            return Y.reshape(b, t, d) @ out_w.T + out_b
        return _ssd(x, A_log, D, B_w, B_b, C_w, C_b, dt_w, dt_b, out_w, out_b)

    def _L0_ffn_ref(x, lut, gate_idx, up_idx, down_idx):
        import jax, jax.numpy as jnp
        import numpy as np
        HIDDEN = 512
        INTER = 1376
        LUT_SIZE = 16

        def _ghost_linear(x, idx, lut):
            w = lut[idx]
            return jnp.einsum('bsh,oh->bso', x, w)
        gate = _ghost_linear(x, gate_idx, lut)
        up = _ghost_linear(x, up_idx, lut)
        h = jax.nn.silu(gate) * up
        return _ghost_linear(h, down_idx, lut)

    def _L1_attn_ref(x, Wcq, g_q, Wdq, Wdqr, Wckv, g_kv, Wdk, Wdv, Wkr, Wo):
        import jax, jax.numpy as jnp
        import numpy as np
        D_MODEL = 512
        N_HEADS = 16
        HEAD_DIM = D_MODEL // N_HEADS
        KV_LORA = 128
        Q_LORA = 192
        ROPE_DIM = 64
        EPS = 1e-06

        def _rmsnorm(x, g):
            var = jnp.mean(x * x, axis=-1, keepdims=True)
            return x * jax.lax.rsqrt(var + EPS) * g

        def _rope(t):
            d = t.shape[-1]
            s = t.shape[-2]
            inv_freq = 1.0 / 10000.0 ** (jnp.arange(0, d, 2, dtype=jnp.float32) / d)
            ang = jnp.arange(s, dtype=jnp.float32)[:, None] * inv_freq[None, :]
            cos = jnp.concatenate([jnp.cos(ang), jnp.cos(ang)], axis=-1)
            sin = jnp.concatenate([jnp.sin(ang), jnp.sin(ang)], axis=-1)
            t1, t2 = (t[..., :d // 2], t[..., d // 2:])
            rot = jnp.concatenate([-t2, t1], axis=-1)
            return t * cos + rot * sin
        b, s, _ = x.shape
        qc = _rmsnorm(x @ Wcq, g_q)
        q_nope = (qc @ Wdq).reshape(b, s, N_HEADS, HEAD_DIM).transpose(0, 2, 1, 3)
        q_rope = (qc @ Wdqr).reshape(b, s, N_HEADS, ROPE_DIM).transpose(0, 2, 1, 3)
        kvc = _rmsnorm(x @ Wckv, g_kv)
        k_nope = (kvc @ Wdk).reshape(b, s, N_HEADS, HEAD_DIM).transpose(0, 2, 1, 3)
        v = (kvc @ Wdv).reshape(b, s, N_HEADS, HEAD_DIM).transpose(0, 2, 1, 3)
        k_rope = (x @ Wkr)[:, None, :, :]
        k_rope = jnp.broadcast_to(k_rope, (b, N_HEADS, s, ROPE_DIM))
        q_rope = _rope(q_rope)
        k_rope = _rope(k_rope)
        q = jnp.concatenate([q_nope, q_rope], axis=-1)
        k = jnp.concatenate([k_nope, k_rope], axis=-1)
        scale = 1.0 / jnp.sqrt(jnp.float32(HEAD_DIM + ROPE_DIM))
        scores = jnp.einsum('bhqd,bhkd->bhqk', q, k) * scale
        attn = jax.nn.softmax(scores, axis=-1)
        o = jnp.einsum('bhqk,bhkd->bhqd', attn, v)
        o = o.transpose(0, 2, 1, 3).reshape(b, s, N_HEADS * HEAD_DIM)
        return o @ Wo

    def _L1_ffn_ref(x, router_w, router_bias, gate_w, up_w, down_w, sh_gate_w, sh_up_w, sh_down_w):
        import jax, jax.numpy as jnp
        import numpy as np
        B, T, D = (1, 512, 512)
        E, K, F = (64, 4, 128)
        S, SF = (2, 128 * 4)
        CAP = 64

        def _moe_forward(x, router_w, router_bias, gate_w, up_w, down_w, sh_gate_w, sh_up_w, sh_down_w):
            b, t, d = x.shape
            flat = x.reshape(b * t, d)
            N = flat.shape[0]
            logits = flat @ router_w.T
            scores = jax.nn.softmax(logits, axis=-1)
            _, topk_idx = jax.lax.top_k(logits + router_bias, K)
            topk_w = jnp.take_along_axis(scores, topk_idx, axis=-1)
            topk_w = topk_w / topk_w.sum(axis=-1, keepdims=True)
            P = N * K
            e_flat = topk_idx.reshape(-1)
            t_flat = jnp.repeat(jnp.arange(N), K)
            w_flat = topk_w.reshape(-1)
            order = jnp.argsort(e_flat)
            e_s, t_s, w_s = (e_flat[order], t_flat[order], w_flat[order])
            counts = jnp.bincount(e_s, length=E)
            starts = jnp.concatenate([jnp.zeros((1,), counts.dtype), jnp.cumsum(counts)[:-1]])
            pos = jnp.arange(P) - starts[e_s]
            slot = jnp.where(pos < CAP, pos, CAP)
            tok_table = jnp.zeros((E, CAP + 1), jnp.int32).at[e_s, slot].set(t_s)[:, :CAP]
            w_table = jnp.zeros((E, CAP + 1), w_s.dtype).at[e_s, slot].set(w_s)[:, :CAP]
            xg = flat[tok_table]
            g = jnp.einsum('ecd,efd->ecf', xg, gate_w)
            u = jnp.einsum('ecd,efd->ecf', xg, up_w)
            y = jnp.einsum('ecf,edf->ecd', jax.nn.silu(g) * u, down_w)
            out = jnp.zeros_like(flat).at[tok_table.reshape(-1)].add((y * w_table[..., None]).reshape(-1, d))
            sg = jnp.einsum('nd,sfd->nsf', flat, sh_gate_w)
            su = jnp.einsum('nd,sfd->nsf', flat, sh_up_w)
            out = out + jnp.einsum('nsf,sdf->nd', jax.nn.silu(sg) * su, sh_down_w)
            return out.reshape(b, t, d)
        return _moe_forward(x, router_w, router_bias, gate_w, up_w, down_w, sh_gate_w, sh_up_w, sh_down_w)
    h = _L0_tok_ref(x, L0_tok_emb_table, L0_tok_norm_weight, L0_tok_proj_weight)
    h = h + _L0_attn_ref(_layernorm(h, axis=-1), L0_attn_A_log, L0_attn_D, L0_attn_B_w, L0_attn_B_b, L0_attn_C_w, L0_attn_C_b, L0_attn_dt_w, L0_attn_dt_b, L0_attn_out_w, L0_attn_out_b)
    h = h + _L0_ffn_ref(_layernorm(h, axis=-1), L0_ffn_lut, L0_ffn_gate_idx, L0_ffn_up_idx, L0_ffn_down_idx)
    h = h + _L1_attn_ref(_layernorm(h, axis=-1), L1_attn_Wcq, L1_attn_g_q, L1_attn_Wdq, L1_attn_Wdqr, L1_attn_Wckv, L1_attn_g_kv, L1_attn_Wdk, L1_attn_Wdv, L1_attn_Wkr, L1_attn_Wo)
    h = h + _L1_ffn_ref(_layernorm(h, axis=-1), L1_ffn_router_w, L1_ffn_router_bias, L1_ffn_gate_w, L1_ffn_up_w, L1_ffn_down_w, L1_ffn_sh_gate_w, L1_ffn_sh_up_w, L1_ffn_sh_down_w)
    return h

_drawn_inputs = setup_inputs


def setup_inputs(seed=0):
    import zlib

    import numpy as np

    out = dict(_drawn_inputs(seed))
    spreads = {'L0_attn_D': (1.0, 0.2),
     'L0_attn_B_b': (0.0, 0.1),
     'L0_attn_C_b': (0.0, 0.1),
     'L0_attn_dt_b': (0.0, 0.296),
     'L0_attn_out_b': (0.0, 0.1),
     'L1_attn_g_q': (1.0, 0.6),
     'L1_attn_g_kv': (1.0, 0.6),
     'L1_ffn_router_bias': (0.0, 0.8)}
    factors = {'L0_tok_norm_weight': 4.781,
     'L1_attn_Wcq': 8.0,
     'L1_attn_Wdq': 8.0,
     'L1_attn_Wdqr': 8.0,
     'L1_attn_Wckv': 4.78,
     'L1_attn_Wdk': 8.0,
     'L1_attn_Wdv': 4.825,
     'L1_attn_Wkr': 8.0,
     'L1_attn_Wo': 4.784,
     'L1_ffn_router_w': 8.0,
     'L1_ffn_gate_w': 8.0,
     'L1_ffn_up_w': 8.0,
     'L1_ffn_down_w': 8.0,
     'L1_ffn_sh_gate_w': 7.712,
     'L1_ffn_sh_up_w': 7.565,
     'L1_ffn_sh_down_w': 7.569}
    for name, (base, spread) in spreads.items():
        noise = np.random.default_rng([zlib.crc32(name.encode()), seed]).standard_normal(out[name].shape)
        drawn = base * np.exp(spread * noise) if base else spread * noise
        out[name] = jnp.asarray(drawn.astype(out[name].dtype))
    for name, factor in factors.items():
        out[name] = (out[name] * factor).astype(out[name].dtype)
    return out
```

```python
from contextlib import ExitStack

import concourse.bass as bass
from concourse import mybir

F32 = mybir.dt.float32
I32 = mybir.dt.int32
U32 = mybir.dt.uint32
ALU = mybir.AluOpType
ACT = mybir.ActivationFunctionType
AX = mybir.AxisListType

P = 128
B = 16
D = 512
KD = D // P
V = 128
H0, HP, N0, CH = 32, 16, 64, 64
INTER = 1376
NF = 11
H1, HD, RD = 16, 32, 64
HQ = HD + RD
QL, KVL = 192, 128
E, TOPK, F, CAP = 64, 4, 128, 64
SHF = 1024
EPS_RMS, EPS_LN = 1e-6, 1e-5
CREDIT = 4
LUTN = 520
LUT_COLS = 2 * KD * INTER + NF * D
NCHUNK = LUT_COLS // LUTN
G4 = 4

C_ID, C_GT, C_LE, C_STR, C_ONE, C_TRI, C_IOTA, C_COS, C_SIN, C_P = 0, 128, 256, 384, 512, 640, 704, 768, 832, 896
C_N = 897


class Steps:

    def __init__(self, sem, base=0):
        self.sem, self.base, self.k = sem, base, 0

    def up(self, ins):
        ins.then_inc(self.sem, 1)
        self.k += 1
        return self.base + self.k

    def now(self):
        return self.base + self.k


class Ring:

    def __init__(self, banks, base=0):
        self.banks, self.base, self.k = banks, base, 0

    def take(self):
        n, bank = self.base + self.k, self.banks[self.k % len(self.banks)]
        self.k += 1
        return n, bank


def wait(e, idle, sem, value):
    e.wait_ge(sem, value)
    if not isinstance(value, int):
        e.sem_inc(idle, 1)


def tower(nc, a, out, stop=None):
    with ExitStack() as ctx:
        def sem(name):
            return ctx.enter_context(nc.semaphore(name))

        def sbuf(scope, name, shape, dt=F32):
            return scope.enter_context(nc.sbuf_tensor(name, shape, dt))

        hres = sbuf(ctx, "hres", [P, B, D])
        wreg = sbuf(ctx, "wreg", [P, LUT_COLS])
        cst = sbuf(ctx, "cst", [P, C_N])
        stat = sbuf(ctx, "stat", [P, 4, 8])
        mv = sbuf(ctx, "mv", [P, 4, 2])
        rstd = sbuf(ctx, "rstd", [P, 4])
        veps = sbuf(ctx, "veps", [P, 4])
        mhalf = sbuf(ctx, "mhalf", [P, 1])
        wslot = sbuf(ctx, "wslot", [P, B, TOPK])
        gslot = sbuf(ctx, "gslot", [P, B, TOPK], I32)
        ident = cst[:, C_ID:C_ID + P]
        psum = ctx.enter_context(nc.psum_tensor("psum", [P, 8, 512], F32))

        s1 = ctx.enter_context(ExitStack())
        onehot = sbuf(s1, "onehot", [P, B * P])
        owT = sbuf(s1, "owT", [P, KD, D])
        small = sbuf(s1, "small", [P, B, P])
        bc = sbuf(s1, "bc", [P, 160])
        ecs = sbuf(s1, "ecs", [P, B, H0])
        dec = sbuf(s1, "dec", [P, B, H0])
        tokix = sbuf(s1, "tokix", [P, B], I32)
        dskip = sbuf(s1, "dskip", [P, H0])
        lutb = sbuf(s1, "lutb", [P, 16])
        lutd = sbuf(s1, "lutd", [P, 8])
        qi = sbuf(s1, "qi", [P, 2, LUTN], I32)
        qm = sbuf(s1, "qm", [P, 4, LUTN], I32)
        qt = sbuf(s1, "qt", [P, 8, LUTN])
        sa = ExitStack()
        xtok = sbuf(sa, "xtok", [P, B * P], I32)
        projT = sbuf(sa, "projT", [P, KD, D])
        emb = sbuf(sa, "emb", [P, D])
        nw = sbuf(sa, "nw", [P, D])
        outb = sbuf(sa, "outb", [P, D])
        junk = sbuf(sa, "junk", [P, D])
        e1 = sbuf(sa, "e1", [P, D])
        hraw = sbuf(sa, "hraw", [P, D])
        htab = sbuf(sa, "htab", [P, D])
        xtab = sbuf(sa, "xtab", [P, D])
        htabb = sbuf(sa, "htabb", [P, D])
        eT = sbuf(sa, "eT", [P, KD, V])
        xtT = sbuf(sa, "xtT", [P, KD, V])
        bcdtT = sbuf(sa, "bcdtT", [P, KD, 160])
        bcb = sbuf(sa, "bcb", [P, 160])
        alog = sbuf(sa, "alog", [P, H0])
        sp4 = sbuf(sa, "sp4", [P, 4, H0])
        stab = sbuf(sa, "stab", [P, P])
        ssq = sbuf(sa, "ssq", [P, 2])
        sa.close()
        xg = sbuf(s1, "xg", [P, 2, D])
        hg = sbuf(s1, "hg", [P, 2, D])
        ixb = sbuf(s1, "ixb", [P, 2], I32)
        segr = sbuf(s1, "segr", [P, 2, 16, CH])
        lg = sbuf(s1, "lg", [P, 2, H0, CH])
        mm = sbuf(s1, "mm", [P, 2, CH])
        bt = sbuf(s1, "bt", [N0, 2, P])
        ct = sbuf(s1, "ct", [N0, 2, P])
        bst = sbuf(s1, "bst", [CH, 2, N0])
        xdt = sbuf(s1, "xdt", [P, 2, D])
        xdd = sbuf(s1, "xdd", [CH, 2, D])
        stt = sbuf(s1, "stt", [N0, 2, D])
        ysb = xg
        yT = xdt[:].rearrange("p s (a b) -> p s a b", a=KD)
        s1.close()

        s2 = ctx.enter_context(ExitStack())
        xn = sbuf(s2, "xn", [P, 2, D])
        wq3 = sbuf(s2, "wq3", [P, KD, 384])
        wdq = sbuf(s2, "wdq", [P, 2, H1 * HQ])
        wdkv = sbuf(s2, "wdkv", [P, 2 * D])
        wo = sbuf(s2, "wo", [P, KD, D])
        gqb = sbuf(s2, "gqb", [P, QL])
        gkb = sbuf(s2, "gkb", [P, KVL])
        sf = ExitStack()
        xT = sbuf(sf, "xT", [P, KD, G4 * P])
        sg = sbuf(sf, "sg", [P, 2, D])
        hT = sbuf(sf, "hT", [P, 2, D])
        sf.close()
        sd = ExitStack()
        xT1 = sbuf(sd, "xT1", [P, 2, KD, P])
        lat = sbuf(sd, "lat", [P, 2, 384])
        qct = xn
        qa = sbuf(sd, "qa", [P, 2, H1, HQ])
        ka = sbuf(sd, "ka", [P, 2, H1, HQ])
        rt1 = sbuf(sd, "rt1", [P, 4, RD])
        rt2 = sbuf(sd, "rt2", [P, 4, RD])
        va = sbuf(sd, "va", [P, 2, D])
        qT = wreg[0:HQ, 3 * SHF * KD:3 * SHF * KD + 2 * H1 * P].rearrange("p (s h t) -> p s h t", s=2, h=H1)
        kT = sbuf(sd, "kT", [HQ, 2, H1, P])
        mx = sbuf(sd, "mx", [P, 2, H1])
        nmx = sbuf(sd, "nmx", [P, 2, H1])
        rs = sbuf(sd, "rs", [P, 2, H1])
        ri = sbuf(sd, "ri", [P, 2, H1])
        pb = sbuf(sd, "pb", [P, 2, 2, D])
        pT = sbuf(sd, "pT", [P, 2, 2, D])
        ob, oT = xn, xT1
        ssd2 = sbuf(sd, "ssd2", [P, 2, 2])
        rr = sbuf(sd, "rr", [P, 2, 2])
        sd.close()
        sr = ExitStack()
        rwT = sbuf(sr, "rwT", [P, KD, E])
        rb = sbuf(sr, "rb", [P, E])
        x3T = sbuf(sr, "x3T", [P, 2, KD, P])
        lgt = sbuf(sr, "lgt", [P, 2, E])
        bia = sbuf(sr, "bia", [P, 2, E])
        ex = sbuf(sr, "ex", [P, 2, E])
        nlm = sbuf(sr, "nlm", [P, 2])
        top = sbuf(sr, "top", [P, 2, 8])
        topi = sbuf(sr, "topi", [P, 2, 8], U32)
        topf = sbuf(sr, "topf", [P, 2, TOPK])
        hot = sbuf(sr, "hot", [P, 2, TOPK, E])
        hw = sbuf(sr, "hw", [P, 2, TOPK, E])
        msk = sbuf(sr, "msk", [P, 2, E])
        cum = sbuf(sr, "cum", [P, 3, E])
        tk = sbuf(sr, "tk", [P, 2, 8, TOPK])
        tsum = sbuf(sr, "tsum", [P, 2, 2])
        islot = sbuf(sr, "islot", [P, 2, TOPK], I32)
        zrow = sbuf(sr, "zrow", [P, D])
        sr.close()
        se = ExitStack()
        xgE = sbuf(se, "xgE", [P, 2, D])
        xgT = sbuf(se, "xgT", [P, 2, KD, P])
        wE = sbuf(se, "wE", [P, 2, 2, 3 * D])
        sgE = sbuf(se, "sgE", [P, 2, P])
        hE = sbuf(se, "hE", [P, 2, P])
        yE = sbuf(se, "yE", [P, 2, D])
        se.close()
        sc = ExitStack()
        yk = sbuf(sc, "yk", [P, 2, TOPK, D])
        cix = sbuf(sc, "cix", [P, 2, TOPK], I32)
        cw = sbuf(sc, "cw", [P, 2, TOPK])
        ac = sbuf(sc, "ac", [P, 2, D])
        sc.close()

        d_h = nc.dram_tensor("tab_h", [V, D], F32).ap()
        d_x = nc.dram_tensor("tab_x", [V, D], F32).ap()
        d_s = nc.dram_tensor("tab_s", [V, P], F32).ap()
        d_xg = nc.dram_tensor("slots_x", [E * CAP, D], F32).ap()
        d_y = nc.dram_tensor("slots_y", [E * CAP, D], F32).ap()

        act_full, act_free = sem("act_full"), sem("act_free")
        dve_full, dve_free = sem("dve_full"), sem("dve_free")
        idle = {k: sem(f"idle_{k}") for k in ("pe", "act", "dve", "pool", "sp")}
        dve_step, act_step, pool_step = sem("dve_step"), sem("act_step"), sem("pool_step")
        phase_end = sem("phase_end")
        ld_a, ld_b, ld_c, ld_d, ld_r = (sem(f"ld_{x}") for x in "abcdr")
        var_ready, rstd_ready = sem("var_ready"), sem("rstd_ready")
        ms_ready = sem("ms_ready")
        x_ready = sem("x_ready")
        hraw_ready, dtin_ready, sp_ready, tab_ready, tab_stored = (
            sem(x) for x in ("hraw_ready", "dtin_ready", "sp_ready", "tab_ready", "tab_stored"))
        small_in, hot_ready, mhalf_ready = sem("small_in"), sem("hot_ready"), sem("mhalf_ready")
        cs_ready = sem("cs_ready")
        xh_used = sem("xh_used")
        segr_ready = sem("segr_ready")
        g_ready, xd_ready, y_ready = sem("g_ready"), sem("xd_ready"), sem("y_ready")
        bst_ready = sem("bst_ready")
        l_ready = sem("l_ready")
        qi_ld, xh_ld, we_ld, xe_ld, yk_ld = (
            [sem(f"{x}_{p}") for p in range(2)] for x in ("qi_in", "xh_in", "we_in", "xe_in", "yk_in"))
        qi_used, qm_ready, qt_ready, qt_used, qw_ready, qw_stored = (
            sem(x) for x in ("qi_used", "qm_ready", "qt_ready", "qt_used", "qw_ready", "qw_stored"))
        sg_ready, hT_ready, hT_used, down_full, down_free = (
            sem(x) for x in ("sg_ready", "hT_ready", "hT_used", "down_full", "down_free"))
        lat_ready, rope_ready, mx_ready, o_ready = (sem(x) for x in ("lat_ready", "rope_ready", "mx_ready", "o_ready"))
        nlm_ready, ex_ready, msk_ready, slot_ready, scattered, xg_zero = (
            sem(x) for x in ("nlm_ready", "ex_ready", "msk_ready", "slot_ready", "scattered", "xg_zero"))
        we_used, he_ready, ye_ready, ye_out, sge_ready = (
            sem(x) for x in ("we_used", "he_ready", "ye_ready", "ye_out", "sge_ready"))
        cix_ready, ac_ready, ac_out = (
            sem(x) for x in ("cix_ready", "ac_ready", "ac_out"))

        NLD_A = 13

        def bank(n):
            return psum[:, n, :]

        A_AB, V_AB = [0, 1, 2, 3], [4, 5, 6, 7]

        def barrier(e, k):
            e.drain().then_inc(phase_end, 1)
            e.wait_ge(phase_end, 5 * k)

        block = ctx.enter_context(nc.Block())

        A_B, V_B = 4, 4
        A_BN, V_BN = 8, 4
        A_C, V_C = A_B + B * A_BN, V_B + B * V_BN
        A_CN, V_CN = 3 + NF, 1 + NF
        A_D, V_D = A_C + 4 * A_CN, V_C + 4 * V_CN
        A_DN, V_DN = 20, 8
        A_R, V_R = A_D + B * A_DN, V_D + B * V_DN
        A_RN, V_RN = 1, 2
        A_S, V_S = A_R + B * A_RN, V_R + B * V_RN
        NSH = SHF // P
        A_SN, V_SN = 4 + NSH, NSH
        A_E, V_E = A_S + 4 * A_SN, V_S + 4 * V_SN
        NPAIR = E // 2
        @block.sync
        def _(e):
            W = lambda s, v: wait(e, idle["sp"], s, v)
            for dst, src in ((cst[:], a["consts"]), (emb[:], a["emb"]), (projT[:], a["projT"]),
                             (nw[:], a["nw"].partition_broadcast(P)), (outb[:], a["outb"].partition_broadcast(P)),
                             (bcdtT[:], a["bcdtT"]), (bcb[:], a["bcb"].partition_broadcast(P)),
                             (alog[:], a["alog"].partition_broadcast(P)),
                             (dskip[:], a["dskip"].partition_broadcast(P)),
                             (lutb[:], a["lut"].partition_broadcast(P)), (tokix[:], a["tokix"]),
                             (xtok[:], a["xtok"].partition_broadcast(P)), (owT[:], a["owT"])):
                e.dma_start(dst, src).then_inc(ld_a, 16)
            e.wait_ge(tab_ready, 3)
            e.dma_start(d_h, htabb[:]).then_inc(tab_stored, 16)
            e.dma_start(d_x, xtab[:]).then_inc(tab_stored, 16)
            e.dma_start(d_s, stab[:]).then_inc(tab_stored, 16)
            barrier(e, 1)
            with e.Fori(0, B // 2) as j:
                for c in range(4):
                    n = j * 4 + c
                    off_in, off_out = e.snap(n * LUTN), e.snap((n - 1) * LUTN) if c else None
                    W(qi_used, n + 1)
                    e.dma_start(qi[:, c % 2, :], a["lutidx"][:, bass.ds(off_in, LUTN)]).then_inc(qi_ld[c % 2], 16)
                    if c:
                        W(qw_ready, n)
                        e.dma_start(wreg[:, bass.ds(off_out, LUTN)], qt[:, 0, :]).then_inc(qw_stored, 16)
                n = j * 4 + 3
                off_out = e.snap(n * LUTN)
                W(qw_ready, n + 1)
                e.dma_start(wreg[:, bass.ds(off_out, LUTN)], qt[:, 0, :]).then_inc(qw_stored, 16)
            e.wait_ge(qw_stored, 16 * NCHUNK + 1)
            barrier(e, 2)
            if stop == "B":
                pass
            else:
                for dst, src in ((wq3[:], a["wq3"]), (wdq[:, 0, :], a["wdq"][0:P]), (wdq[0:QL - P, 1, :], a["wdq"][P:QL]),
                                 (wdkv[:], a["wdkv"]), (wo[:], a["wo"]),
                                 (gqb[:], a["gq"].partition_broadcast(P)), (gkb[:], a["gkv"].partition_broadcast(P))):
                    e.dma_start(dst, src).then_inc(ld_d, 16)
                barrier(e, 3)
            if stop not in ("B", "C"):
                e.dma_start(wreg[:, 0:3 * NSH * D], a["shw"]).then_inc(ld_c, 16)
                barrier(e, 4)
            if stop not in ("B", "C", "D"):
                e.dma_start(rwT[:], a["rwT"]).then_inc(ld_r, 16)
                e.dma_start(rb[:], a["rb"].partition_broadcast(P)).then_inc(ld_r, 16)
                e.wait_ge(xg_zero, 1)
                for n in range(E * CAP // P):
                    e.dma_start(d_xg[n * P:(n + 1) * P, :], zrow[:]).then_inc(xg_zero, 16)
                e.wait_ge(xg_zero, 1 + 16 * (E * CAP // P))
                barrier(e, 5)
                barrier(e, 6)
                with e.Fori(0, NPAIR // 2) as j:
                    offs = [(e.snap((2 * j + q) * 2 * P), e.snap((2 * j + q) * P)) for q in range(2)]
                    for q in range(2):
                        n = 2 * j + q
                        W(we_used, n + 1)
                        e.dma_start(wE[:, q, :, :], a["wexp"][bass.ds(offs[q][0], 2 * P), :]
                                    .rearrange("(e p) n -> p e n", p=P)).then_inc(we_ld[q], 16)
                        e.dma_start(xgE[:, q, :], d_xg[bass.ds(offs[q][1], P), :]).then_inc(xe_ld[q], 16)
                    for q in range(2):
                        n = 2 * j + q
                        W(ye_ready, n + 1)
                        e.dma_start(d_y[bass.ds(offs[q][1], P), :], yE[:, q, :]).then_inc(ye_out, 16)
                e.wait_ge(ye_out, 16 * NPAIR + 1)
                barrier(e, 7)
                out_v = out.rearrange("b t d -> (b t) d")
                with e.Fori(0, B // 2) as j:
                    offs = [e.snap((2 * j + q) * P) for q in range(2)]
                    for q in range(2):
                        W(ac_ready, 2 * j + q + 1)
                        e.dma_start(out_v[bass.ds(offs[q], P), :], ac[:, q, :]).then_inc(ac_out, 16)
                e.wait_ge(ac_out, 16 * B + 1)
            else:
                e.dma_start(out.rearrange("b t d -> t b d"), hres[:]).then_inc(ac_out, 16)
                e.wait_ge(ac_out, 17)

        @block.gpsimd
        def _(e):
            W = lambda s, v: wait(e, idle["pool"], s, v)
            st = Steps(pool_step)
            nr = [0]

            def rsqrt(src, k, scale, eps, src_sem, src_val):
                W(src_sem, src_val)
                st.up(e.tensor_scalar(veps[:, k:k + 1], src, scale, eps, ALU.mult, ALU.add))
                W(pool_step, st.now())
                e.tensor_tensor(rstd[:, k:k + 1], veps[:, k:k + 1], mhalf[:], ALU.pow).then_inc(rstd_ready, 1)

            def gather(dst, tab, ix, s):
                e.indirect_dma_start(dst, None, tab, bass.IndirectOffsetOnAxis(ap=ix, axis=0)).then_inc(s, 16)

            e.memset(mhalf[:], -0.5).then_inc(mhalf_ready, 1)
            e.wait_ge(mhalf_ready, 1)
            rsqrt(ssq[:, 0:1], 0, 1.0 / D, EPS_RMS, ms_ready, 1)
            rsqrt(ssq[:, 1:2], 1, 1.0 / D, EPS_RMS, ms_ready, 2)
            rsqrt(mv[:, 0, 1:2], 2, 1.0, EPS_LN, var_ready, 1)
            e.wait_ge(ld_a, 16 * NLD_A)
            e.wait_ge(tab_stored, 48)
            for i in range(B):
                gather(small[:, i, :], d_s, tokix[:, i:i + 1], small_in)
            e.wait_ge(small_in, 16 * B)
            barrier(e, 1)
            with e.Fori(0, B // 2) as j:
                s = Steps(pool_step, j * 2 + 3)
                for p in range(2):
                    i = 2 * j + p
                    W(xh_used, 2 * i + 1)
                    ix = e.snap(i)
                    s.up(e.tensor_copy(ixb[:, p:p + 1], tokix[:, bass.ds(ix, 1)]))
                    W(pool_step, s.now())
                    gather(xg[:, p, :], d_x, ixb[:, p:p + 1], xh_ld[p])
                    gather(hg[:, p, :], d_h, ixb[:, p:p + 1], xh_ld[p])
                for q in range(2):
                    for p in range(2):
                        i = 2 * j + p
                        if q:
                            W(act_free, A_B + j * 2 * A_BN + 4 + 2 * p + 2 + CREDIT)
                        else:
                            W(act_free, A_B + j * 2 * A_BN - 2 * A_BN + 8 + 2 * p + 2 + CREDIT)
                        e.tensor_tensor(segr[:, p, :, :],
                                        small[:, bass.ds(e.snap(i), 1), 96 + 16 * q:112 + 16 * q].rearrange("p a h -> p (a h)").unsqueeze(2).to_broadcast([P, 16, CH]),
                                        cst[:, C_TRI:C_TRI + CH].unsqueeze(1).to_broadcast([P, 16, CH]),
                                        ALU.mult).then_inc(segr_ready, 1)
            barrier(e, 2)
            if stop == "B":
                return
            base = 3 + B
            done = 3

            def ln_pairs(base, seen, n_pairs):
                with e.Fori(0, n_pairs) as j:
                    s = Steps(pool_step, j * 2 + base)
                    for p in range(2):
                        W(var_ready, seen + 1 + 2 * j + p)
                        s.up(e.tensor_scalar(veps[:, p:p + 1], mv[:, p, 1:2], 1.0, EPS_LN, ALU.mult, ALU.add))
                        W(pool_step, s.now())
                        e.tensor_tensor(rstd[:, p:p + 1], veps[:, p:p + 1], mhalf[:], ALU.pow).then_inc(rstd_ready, 1)

            ln_pairs(base, 1, B // 2)
            base += B
            barrier(e, 3)
            if stop == "C":
                return
            with e.Fori(0, B // 2) as j:
                s = Steps(pool_step, j * 4 + base)
                for p in range(2):
                    W(var_ready, 1 + B + 1 + 2 * j + p)
                    s.up(e.tensor_scalar(veps[:, p:p + 1], mv[:, p, 1:2], 1.0, EPS_LN, ALU.mult, ALU.add))
                    W(pool_step, s.now())
                    e.tensor_tensor(rstd[:, p:p + 1], veps[:, p:p + 1], mhalf[:], ALU.pow).then_inc(rstd_ready, 1)
                for p in range(2):
                    W(ms_ready, 2 + 2 * j + p + 1)
                    s.up(e.tensor_scalar(rr[:, p, :], ssd2[:, p, :], 1.0, EPS_RMS, ALU.mult, ALU.add))
                    W(pool_step, s.now())
                    e.tensor_tensor(rr[:, p, :], rr[:, p, :], mhalf[:].to_broadcast([P, 2]), ALU.pow).then_inc(rstd_ready, 1)
            base += 2 * B
            barrier(e, 4)
            if stop == "D":
                return
            e.memset(zrow[:], 0.0).then_inc(xg_zero, 1)
            e.wait_ge(xg_zero, 1 + 16 * (E * CAP // P))
            with e.Fori(0, B // 2) as j:
                s = Steps(pool_step, j * 2 + base)
                for p in range(2):
                    W(var_ready, 1 + 2 * B + 1 + 2 * j + p)
                    s.up(e.tensor_scalar(veps[:, p:p + 1], mv[:, p, 1:2], 1.0, EPS_LN, ALU.mult, ALU.add))
                    W(pool_step, s.now())
                    e.tensor_tensor(rstd[:, p:p + 1], veps[:, p:p + 1], mhalf[:], ALU.pow).then_inc(rstd_ready, 1)
                for p in range(2):
                    W(slot_ready, 2 * j + p + 1)
                    for k in range(TOPK):
                        e.indirect_dma_start(d_xg, bass.IndirectOffsetOnAxis(ap=islot[:, p, k:k + 1], axis=0),
                                             xn[:, p, :], None, bounds_check=E * CAP - 1,
                                             oob_is_err=False).then_inc(scattered, 16)
            base += B
            e.wait_ge(scattered, 16 * TOPK * B)
            barrier(e, 5)
            ln_pairs(base, 1 + 3 * B, B // 2)
            base += B
            barrier(e, 6)
            barrier(e, 7)
            with e.Fori(0, B // 2) as j:
                for p in range(2):
                    W(cix_ready, 2 * j + p + 1)
                    for k in range(TOPK):
                        gather(yk[:, p, k, :], d_y, cix[:, p, k:k + 1], yk_ld[p])

        @block.tensor
        def _(e):
            W = lambda s, v: wait(e, idle["pe"], s, v)

            def fill(ring, free, depth):
                n, b = ring.take()
                W(free, n - depth + 1 + CREDIT)
                return n, psum[:, b, :]

            def turn(dst, src, w=P):
                return e.transpose(dst, src, ident[0:w, 0:w])

            ra, rv = Ring(A_AB), Ring(V_AB)
            e.wait_ge(ld_a, 16 * NLD_A)
            e.wait_ge(x_ready, 1)
            n, ps = fill(ra, act_free, 4)
            for k in range(KD):
                t = turn(ps[:, k * P:(k + 1) * P], e1[:, k * P:(k + 1) * P])
            t.then_inc(act_full, 1)
            e.wait_ge(act_free, n + 1 + CREDIT)
            n, ps = fill(rv, dve_free, 4)
            for k in range(KD):
                t = e.matmul(ps, eT[:, k, :], projT[:, k, :], start=k == 0, stop=k == KD - 1)
            t.then_inc(dve_full, 1)
            e.wait_ge(x_ready, 2)
            n, ps = fill(ra, act_free, 4)
            for k in range(KD):
                t = turn(ps[:, k * P:(k + 1) * P], xtab[:, k * P:(k + 1) * P])
            t.then_inc(act_full, 1)
            e.wait_ge(act_free, n + 1 + CREDIT)
            n, ps = fill(rv, dve_free, 4)
            for k in range(KD):
                t = e.matmul(ps[:, 0:160], xtT[:, k, :], bcdtT[:, k, :], start=k == 0, stop=k == KD - 1)
            t.then_inc(dve_full, 1)
            e.wait_ge(small_in, 16 * B)
            for m in (C_LE, C_GT):
                n, ps = fill(ra, act_free, 4)
                e.matmul(ps.rearrange("p (a b) -> p a b", a=B), cst[:, m:m + P], small[:, :, 96:128],
                         start=True, stop=True).then_inc(act_full, 1)
            for _ in range(2):
                rv.take()
            barrier(e, 1)

            e.wait_ge(hot_ready, 1)
            with e.Fori(0, B // 2) as j:
                ra, rv = Ring(A_AB, A_B + j * 2 * A_BN), Ring(V_AB, V_B + j * 2 * V_BN)
                got = {}
                for p in range(2):
                    i = 2 * j + p
                    col = e.snap(i * P)
                    for c, nm in ((0, "b"), (1, "c")):
                        got[nm, p], ps = fill(ra, act_free, 4)
                        e.matmul(ps[0:N0, 0:P], bc[:, 64 * c:64 * c + 64], onehot[:, bass.ds(col, P)],
                                 start=True, stop=True).then_inc(act_full, 1)
                for p in range(2):
                    W(act_free, got["c", p] + 1 + CREDIT)
                    n, ps = fill(rv, dve_free, 4)
                    for c in range(2):
                        t = e.matmul(ps[CH * c:CH * c + CH, 0:CH], bt[:, p, CH * c:CH * c + CH],
                                     ct[:, p, CH * c:CH * c + CH], start=True, stop=True)
                    t.then_inc(dve_full, 1)
                for q in range(2):
                    for p in range(2):
                        W(segr_ready, 4 * j + 2 * q + p + 1)
                        for hh in range(2):
                            n, ps = fill(ra, act_free, 4)
                            t = e.matmul(ps, cst[:, C_GT:C_GT + P],
                                         segr[:, p, 8 * hh:8 * hh + 8, :].rearrange("p a b -> p (a b)"),
                                         start=True, stop=True)
                            t.then_inc(act_full, 1)
                for p in range(2):
                    W(xd_ready, 2 * j + p + 1)
                    W(bst_ready, 2 * j + p + 1)
                    got["s", p], ps = fill(ra, act_free, 4)
                    e.matmul(ps[0:N0, :], bst[:, p, :], xdd[:, p, :], start=True, stop=True).then_inc(act_full, 1)
                for p in range(2):
                    W(g_ready, 8 * j + 6 + 2 * p)
                    n, ps = fill(rv, dve_free, 4)
                    for h in range(H0):
                        for c in range(2):
                            r = slice(CH * c, CH * c + CH)
                            t = e.matmul(ps[r, HP * h:HP * h + HP], lg[r, p, h, :], xdt[r, p, HP * h:HP * h + HP],
                                         start=True, stop=True)
                    t.then_inc(dve_full, 1)
                    W(act_free, got["s", p] + 1 + CREDIT)
                    n, ps = fill(rv, dve_free, 4)
                    e.matmul(ps[CH:P, :], ct[:, p, CH:P], stt[:, p, :], start=True, stop=True).then_inc(dve_full, 1)
                for p in range(2):
                    W(y_ready, 2 * j + p + 1)
                    got["y", p], ps = fill(ra, act_free, 4)
                    for k in range(KD):
                        t = turn(ps[:, k * P:(k + 1) * P], ysb[:, p, k * P:(k + 1) * P])
                    t.then_inc(act_full, 1)
                for p in range(2):
                    W(act_free, got["y", p] + 1 + CREDIT)
                    n, ps = fill(rv, dve_free, 4)
                    for k in range(KD):
                        t = e.matmul(ps, yT[:, p, k, :], owT[:, k, :], start=k == 0, stop=k == KD - 1)
                    t.then_inc(dve_full, 1)
                assert ra.k == 2 * A_BN and rv.k == 2 * V_BN, (ra.k, rv.k)
            barrier(e, 2)
            if stop == "B":
                return

            def ffn(base_a, base_v, na, nv, nf, seen, gate, up, down, rows, groups_before, act_t):
                with e.Fori(0, 4) as g:
                    ra, rv = Ring([0, 1], base_a + g * na), Ring([2, 3], base_v + g * nv)
                    last = None
                    for q in range(4):
                        W(x_ready, seen + g * 4 + q + 1)
                        ring, free, full = (ra, act_free, act_full) if q < act_t else (rv, dve_free, dve_full)
                        n, ps = fill(ring, free, 2)
                        for k in range(KD):
                            t = turn(ps[:, k * P:(k + 1) * P], xn[:, q % 2, k * P:(k + 1) * P])
                        t.then_inc(full, 1)
                        if q == act_t - 1:
                            la = n
                    W(act_free, la + 1 + CREDIT)
                    if act_t < 4:
                        W(dve_free, n + 1 + CREDIT)
                    for f in range(nf + 1):
                        if f < nf:
                            m = rows(f)
                            for ring, free, full, w in ((ra, act_free, act_full, gate), (rv, dve_free, dve_full, up)):
                                n, ps = fill(ring, free, 2)
                                for k in range(KD):
                                    t = e.matmul(ps[0:m, :], w(k, f), xT[:, k, :], start=k == 0, stop=k == KD - 1)
                                t.then_inc(full, 1)
                        if f:
                            m = rows(f - 1)
                            if f == 1:
                                W(down_free, (groups_before + g) * 4 + CREDIT)
                            W(hT_ready, base_h(groups_before, nf) + g * nf + f)
                            for q in range(4):
                                t = e.matmul(psum[:, 4 + q, :], hT[0:m, (f - 1) % 2, q * P:(q + 1) * P], down(f - 1),
                                             start=f == 1, stop=f == nf)
                            t.then_inc(hT_used, 1)
                    e.drain().then_inc(down_full, 1)
                    assert ra.k == na and rv.k == nv

            def base_h(groups_before, nf):
                return groups_before * NF

            ffn(A_C, V_C, A_CN, V_CN, NF, 2,
                lambda k, f: wreg[:, k * INTER + f * P:k * INTER + f * P + rows0(f)],
                lambda k, f: wreg[:, (KD + k) * INTER + f * P:(KD + k) * INTER + f * P + rows0(f)],
                lambda f: wreg[0:rows0(f), 2 * KD * INTER + f * D:2 * KD * INTER + (f + 1) * D],
                rows0, 0, 3)
            barrier(e, 3)
            if stop == "C":
                return

            e.wait_ge(ld_d, 16 * 7)
            with e.Fori(0, B // 2) as j:
                ra, rv = Ring(A_AB, A_D + j * 2 * A_DN), Ring(V_AB, V_D + j * 2 * V_DN)
                got = {}
                for p in range(2):
                    W(x_ready, 2 + B + 2 * j + p + 1)
                    got["x", p], ps = fill(ra, act_free, 4)
                    for k in range(KD):
                        t = turn(ps[:, k * P:(k + 1) * P], xn[:, p, k * P:(k + 1) * P])
                    t.then_inc(act_full, 1)
                for p in range(2):
                    W(act_free, got["x", p] + 1 + CREDIT)
                    n, ps = fill(rv, dve_free, 4)
                    for k in range(KD):
                        t = e.matmul(ps[:, 0:384], xT1[:, p, k, :], wq3[:, k, :], start=k == 0, stop=k == KD - 1)
                    t.then_inc(dve_full, 1)
                for p in range(2):
                    W(lat_ready, 2 * j + p + 1)
                    got["l", p], ps = fill(ra, act_free, 4)
                    turn(ps[:, 0:P], lat[:, p, 0:P])
                    turn(ps[0:QL - P, P:2 * P], lat[:, p, P:QL])
                    turn(ps[:, 2 * P:3 * P], lat[:, p, QL:QL + KVL]).then_inc(act_full, 1)
                for p in range(2):
                    W(act_free, got["l", p] + 1 + CREDIT)
                    for g in range(4):
                        n, ps = fill(rv, dve_free, 4)
                        e.matmul(ps[:, 0:384], qct[:, p, 0:P], wdq[:, 0, g * 384:(g + 1) * 384], start=True, stop=False)
                        e.matmul(ps[:, 0:384], qct[0:QL - P, p, P:2 * P], wdq[0:QL - P, 1, g * 384:(g + 1) * 384],
                                 start=False, stop=True).then_inc(dve_full, 1)
                    n, ps = fill(rv, dve_free, 4)
                    e.matmul(ps, qct[:, p, 2 * P:3 * P], wdkv[:, 0:D], start=True, stop=True).then_inc(dve_full, 1)
                    n, ps = fill(ra, act_free, 4)
                    e.matmul(ps, qct[:, p, 2 * P:3 * P], wdkv[:, D:2 * D], start=True, stop=True).then_inc(act_full, 1)
                for p in range(2):
                    for src, w in ((qa, 0), (ka, 1)):
                        for g in range(4):
                            if g == 0 or not w:
                                W(rope_ready, 5 * (2 * j + p) + (5 if w else g + 1))
                            n, ps = fill(ra, act_free, 4)
                            for h in range(4):
                                t = turn(ps[0:HQ, h * P:(h + 1) * P], src[:, p, 4 * g + h, :])
                            t.then_inc(act_full, 1)
                    got["kT", p] = n
                ob_ps = {}
                for what, g in (("S", 0), ("S", 1), ("T", 0), ("S", 2), ("T", 1), ("V", 0), ("S", 3), ("T", 2),
                                ("V", 1), ("T", 3), ("V", 2), ("V", 3)):
                    for p in range(2):
                        if what == "S":
                            if g == 0:
                                W(act_free, got["kT", p] + 1 + CREDIT)
                            got["S", p, g], ps = fill(ra, act_free, 4)
                            for h in range(4):
                                t = e.matmul(ps[:, h * P:(h + 1) * P], qT[:, p, 4 * g + h, :], kT[:, p, 4 * g + h, :],
                                             start=True, stop=True)
                            t.then_inc(act_full, 1)
                        elif what == "T":
                            W(act_free, got["S", p, g] + 1 + CREDIT)
                            got["T", p, g], ps = fill(ra, act_free, 4)
                            for h in range(4):
                                t = turn(ps[:, h * P:(h + 1) * P], pb[:, p, g % 2, h * P:(h + 1) * P])
                            t.then_inc(act_full, 1)
                        else:
                            W(act_free, got["T", p, g] + 1 + CREDIT)
                            if g == 0:
                                n, ob_ps[p] = fill(rv, dve_free, 4)
                            for h in range(4):
                                c = (4 * g + h) * HD
                                t = e.matmul(ob_ps[p][:, c:c + HD], pT[:, p, g % 2, h * P:(h + 1) * P],
                                             va[:, p, c:c + HD], start=True, stop=True)
                            if g == 3:
                                t.then_inc(dve_full, 1)
                for p in range(2):
                    W(o_ready, 2 * j + p + 1)
                    got["o", p], ps = fill(ra, act_free, 4)
                    for k in range(KD):
                        t = turn(ps[:, k * P:(k + 1) * P], ob[:, p, k * P:(k + 1) * P])
                    t.then_inc(act_full, 1)
                for p in range(2):
                    W(act_free, got["o", p] + 1 + CREDIT)
                    n, ps = fill(rv, dve_free, 4)
                    for k in range(KD):
                        t = e.matmul(ps, oT[:, p, k, :], wo[:, k, :], start=k == 0, stop=k == KD - 1)
                    t.then_inc(dve_full, 1)
                assert ra.k == 2 * A_DN and rv.k == 2 * V_DN, (ra.k, rv.k)
            barrier(e, 4)
            if stop == "D":
                return

            e.wait_ge(ld_r, 32)
            with e.Fori(0, B // 2) as j:
                ra, rv = Ring([0, 1], A_R + j * 2 * A_RN), Ring([4, 5], V_R + j * 2 * V_RN)
                got = {}
                for p in range(2):
                    W(x_ready, 2 + 2 * B + 2 * j + p + 1)
                    got[p], ps = fill(ra, act_free, 2)
                    for k in range(KD):
                        t = turn(ps[:, k * P:(k + 1) * P], xn[:, p, k * P:(k + 1) * P])
                    t.then_inc(act_full, 1)
                for p in range(2):
                    W(act_free, got[p] + 1 + CREDIT)
                    n, ps = fill(rv, dve_free, 2)
                    for k in range(KD):
                        t = e.matmul(ps[:, 0:E], x3T[:, p, k, :], rwT[:, k, :], start=k == 0, stop=k == KD - 1)
                    t.then_inc(dve_full, 1)
                for p in range(2):
                    W(msk_ready, 2 * (2 * j + p + 1))
                    n, ps = fill(rv, dve_free, 2)
                    e.matmul(ps[:, 0:E], cst[:, C_STR:C_STR + P], msk[:, p, :], start=True, stop=False)
                    e.matmul(ps[:, 0:E], cst[:, C_ONE:C_ONE + P], cum[:, p, :], start=False, stop=True).then_inc(dve_full, 1)
            barrier(e, 5)

            e.wait_ge(ld_c, 16)
            ffn(A_S, V_S, A_SN, V_SN, NSH, 2 + 3 * B,
                lambda k, f: wreg[:, k * SHF + f * P:k * SHF + (f + 1) * P],
                lambda k, f: wreg[:, (KD + k) * SHF + f * P:(KD + k) * SHF + (f + 1) * P],
                lambda f: wreg[:, 2 * KD * SHF + f * D:2 * KD * SHF + (f + 1) * D],
                lambda f: P, 4, 4)
            barrier(e, 6)

            with e.Fori(0, NPAIR // 2) as j:
                ra, rv = Ring([0, 1, 2, 3], A_E + j * 4), Ring([4, 5, 6, 7], V_E + j * 4)
                got = {}
                for q in range(2):
                    W(xe_ld[q], 16 * j + 16)
                    got[q], ps = fill(ra, act_free, 4)
                    for k in range(KD):
                        t = turn(ps[:, k * P:(k + 1) * P], xgE[:, q, k * P:(k + 1) * P])
                    t.then_inc(act_full, 1)
                for q in range(2):
                    W(we_ld[q], 16 * j + 16)
                    W(act_free, got[q] + 1 + CREDIT)
                    for c, (ring, free, full) in enumerate(((ra, act_free, act_full), (rv, dve_free, dve_full))):
                        n, ps = fill(ring, free, 4)
                        for x in range(2):
                            for k in range(KD):
                                t = e.matmul(ps[:, CAP * x:CAP * x + CAP], wE[:, q, x, c * D + k * P:c * D + (k + 1) * P],
                                             xgT[:, q, k, CAP * x:CAP * x + CAP], start=k == 0, stop=k == KD - 1)
                        t.then_inc(full, 1)
                for q in range(2):
                    n2 = 2 * j + q
                    W(he_ready, n2 + 1)
                    n, ps = fill(rv, dve_free, 4)
                    for x in range(2):
                        t = e.matmul(ps[CAP * x:CAP * x + CAP, :], hE[:, q, CAP * x:CAP * x + CAP],
                                     wE[:, q, x, 2 * D:3 * D], start=True, stop=True)
                    t.then_inc(dve_full, 1)
                assert ra.k == 4 and rv.k == 4
            barrier(e, 7)

        @block.scalar
        def _(e):
            W = lambda s, v: wait(e, idle["act"], s, v)

            def drawn(ring):
                n, b = ring.take()
                W(act_full, n + 1)
                return psum[:, b, :]

            def give(ins):
                ins.then_inc(act_free, 1)

            def copy(dst, src):
                return e.activation(dst, src, ACT.Copy)

            e.sem_inc(act_free, CREDIT)
            e.wait_ge(ld_a, 16 * NLD_A)
            ra = Ring(A_AB)
            e.activation(junk[:], emb[:], ACT.Square, accum_out=ssq[:, 0:1]).then_inc(ms_ready, 1)
            give(copy(eT[:].rearrange("p a b -> p (a b)"), drawn(ra)))
            e.wait_ge(hraw_ready, 1)
            e.wait_ge(ms_ready, 1)
            e.activation(junk[:], hraw[:], ACT.Square, accum_out=ssq[:, 1:2]).then_inc(ms_ready, 1)
            give(copy(xtT[:].rearrange("p a b -> p (a b)"), drawn(ra)))
            e.wait_ge(dtin_ready, 1)
            e.activation(sp4[:, 1, :], sp4[:, 0, :], ACT.Exp).then_inc(act_step, 1)
            e.wait_ge(act_step, 1)
            e.activation(sp4[:, 2, :], sp4[:, 1, :], ACT.Ln, bias=1.0).then_inc(sp_ready, 1)
            e.activation(alog[:], alog[:], ACT.Exp).then_inc(sp_ready, 1)
            for dst in (ecs, dec):
                give(e.activation(dst[:].rearrange("p a b -> p (a b)"), drawn(ra), ACT.Exp))
            barrier(e, 1)

            with e.Fori(0, B // 2) as j:
                ra = Ring(A_AB, A_B + j * 2 * A_BN)
                done = 0

                def look(c):
                    n = 4 * j + c
                    W(qm_ready, n + 1)
                    W(qw_stored, 16 * n + 1)
                    for t in range(8):
                        if t == 1:
                            W(qt_used, n + 1)
                        e.activation(qt[:, t, :], qm[:, 0, :], ACT.Identity, scale=lutd[:, t:t + 1],
                                     bias=lutb[:, 2 * t:2 * t + 1]).then_inc(qt_ready, 1)

                for p in range(2):
                    give(copy(bt[:, p, :], drawn(ra)[0:N0, 0:P]))
                    give(copy(ct[:, p, :], drawn(ra)[0:N0, 0:P]))
                    copy(bst[:, p, :], small[0:CH, bass.ds(e.snap(2 * j + p), 1), 0:N0].rearrange("p a n -> p (a n)")).then_inc(bst_ready, 1)
                look(0)
                for q in range(2):
                    for p in range(2):
                        for hh in range(2):
                            ps = drawn(ra)
                            h = 16 * q + 8 * hh
                            e.activation(lg[:, p, h:h + 8, :].rearrange("p a b -> p (a b)"), ps, ACT.Exp).then_inc(act_free, 1)
                    look(1 + q)
                for p in range(2):
                    give(copy(stt[:, p, :], drawn(ra)[0:N0, :]))
                look(3)
                for p in range(2):
                    give(copy(xdt[:, p, :], drawn(ra)))
            barrier(e, 2)
            if stop == "B":
                return

            def ffn(base_a, na, nf, rows, groups_before, act_t):
                with e.Fori(0, 4) as g:
                    ra = Ring([0, 1], base_a + g * na)
                    for q in range(act_t):
                        give(copy(xT[:, :, q * P:(q + 1) * P], drawn(ra).rearrange("p (a b) -> p a b", a=KD)))
                    for f in range(nf):
                        m = rows(f)
                        ps = drawn(ra)
                        if f >= 2:
                            W(hT_ready, groups_before * NF + g * nf + f - 1)
                        e.activation(sg[0:m, f % 2, :], ps[0:m, :], ACT.Silu).then_inc(act_free, 1)

            ffn(A_C, A_CN, NF, rows0, 0, 3)
            barrier(e, 3)
            if stop == "C":
                return

            SC = float(HQ) ** -0.5
            with e.Fori(0, B // 2) as j:
                ra = Ring(A_AB, A_D + j * 2 * A_DN)
                for p in range(2):
                    give(copy(xT1[:, p, :, :].rearrange("p a b -> p (a b)"), drawn(ra)))
                for p in range(2):
                    W(dve_step, D_STEPS0 + j * D_PERIOD + D_LAT[p])
                    e.activation(pb[:, p, 0, 0:QL], lat[:, p, 0:QL], ACT.Square, scale=float(QL) ** -0.5,
                                 accum_out=ssd2[:, p, 0:1]).then_inc(act_step, 1)
                    e.activation(pb[:, p, 1, 0:KVL], lat[:, p, QL:QL + KVL], ACT.Square, scale=float(KVL) ** -0.5,
                                 accum_out=ssd2[:, p, 1:2]).then_inc(ms_ready, 1)
                for p in range(2):
                    ps = drawn(ra)
                    copy(qct[:, p, 0:P], ps[:, 0:P])
                    copy(qct[0:QL - P, p, P:2 * P], ps[0:QL - P, P:2 * P])
                    give(copy(qct[:, p, 2 * P:3 * P], ps[:, 2 * P:3 * P]))
                for p in range(2):
                    give(copy(va[:, p, :], drawn(ra)))
                for p in range(2):
                    for dst in (qT, kT):
                        for g in range(4):
                            give(copy(dst[:, p, 4 * g:4 * g + 4, :].rearrange("p a b -> p (a b)"), drawn(ra)[0:HQ, :]))
                for what, g in (("S", 0), ("S", 1), ("T", 0), ("S", 2), ("T", 1), ("S", 3), ("T", 2), ("T", 3)):
                    for p in range(2):
                        ps = drawn(ra)
                        if what == "S":
                            W(mx_ready, (2 * j) * 4 + 2 * g + p + 1)
                            for h in range(4):
                                hh = 4 * g + h
                                t = e.activation(pb[:, p, g % 2, h * P:(h + 1) * P], ps[:, h * P:(h + 1) * P], ACT.Exp,
                                                 bias=nmx[:, p, hh:hh + 1], scale=SC, accum_out=rs[:, p, hh:hh + 1])
                            give(t)
                        else:
                            give(copy(pT[:, p, g % 2, :], ps))
                for p in range(2):
                    give(copy(oT[:, p, :, :].rearrange("p a b -> p (a b)"), drawn(ra)))
            barrier(e, 4)
            if stop == "D":
                return

            with e.Fori(0, B // 2) as j:
                ra = Ring([0, 1], A_R + j * 2 * A_RN)
                for p in range(2):
                    give(copy(x3T[:, p, :, :].rearrange("p a b -> p (a b)"), drawn(ra)))
                for p in range(2):
                    W(nlm_ready, 2 * j + p + 1)
                    e.activation(ex[:, p, :], lgt[:, p, :], ACT.Exp, bias=nlm[:, p:p + 1]).then_inc(ex_ready, 1)
            barrier(e, 5)
            ffn(A_S, A_SN, NSH, lambda f: P, 4, 4)
            barrier(e, 6)
            with e.Fori(0, NPAIR // 2) as j:
                ra = Ring([0, 1, 2, 3], A_E + j * 4)
                for q in range(2):
                    give(copy(xgT[:, q, :, :].rearrange("p a b -> p (a b)"), drawn(ra)))
                for q in range(2):
                    ps = drawn(ra)
                    e.activation(sgE[:, q, :], ps[:, 0:P], ACT.Silu).then_inc(act_free, 1)
            barrier(e, 7)

        @block.vector
        def _(e):
            W = lambda s, v: wait(e, idle["dve"], s, v)
            tt, ts, stt_ = e.tensor_tensor, e.tensor_scalar, e.scalar_tensor_tensor
            st = Steps(dve_step)

            def link(ins):
                v = st.up(ins)
                W(dve_step, v)

            def drawn(ring):
                n, b = ring.take()
                W(dve_full, n + 1)
                return psum[:, b, :]

            def give(ins):
                ins.then_inc(dve_free, 1)

            def spread(x, h, w):
                return x.unsqueeze(2).to_broadcast([x.shape[0], h, w])

            def stats(src, k):
                link(e.bn_stats(stat[:, k, 0:6], src))
                e.bn_aggr(mv[:, k, :], stat[:, k, 0:6]).then_inc(var_ready, 1)

            e.sem_inc(dve_free, CREDIT)
            e.sem_inc(down_free, CREDIT)
            e.sem_inc(qi_used, 2)
            e.sem_inc(qt_used, 1)
            e.sem_inc(xh_used, 3)
            for s in (qw_stored, ye_out, ac_out):
                e.sem_inc(s, 1)
            e.wait_ge(ld_a, 16 * NLD_A)
            rv = Ring(V_AB)
            e.wait_ge(rstd_ready, 1)
            stt_(e1[:], emb[:], rstd[:, 0:1], nw[:], ALU.mult, ALU.mult).then_inc(x_ready, 1)
            tt(lutd[:], lutb[:].rearrange("p (a b) -> p a b", b=2)[:, :, 1], lutb[:].rearrange("p (a b) -> p a b", b=2)[:, :, 0],
               ALU.subtract)
            ts(onehot[:], xtok[:], cst[:, C_P:C_P + 1], None, ALU.is_equal).then_inc(hot_ready, 1)
            ps = drawn(rv)
            t = e.tensor_copy(hraw[:], ps)
            t.then_inc(hraw_ready, 1)
            e.wait_ge(hraw_ready, 1)
            e.sem_inc(dve_free, 1)
            e.wait_ge(rstd_ready, 2)
            link(ts(htab[:], hraw[:], rstd[:, 1:2], None, ALU.mult))
            tt(htabb[:], htab[:], outb[:], ALU.add).then_inc(tab_ready, 1)
            stats(htab[:], 0)
            e.wait_ge(var_ready, 1)
            e.wait_ge(rstd_ready, 3)
            t = ts(xtab[:], htab[:], mv[:, 0, 0:1], rstd[:, 2:3], ALU.subtract, ALU.mult)
            t.then_inc(x_ready, 1)
            e.wait_ge(x_ready, 2)
            ps = drawn(rv)
            link(tt(bc[:], ps[:, 0:160], bcb[:], ALU.add))
            e.sem_inc(dve_free, 1)
            link(ts(sp4[:, 3, :], bc[:, 128:160], -1.0, None, ALU.mult))
            tt(sp4[:, 0, :], sp4[:, 3, :], bc[:, 128:160], ALU.min).then_inc(dtin_ready, 1)
            e.tensor_copy(stab[:, 0:64], bc[:, 0:64])
            e.wait_ge(sp_ready, 2)
            link(stt_(stab[:, 64:96], bc[:, 128:160], 0.0, sp4[:, 2, :], ALU.max, ALU.add))
            link(stt_(stab[:, 96:128], stab[:, 64:96], -1.0, alog[:], ALU.mult, ALU.mult))
            e.drain().then_inc(tab_ready, 2)
            e.sem_inc(dve_free, 2)
            e.sem_inc(dve_full, 2)
            barrier(e, 1)
            base = st.now()
            stc = [st]

            def link(ins):
                v = stc[0].up(ins)
                W(dve_step, v)

            BPER = SSD_LINKS
            with e.Fori(0, B // 2) as j:
                stc[0] = Steps(dve_step, base + j * BPER)
                rv = Ring(V_AB, V_B + j * 2 * V_BN)

                def masks(c):
                    n = 4 * j + c
                    W(qi_ld[c % 2], 32 * j + 16 * (c // 2) + 16)
                    for b in (3, 2, 1, 0):
                        t = ts(qm[:, b, :], qi[:, c % 2, :], 1 << b, None, ALU.bitwise_and)
                    link(t)
                    e.sem_inc(qm_ready, 1)
                    e.sem_inc(qi_used, 1)

                def pick(c):
                    n = 4 * j + c
                    W(qt_ready, 8 * n + 8)
                    for lv, w in ((1, 1), (2, 2), (3, 4)):
                        for t in range(0, 8, 2 * w):
                            x = e.copy_predicated(qt[:, t, :], qm[:, lv, :], qt[:, t + w, :])
                        link(x)
                    e.sem_inc(qw_ready, 1)
                    e.sem_inc(qt_used, 1)

                for p in range(2):
                    i = 2 * j + p
                    ii = e.snap(i)
                    W(xh_ld[p], 32 * j + 32)
                    link(tt(xdt[:, p, :].rearrange("p (h w) -> p h w", w=HP), xg[:, p, :].rearrange("p (h w) -> p h w", w=HP),
                            spread(small[:, bass.ds(ii, 1), 64:96].rearrange("p a h -> p (a h)"), H0, HP), ALU.mult))
                    tt(xdd[:, p, :].rearrange("p (h w) -> p h w", w=HP), xdt[0:CH, p, :].rearrange("p (h w) -> p h w", w=HP),
                       spread(dec[0:CH, bass.ds(ii, 1), :].rearrange("p a h -> p (a h)"), H0, HP), ALU.mult).then_inc(xd_ready, 1)
                masks(0)
                for p in range(2):
                    ps = drawn(rv)
                    link(tt(mm[:, p, :], ps[:, 0:CH], cst[:, C_TRI:C_TRI + CH], ALU.mult))
                    e.sem_inc(dve_free, 1)
                pick(0)
                masks(1)
                for q in range(2):
                    for p in range(2):
                        for hh in range(2):
                            h = 16 * q + 8 * hh
                            W(act_free, A_B + j * 2 * A_BN + 4 + 4 * q + 2 * p + hh + 1 + CREDIT)
                            tt(lg[:, p, h:h + 8, :], lg[:, p, h:h + 8, :],
                               mm[:, p, :].unsqueeze(1).to_broadcast([P, 8, CH]), ALU.mult).then_inc(g_ready, 1)
                    pick(1 + q)
                    masks(2 + q)
                for p in range(2):
                    i = 2 * j + p
                    ii = e.snap(i)
                    ps = drawn(rv)
                    x3 = xg[:, p, :].rearrange("p (h w) -> p h w", w=HP)
                    link(tt(ysb[:, p, :].rearrange("p (h w) -> p h w", w=HP), x3, spread(dskip[:], H0, HP), ALU.mult))
                    link(tt(ysb[:, p, :], ysb[:, p, :], ps, ALU.add))
                    e.sem_inc(dve_free, 1)
                    ps = drawn(rv)
                    link(tt(xdt[CH:P, p, :].rearrange("p (h w) -> p h w", w=HP), ps[CH:P, :].rearrange("p (h w) -> p h w", w=HP),
                            spread(ecs[CH:P, bass.ds(ii, 1), :].rearrange("p a h -> p (a h)"), H0, HP), ALU.mult))
                    e.sem_inc(dve_free, 1)
                    tt(ysb[CH:P, p, :], ysb[CH:P, p, :], xdt[CH:P, p, :], ALU.add).then_inc(y_ready, 1)
                pick(3)
                for p in range(2):
                    i = 2 * j + p
                    ii = e.snap(i)
                    ps = drawn(rv)
                    link(tt(hres[:, bass.ds(ii, 1), :].rearrange("p a d -> p (a d)"), ps, hg[:, p, :], ALU.add))
                    e.sem_inc(dve_free, 1)
                    e.sem_inc(xh_used, 2)
                assert stc[0].k == BPER, stc[0].k
            base += B // 2 * BPER
            barrier(e, 2)
            if stop == "B":
                return

            def norm(ii, q, seen_v, seen_r, seen_full, out_sem):
                pass

            def ffn(base, base_v, nv, nf, seen_x, seen_r, rows, groups_before, act_t, base_a, na):
                per = None
                with e.Fori(0, 4) as g:
                    stc[0] = Steps(dve_step, base + g * FFN_LINKS)
                    rv = Ring([2, 3], base_v + g * nv)
                    for q in range(4):
                        ii = e.snap(g * 4 + q)
                        hrow = hres[:, bass.ds(ii, 1), :].rearrange("p a d -> p (a d)")
                        link(e.bn_stats(stat[:, q % 2, 0:6], hrow))
                        e.bn_aggr(mv[:, q % 2, :], stat[:, q % 2, 0:6]).then_inc(var_ready, 1)
                        W(rstd_ready, seen_r + g * 4 + q + 1)
                        W(var_ready, seen_x - 1 + g * 4 + q + 1)
                        if q >= 2:
                            W(act_full, base_a + g * na + q - 1)
                        ts(xn[:, q % 2, :], hrow, mv[:, q % 2, 0:1], rstd[:, q % 2:q % 2 + 1],
                           ALU.subtract, ALU.mult).then_inc(x_ready, 1)
                        if q >= act_t:
                            ps = drawn(rv)
                            give(e.tensor_copy(xT[:, :, q * P:(q + 1) * P], ps.rearrange("p (a b) -> p a b", a=KD)))
                    for f in range(nf):
                        m = rows(f)
                        ps = drawn(rv)
                        W(act_free, base_a + g * na + act_t + f + 1 + CREDIT)
                        if f >= 2:
                            W(hT_used, groups_before * NF + g * nf + f - 1)
                        t = tt(hT[0:m, f % 2, :], sg[0:m, f % 2, :], ps[0:m, :], ALU.mult)
                        t.then_inc(hT_ready, 1)
                        W(hT_ready, groups_before * NF + g * nf + f + 1)
                        e.sem_inc(dve_free, 1)
                    W(down_full, groups_before + g + 1)
                    for q in range(4):
                        ii = e.snap(g * 4 + q)
                        hrow = hres[:, bass.ds(ii, 1), :].rearrange("p a d -> p (a d)")
                        link(tt(hrow, psum[:, 4 + q, :], hrow, ALU.add))
                        e.sem_inc(down_free, 1)
                    assert stc[0].k == FFN_LINKS, stc[0].k

            e.sem_inc(idle["dve"], 1)
            ffn(base, V_C, V_CN, NF, 2, 3, rows0, 0, 3, A_C, A_CN)
            base += 4 * FFN_LINKS
            barrier(e, 3)
            if stop == "C":
                return
            assert base == D_STEPS0, base

            e.wait_ge(ld_d, 16 * 7)
            cos = cst[:, C_COS:C_COS + RD]
            sin = cst[:, C_SIN:C_SIN + RD]
            HR = RD // 2
            with e.Fori(0, B // 2) as j:
                stc[0] = Steps(dve_step, base + j * D_PERIOD)
                rv = Ring(V_AB, V_D + j * 2 * V_DN)
                RB = 3 + B
                for p in range(2):
                    ii = e.snap(2 * j + p)
                    hrow = hres[:, bass.ds(ii, 1), :].rearrange("p a d -> p (a d)")
                    link(e.bn_stats(stat[:, p, 0:6], hrow))
                    e.bn_aggr(mv[:, p, :], stat[:, p, 0:6]).then_inc(var_ready, 1)
                for p in range(2):
                    ii = e.snap(2 * j + p)
                    hrow = hres[:, bass.ds(ii, 1), :].rearrange("p a d -> p (a d)")
                    W(rstd_ready, RB + 4 * j + p + 1)
                    W(var_ready, 1 + B + 2 * j + p + 1)
                    ts(xn[:, p, :], hrow, mv[:, p, 0:1], rstd[:, p:p + 1], ALU.subtract, ALU.mult).then_inc(x_ready, 1)
                for p in range(2):
                    ps = drawn(rv)
                    link(e.tensor_copy(lat[:, p, :], ps[:, 0:384]))
                    assert stc[0].k == D_LAT[p], stc[0].k
                    e.sem_inc(dve_free, 1)
                    link(tt(rt1[:, 0, :], lat[:, p, 320:384], cos, ALU.mult))
                    tt(rt2[:, 0, 0:HR], lat[:, p, 320 + HR:384], sin[:, 0:HR], ALU.mult)
                    link(tt(rt2[:, 0, HR:RD], lat[:, p, 320:320 + HR], sin[:, HR:RD], ALU.mult))
                    link(tt(rt1[:, 0, :], rt1[:, 0, :], rt2[:, 0, :], ALU.add))
                    link(e.tensor_copy(ka[:, p, :, HD:HQ], rt1[:, 0, :].unsqueeze(1).to_broadcast([P, H1, RD])))
                for p in range(2):
                    W(rstd_ready, RB + 4 * j + 2 + p + 1)
                    link(stt_(lat[:, p, 0:QL], lat[:, p, 0:QL], rr[:, p, 0:1], gqb[:], ALU.mult, ALU.mult))
                    link(stt_(lat[:, p, QL:QL + KVL], lat[:, p, QL:QL + KVL], rr[:, p, 1:2], gkb[:], ALU.mult, ALU.mult))
                    e.sem_inc(lat_ready, 1)
                for p in range(2):
                    for g in range(4):
                        ps = drawn(rv)[:, 0:384].rearrange("p (h w) -> p h w", w=HQ)
                        e.tensor_copy(qa[:, p, 4 * g:4 * g + 4, 0:HD], ps[:, :, 0:HD])
                        tt(rt1[:], ps[:, :, HD:HQ], cos.unsqueeze(1).to_broadcast([P, 4, RD]), ALU.mult)
                        tt(rt2[:, :, 0:HR], ps[:, :, HD + HR:HQ], sin[:, 0:HR].unsqueeze(1).to_broadcast([P, 4, HR]), ALU.mult)
                        link(tt(rt2[:, :, HR:RD], ps[:, :, HD:HD + HR], sin[:, HR:RD].unsqueeze(1).to_broadcast([P, 4, HR]), ALU.mult))
                        e.sem_inc(dve_free, 1)
                        link(tt(qa[:, p, 4 * g:4 * g + 4, HD:HQ], rt1[:], rt2[:], ALU.add))
                        e.sem_inc(rope_ready, 1)
                    ps = drawn(rv)
                    link(e.tensor_copy(ka[:, p, :, 0:HD], ps.rearrange("p (h w) -> p h w", w=HD)))
                    e.sem_inc(dve_free, 1)
                    e.sem_inc(rope_ready, 1)
                at = {0: 22, 1: 24, 2: 28, 3: 32}
                for g in range(4):
                    for p in range(2):
                        k = at[g] + p
                        W(act_full, A_D + j * 2 * A_DN + k + 1)
                        ps = psum[:, A_AB[k % 4], :]
                        link(e.tensor_reduce(mx[:, p, 4 * g:4 * g + 4], ps.rearrange("p (h w) -> p h w", w=P), AX.X, ALU.max))
                        ts(nmx[:, p, 4 * g:4 * g + 4], mx[:, p, 4 * g:4 * g + 4], -float(HQ) ** -0.5, None, ALU.mult).then_inc(mx_ready, 1)
                for p in range(2):
                    W(act_free, A_D + j * 2 * A_DN + at[3] + p + 1 + CREDIT)
                    link(e.reciprocal(ri[:, p, :], rs[:, p, :]))
                    ps = drawn(rv)
                    link(tt(ob[:, p, :].rearrange("p (h w) -> p h w", w=HD), ps.rearrange("p (h w) -> p h w", w=HD),
                            spread(ri[:, p, :], H1, HD), ALU.mult))
                    e.sem_inc(dve_free, 1)
                    e.sem_inc(o_ready, 1)
                for p in range(2):
                    ii = e.snap(2 * j + p)
                    hrow = hres[:, bass.ds(ii, 1), :].rearrange("p a d -> p (a d)")
                    ps = drawn(rv)
                    link(tt(hrow, ps, hrow, ALU.add))
                    e.sem_inc(dve_free, 1)
                assert stc[0].k == D_PERIOD, stc[0].k
            base += B // 2 * D_PERIOD
            barrier(e, 4)
            if stop == "D":
                return

            e.wait_ge(ld_r, 32)
            stc[0] = Steps(dve_step, base)
            link(e.memset(cum[:, 2, :], 0.0))
            base += 1
            iota = cst[:, C_IOTA:C_IOTA + E]
            with e.Fori(0, B // 2) as j:
                stc[0] = Steps(dve_step, base + j * R_PERIOD)
                rv = Ring([4, 5], V_R + j * 2 * V_RN)
                RB = 3 + B + 2 * B
                link(e.tensor_copy(cum[:, 0, :], cum[:, 2, :]))
                for p in range(2):
                    ii = e.snap(2 * j + p)
                    hrow = hres[:, bass.ds(ii, 1), :].rearrange("p a d -> p (a d)")
                    link(e.bn_stats(stat[:, p, 0:6], hrow))
                    e.bn_aggr(mv[:, p, :], stat[:, p, 0:6]).then_inc(var_ready, 1)
                for p in range(2):
                    ii = e.snap(2 * j + p)
                    hrow = hres[:, bass.ds(ii, 1), :].rearrange("p a d -> p (a d)")
                    W(rstd_ready, RB + 2 * j + p + 1)
                    W(var_ready, 1 + 2 * B + 2 * j + p + 1)
                    ts(xn[:, p, :], hrow, mv[:, p, 0:1], rstd[:, p:p + 1], ALU.subtract, ALU.mult).then_inc(x_ready, 1)
                for p in range(2):
                    ps = drawn(rv)
                    e.tensor_copy(lgt[:, p, :], ps[:, 0:E])
                    link(tt(bia[:, p, :], ps[:, 0:E], rb[:], ALU.add))
                    e.sem_inc(dve_free, 1)
                    link(e.tensor_reduce(nlm[:, p:p + 1], lgt[:, p, :], AX.X, ALU.max, negate=True))
                    e.sem_inc(nlm_ready, 1)
                    link(e.max(top[:, p, :], bia[:, p, :]))
                    link(e.max_index(topi[:, p, :], top[:, p, :], bia[:, p, :]))
                    link(e.tensor_copy(topf[:, p, :], topi[:, p, 0:TOPK]))
                    link(tt(hot[:, p, :, :], iota.unsqueeze(1).to_broadcast([P, TOPK, E]),
                            spread(topf[:, p, :], TOPK, E), ALU.is_equal))
                    link(e.tensor_reduce(msk[:, p, :], hot[:, p, :, :].rearrange("p k e -> p e k"), AX.X, ALU.add))
                    e.sem_inc(msk_ready, 1)
                    link(tt(cum[:, p + 1, :], cum[:, p, :], msk[:, p, :], ALU.add))
                    e.sem_inc(msk_ready, 1)
                for p in range(2):
                    ii = e.snap(2 * j + p)
                    W(ex_ready, 2 * j + p + 1)
                    link(tt(hw[:, p, :, :], hot[:, p, :, :], ex[:, p, :].unsqueeze(1).to_broadcast([P, TOPK, E]), ALU.mult))
                    link(e.tensor_reduce(tk[:, p, 0, :], hw[:, p, :, :], AX.X, ALU.add))
                    link(e.tensor_reduce(tsum[:, p, 0:1], tk[:, p, 0, :], AX.X, ALU.add))
                    link(e.reciprocal(tsum[:, p, 1:2], tsum[:, p, 0:1]))
                    ps = drawn(rv)
                    link(tt(hw[:, p, :, :], hot[:, p, :, :], ps[:, 0:E].unsqueeze(1).to_broadcast([P, TOPK, E]), ALU.mult))
                    e.sem_inc(dve_free, 1)
                    link(e.tensor_reduce(tk[:, p, 1, :], hw[:, p, :, :], AX.X, ALU.add))
                    link(ts(tk[:, p, 2, :], tk[:, p, 1, :], float(CAP), None, ALU.is_lt))
                    link(stt_(tk[:, p, 3, :], topf[:, p, :], float(CAP), tk[:, p, 1, :], ALU.mult, ALU.add))
                    link(tt(tk[:, p, 4, :], tk[:, p, 3, :], tk[:, p, 2, :], ALU.mult))
                    e.tensor_copy(gslot[:, bass.ds(ii, 1), :].rearrange("p a k -> p (a k)"), tk[:, p, 4, :])
                    stt_(wslot[:, bass.ds(ii, 1), :].rearrange("p a k -> p (a k)"), tk[:, p, 0, :], tsum[:, p, 1:2], tk[:, p, 2, :], ALU.mult, ALU.mult)
                    link(ts(tk[:, p, 5, :], tk[:, p, 2, :], -2.0 * E * CAP, 2.0 * E * CAP, ALU.mult, ALU.add))
                    link(tt(islot[:, p, :], tk[:, p, 4, :], tk[:, p, 5, :], ALU.add))
                    e.sem_inc(slot_ready, 1)
                W(scattered, 16 * 2 * TOPK * (j + 1))
                assert stc[0].k == R_PERIOD, stc[0].k
            base += B // 2 * R_PERIOD
            barrier(e, 5)
            ffn(base, V_S, V_SN, NSH, 2 + 3 * B, 3 + 4 * B, lambda f: P, 4, 4, A_S, A_SN)
            base += 4 * FFN_LINKS
            e.sem_inc(we_used, 2)
            barrier(e, 6)
            with e.Fori(0, NPAIR // 2) as j:
                stc[0] = Steps(dve_step, base + j * 4)
                rv = Ring([4, 5, 6, 7], V_E + j * 4)
                for q in range(2):
                    n = 2 * j + q
                    ps = drawn(rv)
                    W(act_free, A_E + j * 4 + 2 + q + 1 + CREDIT)
                    link(tt(hE[:, q, :], sgE[:, q, :], ps[:, 0:P], ALU.mult))
                    e.sem_inc(dve_free, 1)
                    e.sem_inc(he_ready, 1)
                W(ye_out, 32 * j + 1)
                for q in range(2):
                    link(e.tensor_copy(yE[:, q, :], drawn(rv)))
                    e.sem_inc(dve_free, 1)
                    e.sem_inc(ye_ready, 1)
                    e.sem_inc(we_used, 1)
            base += NPAIR // 2 * 4
            barrier(e, 7)
            with e.Fori(0, B // 2) as j:
                stc[0] = Steps(dve_step, base + j * 10)
                for p in range(2):
                    ii = e.snap(2 * j + p)
                    W(ac_out, 32 * j + 1)
                    e.tensor_copy(cw[:, p, :], wslot[:, bass.ds(ii, 1), :].rearrange("p a k -> p (a k)"))
                    link(e.tensor_copy(cix[:, p, :], gslot[:, bass.ds(ii, 1), :].rearrange("p a k -> p (a k)")))
                    e.sem_inc(cix_ready, 1)
                for p in range(2):
                    ii = e.snap(2 * j + p)
                    W(yk_ld[p], 64 * j + 64)
                    for k in range(TOPK):
                        link(stt_(ac[:, p, :], yk[:, p, k, :], cw[:, p, k:k + 1],
                                  ac[:, p, :] if k else hres[:, bass.ds(ii, 1), :].rearrange("p a d -> p (a d)"),
                                  ALU.mult, ALU.add))
                    e.sem_inc(ac_ready, 1)


def rows0(f):
    return P if f < NF - 1 else INTER - (NF - 1) * P


SSD_LINKS = 28
FFN_LINKS = 8
D_LAT = (3, 8)
D_PERIOD = 48
D_STEPS0 = 6 + 8 * SSD_LINKS + 4 * FFN_LINKS
R_PERIOD = 41


def constants():
    import numpy as np
    c = np.zeros((P, C_N), np.float32)
    k, m = np.arange(P)[:, None], np.arange(P)[None, :]
    same = (k // CH) == (m // CH)
    c[:, C_ID:C_ID + P] = k == m
    c[:, C_GT:C_GT + P] = same & (k > m)
    c[:, C_LE:C_LE + P] = same & (k <= m)
    c[:, C_STR:C_STR + P] = k < m
    c[:, C_ONE:C_ONE + P] = 1.0
    c[:, C_TRI:C_TRI + CH] = (k % CH) <= m[:, :CH]
    c[:, C_IOTA:C_IOTA + E] = m[:, :E]
    inv = np.float32(1.0) / np.float32(10000.0) ** (np.arange(0, RD, 2, dtype=np.float32) / np.float32(RD))
    ang = np.arange(P, dtype=np.float32)[:, None] * inv[None, :]
    c[:, C_COS:C_COS + RD] = np.concatenate([np.cos(ang)] * 2, 1)
    c[:, C_SIN:C_SIN + RD] = np.concatenate([-np.sin(ang), np.sin(ang)], 1)
    c[:, C_P] = np.arange(P)
    return c


def arrange(x):
    import numpy as np
    x = {k: np.asarray(v) for k, v in x.items()}

    def tiles(w):
        return np.ascontiguousarray(w.reshape(-1, P, w.shape[1]).transpose(1, 0, 2))

    o = {"consts": constants()}
    tok = x["x"]
    o["tokix"], o["xtok"] = np.ascontiguousarray(tok.T), tok.reshape(-1)
    o["emb"], o["nw"] = x["L0_tok_emb_table"], x["L0_tok_norm_weight"]
    o["projT"] = tiles(x["L0_tok_proj_weight"].T)
    o["bcdtT"] = tiles(np.concatenate([x["L0_attn_B_w"], x["L0_attn_C_w"], x["L0_attn_dt_w"]], 0).T)
    o["bcb"] = np.concatenate([x["L0_attn_B_b"], x["L0_attn_C_b"], x["L0_attn_dt_b"]])
    o["alog"], o["dskip"] = x["L0_attn_A_log"], x["L0_attn_D"]
    o["owT"], o["outb"] = tiles(x["L0_attn_out_w"].T), x["L0_attn_out_b"]
    o["lut"] = x["L0_ffn_lut"]
    down = np.zeros((NF * P, D), np.int32)
    down[:INTER] = x["L0_ffn_down_idx"].T
    o["lutidx"] = np.concatenate([tiles(w).reshape(P, -1) for w in
                                  (x["L0_ffn_gate_idx"].T, x["L0_ffn_up_idx"].T, down)], 1)
    o["wq3"] = tiles(np.concatenate([x["L1_attn_Wcq"], x["L1_attn_Wckv"], x["L1_attn_Wkr"]], 1))
    o["wdq"] = np.concatenate([x["L1_attn_Wdq"].reshape(QL, H1, HD), x["L1_attn_Wdqr"].reshape(QL, H1, RD)],
                              2).reshape(QL, H1 * HQ)
    o["wdkv"] = np.concatenate([x["L1_attn_Wdk"], x["L1_attn_Wdv"]], 1)
    o["wo"] = tiles(x["L1_attn_Wo"])
    o["gq"], o["gkv"] = x["L1_attn_g_q"], x["L1_attn_g_kv"]
    o["rwT"], o["rb"] = tiles(x["L1_ffn_router_w"].T), x["L1_ffn_router_bias"]
    sg, su, sd = x["L1_ffn_sh_gate_w"], x["L1_ffn_sh_up_w"], x["L1_ffn_sh_down_w"]
    o["shw"] = np.concatenate([tiles(w).reshape(P, -1) for w in
                               (sg.reshape(SHF, D).T, su.reshape(SHF, D).T, sd.transpose(0, 2, 1).reshape(SHF, D))], 1)

    def expert(w):
        return w.transpose(0, 2, 1).reshape(E, KD, P, F).transpose(0, 2, 1, 3).reshape(E, P, KD * F)

    o["wexp"] = np.concatenate([expert(x["L1_ffn_gate_w"]), expert(x["L1_ffn_up_w"]),
                                x["L1_ffn_down_w"].transpose(0, 2, 1)], 2).reshape(E * P, 3 * D)
    return {k: np.ascontiguousarray(v) for k, v in o.items()}


def kernel(**inputs):
    import concourse.bacc as bacc
    from concourse.bass_utils import run_bass_kernel_spmd

    arrays = arrange(inputs)
    nc = bacc.Bacc("TRN2", target_bir_lowering=False, num_devices=1)
    a = {k: nc.dram_tensor(f"in_{k}", v.shape, mybir.dt.from_np(v.dtype), kind="ExternalInput").ap()
         for k, v in arrays.items()}
    out = nc.dram_tensor("out_h", (B, P, D), F32, kind="ExternalOutput").ap()
    tower(nc, a, out)
    r = run_bass_kernel_spmd(nc, [{f"in_{k}": v for k, v in arrays.items()}], core_ids=[0])
    return r.results[0]["out_h"]
```

```python
from contextlib import ExitStack

import concourse.bass as bass
from concourse import mybir

F32 = mybir.dt.float32
F32R = mybir.dt.float32r
I32 = mybir.dt.int32
U32 = mybir.dt.uint32
ALU = mybir.AluOpType
ACT = mybir.ActivationFunctionType
AX = mybir.AxisListType

P = 128
B = 16
D = 512
KD = D // P
V = 128
H0, HP, N0 = 32, 16, 64
HG = 4
NG = H0 // HG
INTER = 1376
NF = 11
H1, HD, RD = 16, 32, 64
HQ = HD + RD
QL, KVL = 192, 128
E, TOPK, F, CAP = 64, 4, 128, 64
SHF = 1024
EPS_RMS, EPS_LN = 1e-6, 1e-5
CREDIT = 4
LUTN = 520
LUT_COLS = 2 * KD * INTER + NF * D
NCHUNK = LUT_COLS // LUTN
G4 = 4

C_ID, C_GT, C_TRI, C_STR, C_ONE, C_IOTA, C_COS, C_SIN, C_P = 0, 128, 256, 384, 512, 640, 704, 768, 832
C_TOK = C_P + 1
C_ODD = C_TOK + B
C_META = C_ODD + 1
C_N = C_META + 2 * E * CAP // P
ACC = B * P + CAP


class Steps:

    def __init__(self, sem, base=0):
        self.sem, self.base, self.k = sem, base, 0

    def up(self, ins):
        ins.then_inc(self.sem, 1)
        self.k += 1
        return self.base + self.k

    def now(self):
        return self.base + self.k


class Ring:

    def __init__(self, banks, base=0, shift=0):
        self.banks, self.base, self.shift, self.k = banks, base, shift, 0

    def take(self):
        n, bank = self.base + self.k, self.banks[(self.k + self.shift) % len(self.banks)]
        self.k += 1
        return n, bank


def at(e, x):
    return x if isinstance(x, int) else e.snap(x)


def wait(e, idle, sem, value):
    e.wait_ge(sem, value)
    if not isinstance(value, int):
        e.sem_inc(idle, 1)


def tower(nc, a, out, stop=None):
    with ExitStack() as ctx:
        def sem(name):
            return ctx.enter_context(nc.semaphore(name))

        def sbuf(scope, name, shape, dt=F32):
            return scope.enter_context(nc.sbuf_tensor(name, shape, dt))

        hres = sbuf(ctx, "hres", [P, B, D])
        cst = sbuf(ctx, "cst", [P, C_N])
        stat = sbuf(ctx, "stat", [P, 4, 8])
        mv = sbuf(ctx, "mv", [P, 4, 2])
        rstd = sbuf(ctx, "rstd", [P, 4])
        veps = sbuf(ctx, "veps", [P, 4])
        mhalf = sbuf(ctx, "mhalf", [P, 1])
        ident = cst[:, C_ID:C_ID + P]
        psum = ctx.enter_context(nc.psum_tensor("psum", [P, 8, 512], F32))

        sw = ExitStack()
        wreg = sbuf(sw, "wreg", [P, LUT_COLS])
        sw.close()
        sw = ExitStack()
        wlo = sbuf(sw, "wlo", [P, LUT_COLS], F32R)
        sw.close()
        sw = ExitStack()
        slo = sbuf(sw, "slo", [P, 3 * SHF * KD], F32R)
        xhiS = sbuf(sw, "xhiS", [P, KD, G4 * P], F32R)
        xgT = sbuf(sw, "xgT", [P, 2, KD, P])
        yE = sbuf(sw, "yE", [P, 2, D])
        sw.close()
        sw = ctx.enter_context(ExitStack())
        sbuf(sw, "w_region", [P, LUT_COLS])

        s1 = ctx.enter_context(ExitStack())
        zrow = sbuf(s1, "zrow", [P, D])
        onehot = sbuf(s1, "onehot", [P, B * P])
        owT = sbuf(s1, "owT", [P, KD, D])
        small = sbuf(s1, "small", [P, B, 2 * H0])
        bc = sbuf(s1, "bc", [P, 160])
        tokix = sbuf(s1, "tokix", [P, B], I32)
        dskip = sbuf(s1, "dskip", [P, H0])
        lutb = sbuf(s1, "lutb", [P, 16])
        lutd = sbuf(s1, "lutd", [P, 8])
        qi = sbuf(s1, "qi", [P, 2, LUTN], I32)
        qm = sbuf(s1, "qm", [P, 3, LUTN], I32)
        qm0 = sbuf(s1, "qm0", [P, 2, LUTN], I32)
        qt = sbuf(s1, "qt", [P, 2, 8, LUTN])
        sa = ExitStack()
        xtok = sbuf(sa, "xtok", [P, B * P], I32)
        projT = wreg[:, 0:KD * D].rearrange("p (k n) -> p k n", k=KD)
        emb = sbuf(sa, "emb", [P, D])
        nw = sbuf(sa, "nw", [P, D])
        outb = sbuf(sa, "outb", [P, D])
        junk = sbuf(sa, "junk", [P, D])
        e1 = sbuf(sa, "e1", [P, D])
        hraw = sbuf(sa, "hraw", [P, D])
        htab = sbuf(sa, "htab", [P, D])
        xtab = sbuf(sa, "xtab", [P, D])
        htabb = sbuf(sa, "htabb", [P, D])
        eT = sbuf(sa, "eT", [P, KD, V])
        xtT = sbuf(sa, "xtT", [P, KD, V])
        bcdtT = sbuf(sa, "bcdtT", [P, KD, 160])
        bcb = sbuf(sa, "bcb", [P, 160])
        alog = sbuf(sa, "alog", [P, H0])
        sp4 = sbuf(sa, "sp4", [P, 4, H0])
        stab = sbuf(sa, "stab", [P, 2 * H0])
        ssq = sbuf(sa, "ssq", [P, 2])
        sa.close()
        xg = sbuf(s1, "xg", [P, 2, D])
        hg = sbuf(s1, "hg", [P, 2, D])
        ixb = sbuf(s1, "ixb", [P, 2, 2], I32)
        segr = sbuf(s1, "segr", [P, 4, HG, P])
        lg = sbuf(s1, "lg", [P, 4, HG, P])
        mm = sbuf(s1, "mm", [P, 2, P])
        bct = sbuf(s1, "bct", [N0, 2, 2 * P])
        xdt = sbuf(s1, "xdt", [P, 2, D])
        xD = sbuf(s1, "xD", [P, 2, D])
        yT = xdt[:].rearrange("p s (a b) -> p s a b", a=KD)
        s1.close()

        sf = ExitStack()
        xn = sbuf(sf, "xn", [P, 2, D])
        sg = sbuf(sf, "sg", [P, 2, D])
        hhi = sbuf(sf, "hhi", [P, 2, D], F32R)
        hlo = sbuf(sf, "hlo", [P, 2, D], F32R)
        xlo = sbuf(sf, "xlo", [P, KD, G4 * P], F32R)
        sx = ExitStack()
        xhi = sbuf(sx, "xhi", [P, KD, G4 * P], F32R)
        whi = sbuf(sx, "whi", [P, LUT_COLS], F32R)
        sx.close()
        shi = sbuf(sf, "shi", [P, 3 * SHF * KD], F32R)
        xgE = sbuf(sf, "xgE", [P, 2, D])
        xm = sbuf(sf, "xm", [P, 2, 2])
        xix = sbuf(sf, "xix", [P, 2], I32)
        wE = sbuf(sf, "wE", [P, 2, 2, 3 * D])
        sgE = sbuf(sf, "sgE", [P, 2, P])
        hE = sbuf(sf, "hE", [P, 2, P])
        sf.close()

        s2 = ctx.enter_context(ExitStack())
        xa = sbuf(s2, "xa", [P, 2, D])
        wq3 = sbuf(s2, "wq3", [P, KD, 384])
        wdq = sbuf(s2, "wdq", [P, 2, H1 * HQ])
        wdkv = sbuf(s2, "wdkv", [P, 2 * D])
        wo = sbuf(s2, "wo", [P, KD, D])
        gqb = sbuf(s2, "gqb", [P, QL])
        gkb = sbuf(s2, "gkb", [P, KVL])
        sd = ExitStack()
        xT1 = sbuf(sd, "xT1", [P, 2, KD, P])
        lat = sbuf(sd, "lat", [P, 2, 384])
        qct = xa
        qa = sbuf(sd, "qa", [P, 2, H1, HQ])
        ka = sbuf(sd, "ka", [P, 2, H1, HQ])
        rt1 = sbuf(sd, "rt1", [P, 4, RD])
        rt2 = sbuf(sd, "rt2", [P, 4, RD])
        va = sbuf(sd, "va", [P, 2, D])
        qT, kT = (wreg[0:HQ, c:c + 2 * H1 * P].rearrange("p (s h t) -> p s h t", s=2, h=H1)
                  for c in (2 * KD * SHF, 2 * KD * SHF + 2 * H1 * P))
        mx = sbuf(sd, "mx", [P, 2, H1])
        nmx = sbuf(sd, "nmx", [P, 2, H1])
        rs = sbuf(sd, "rs", [P, 2, H1])
        ri = sbuf(sd, "ri", [P, 2, H1])
        pb = sbuf(sd, "pb", [P, 2, 2, D])
        pT = sbuf(sd, "pT", [P, 2, 2, D])
        qa_rows = qa[:].rearrange("p s h w -> p s (h w)")
        ob, oT, scratch = (qa_rows[:, :, c * D:(c + 1) * D] for c in range(3))
        oT = oT.rearrange("p s (a b) -> p s a b", a=KD)
        ssd2 = sbuf(sd, "ssd2", [P, 2, 2])
        rr = sbuf(sd, "rr", [P, 2, 2])
        rv2 = sbuf(sd, "rv2", [P, 2, 2])
        sr = sd
        xr = sbuf(sr, "xr", [P, 2, D])
        rwT = wreg[:, 2 * KD * SHF + 4 * H1 * P:2 * KD * SHF + 4 * H1 * P + KD * E].rearrange("p (k e) -> p k e", k=KD)
        rb = sbuf(sr, "rb", [P, E])
        x3T = sbuf(sr, "x3T", [P, 2, KD, P])
        lgt = sbuf(sr, "lgt", [P, 2, E])
        bia = sbuf(sr, "bia", [P, 2, E])
        ex = sbuf(sr, "ex", [P, 2, E])
        nlm = sbuf(sr, "nlm", [P, 2])
        top = sbuf(sr, "top", [P, 2, 8])
        topi = sbuf(sr, "topi", [P, 2, 8], U32)
        topf = sbuf(sr, "topf", [P, 2, TOPK])
        hot = sbuf(sr, "hot", [P, 2, TOPK, E])
        hw = sbuf(sr, "hw", [P, 2, TOPK, E])
        hp = sbuf(sr, "hp", [P, 2, TOPK, E])
        msk = sbuf(sr, "msk", [P, 2, E])
        cum = sbuf(sr, "cum", [P, 3, E])
        tk = sbuf(sr, "tk", [P, 6, 2, TOPK])
        tsum = sbuf(sr, "tsum", [P, 2, 2])
        islot = sbuf(sr, "islot", [P, 2, TOPK], I32)
        meta = sbuf(sr, "meta", [P, 2, TOPK, 2])
        sr.close()
        sc = ExitStack()
        ya = sbuf(sc, "ya", [P, 2, 2, D])
        ac = sbuf(sc, "ac", [P, 2, D])
        sc.close()

        d_h = nc.dram_tensor("tab_h", [V, D], F32).ap()
        d_x = nc.dram_tensor("tab_x", [V, D], F32).ap()
        d_s = nc.dram_tensor("tab_s", [V, 2 * H0], F32).ap()
        d_xg = nc.dram_tensor("slots_x", [E * CAP, D], F32).ap()
        d_meta = nc.dram_tensor("slots_meta", [E * CAP, 2], F32).ap()
        d_acc = nc.dram_tensor("acc", [2 * ACC, D], F32).ap()

        act_full, act_free = sem("act_full"), sem("act_free")
        dve_full, dve_free = sem("dve_full"), sem("dve_free")
        idle = {k: sem(f"idle_{k}") for k in ("pe", "act", "dve", "pool", "sp")}
        dve_step, act_step, pool_step = sem("dve_step"), sem("act_step"), sem("pool_step")
        phase_end = sem("phase_end")
        ld_a, ld_b, ld_c, ld_d, ld_r = (sem(f"ld_{x}") for x in "abcdr")
        var_ready, rstd_ready = sem("var_ready"), sem("rstd_ready")
        ms_ready = sem("ms_ready")
        x_ready = sem("x_ready")
        hraw_ready, dtin_ready, sp_ready, tab_ready, tab_stored = (
            sem(x) for x in ("hraw_ready", "dtin_ready", "sp_ready", "tab_ready", "tab_stored"))
        small_in, hot_ready, mhalf_ready = sem("small_in"), sem("hot_ready"), sem("mhalf_ready")
        xh_used = sem("xh_used")
        segr_ready = sem("segr_ready")
        g_ready, xd_ready, y_ready = sem("g_ready"), sem("xd_ready"), sem("y_ready")
        y_done = sem("y_done")
        qi_ld, xg_ld, hg_ld, qw_stored, we_ld, xe_ld, ya_ld = (
            [sem(f"{x}_{p}") for p in range(2)]
            for x in ("qi_in", "xg_in", "hg_in", "qw_stored", "we_in", "xe_in", "ya_in"))
        qi_used, qm_ready, qt_ready, qw_ready = (
            sem(x) for x in ("qi_used", "qm_ready", "qt_ready", "qw_ready"))
        xhi_ready, h_ready, hi_ready, hT_ready, hT_used, down_full, down_free = (
            sem(x) for x in ("xhi_ready", "h_ready", "hi_ready", "hT_ready", "hT_used", "down_full", "down_free"))
        whi_ready, wlo_ready, wlo_pool = sem("whi_ready"), sem("wlo_ready"), sem("wlo_pool")
        zrow_ready, dram_init = sem("zrow_ready"), sem("dram_init")
        lat_in, lat_ready, rope_ready, mx_ready, o_ready = (
            sem(x) for x in ("lat_in", "lat_ready", "rope_ready", "mx_ready", "o_ready"))
        var3_ready, rstd3_ready, x3_ready, xr_free = (
            sem(x) for x in ("var3_ready", "rstd3_ready", "x3_ready", "xr_free"))
        nlm_ready, ex_ready, msk_ready, slot_ready, scattered = (
            sem(x) for x in ("nlm_ready", "ex_ready", "msk_ready", "slot_ready", "scattered"))
        we_used, he_ready, ye_ready, ye_free, acc_added = (
            sem(x) for x in ("we_used", "he_ready", "ye_ready", "ye_free", "acc_added"))
        ya_used, ac_ready, ac_out = (sem(x) for x in ("ya_used", "ac_ready", "ac_out"))

        NLD_A = 13

        def bank(n):
            return psum[:, n, :]

        A_AB, V_AB = [0, 1, 2, 3], [4, 5, 6, 7]

        def barrier(e, k):
            e.drain().then_inc(phase_end, 1)
            e.wait_ge(phase_end, 5 * k)

        block = ctx.enter_context(nc.Block())

        A_B, V_B = 2, 2
        A_BN, V_BN = NG + 2, 2

        def ssd_rings(i, odd):
            if isinstance(i, int) and i == 0:
                a, v = 3, 1
                sa_, sv = 3, 1
            else:
                a, v = A_BN * i + 2, V_BN * i
                sa_, sv = 0 if odd else 2, 0
            return Ring(A_AB, A_B + a, sa_), Ring([4, 5], V_B + v, sv)

        def each_sequence(e, body):
            body(0, 0, True, False)
            with e.Fori(0, B // 2 - 1) as j:
                body(j, 1, False, False)
                body(j + 1, 0, False, False)
            body(B // 2 - 1, 1, False, True)
        A_C, V_C = A_B + B * A_BN, V_B + B * V_BN
        A_CN, V_CN = NF + 1, 4 + NF + 1
        A_D, V_D = A_C + 4 * A_CN, V_C + 4 * V_CN
        A_DN, V_DN, V_RN = 20, 8, 2
        A_S, V_S = A_D + B * A_DN, V_D + B * (V_DN + V_RN)

        def attention_rings(j):
            routed = 0 if isinstance(j, int) and j == 0 else j - 1
            early = 0 if isinstance(j, int) and j == B // 2 else 2
            return (Ring(A_AB, A_D + 2 * early + j * 2 * A_DN),
                    Ring(V_AB, V_D + early + j * 2 * V_DN + routed * 2 * V_RN, early))

        HEAD_STEPS = (("S", 0), ("S", 1), ("X", 0), ("T", 0), ("C", 0), ("S", 2), ("T", 1), ("V", 0), ("S", 3),
                      ("T", 2), ("V", 1), ("T", 3), ("V", 2), ("L", 0), ("V", 3))

        def score_places(last):
            k, places = 2 + 16, {}
            for what, g in HEAD_STEPS:
                if what == "S":
                    places[g] = k
                if what in "ST" or what in "XL" and not last:
                    k += 2
            return places
        NSH = SHF // P
        A_SN, V_SN = 3 * NSH, 4 + 3 * NSH
        SC_G, SC_D = KD * SHF, 2 * KD * SHF
        NPAIR = E // 2
        @block.sync
        def _(e):
            W = lambda s, v: wait(e, idle["sp"], s, v)
            for dst, src in ((cst[:], a["consts"]), (emb[:], a["emb"]), (projT, a["projT"]),
                             (nw[:], a["nw"].partition_broadcast(P)), (outb[:], a["outb"].partition_broadcast(P)),
                             (bcdtT[:], a["bcdtT"]), (bcb[:], a["bcb"].partition_broadcast(P)),
                             (alog[:], a["alog"].partition_broadcast(P)),
                             (dskip[:], a["dskip"].partition_broadcast(P)),
                             (lutb[:], a["lut"].partition_broadcast(P)), (tokix[:], a["tokix"]),
                             (xtok[:], a["xtok"].partition_broadcast(P)), (owT[:], a["owT"])):
                e.dma_start(dst, src).then_inc(ld_a, 16)
            e.wait_ge(tab_ready, 3)
            e.dma_start(d_h, htabb[:]).then_inc(tab_stored, 16)
            e.dma_start(d_x, xtab[:]).then_inc(tab_stored, 16)
            e.dma_start(d_s, stab[:]).then_inc(tab_stored, 16)
            barrier(e, 1)
            e.wait_ge(zrow_ready, 1)
            e.wait_ge(ld_a, 16 * NLD_A)
            def load(n, c):
                off = at(e, n * LUTN)
                if not (isinstance(n, int) and n < 2):
                    W(qi_used, n - 1)
                e.dma_start(qi[:, c, :], a["lutidx"][:, bass.ds(off, LUTN)]).then_inc(qi_ld[c], 16)

            def store(n, c):
                off, row = at(e, n * LUTN), at(e, n * P)
                e.dma_start(d_xg[bass.ds(row, P), :], zrow[:]).then_inc(dram_init, 16)
                e.dma_start(d_acc[bass.ds(row, P), :], zrow[:]).then_inc(dram_init, 16)
                W(qw_ready, n + 1)
                e.dma_start(wreg[:, bass.ds(off, LUTN)], qt[:, c, 0, :]).then_inc(qw_stored[c], 16)

            load(0, 0)
            load(1, 1)
            with e.Fori(0, NCHUNK // 2 - 1) as j:
                for c in range(2):
                    load(2 * j + 2 + c, c)
                    store(2 * j + c, c)
            store(NCHUNK - 2, 0)
            store(NCHUNK - 1, 1)
            e.dma_start(d_acc[NCHUNK * P:2 * ACC, :], zrow[:]).then_inc(dram_init, 16)
            e.dma_start(d_meta.rearrange("(n p) c -> p n c", p=P),
                        cst[:, C_META:C_N].rearrange("p (n c) -> p n c", c=2)).then_inc(dram_init, 16)
            e.wait_ge(dram_init, 16 * (2 * NCHUNK + 2))
            for c in range(2):
                e.wait_ge(qw_stored[c], 16 * NCHUNK // 2)
            barrier(e, 2)
            if stop != "B":
                barrier(e, 3)
                for dst, src in ((wq3[:], a["wq3"]), (wdq[:, 0, :], a["wdq"][0:P]), (wdq[0:QL - P, 1, :], a["wdq"][P:QL]),
                                 (wdkv[:], a["wdkv"]), (wo[:], a["wo"]),
                                 (gqb[:], a["gq"].partition_broadcast(P)), (gkb[:], a["gkv"].partition_broadcast(P))):
                    e.dma_start(dst, src).then_inc(ld_d, 16)
                e.dma_start(rwT, a["rwT"]).then_inc(ld_r, 16)
                e.dma_start(rb[:], a["rb"].partition_broadcast(P)).then_inc(ld_r, 16)
                e.dma_start(wreg[:, 0:SC_D], a["shw"][:, 0:SC_D]).then_inc(ld_c, 16)
                e.wait_ge(ld_c, 16)
                e.wait_ge(ld_d, 16 * 7)
                e.wait_ge(ld_r, 32)
            if stop not in ("B", "C"):
                barrier(e, 4)
            if stop not in ("B", "C", "D"):
                e.dma_start(wreg[:, SC_D:3 * SHF * KD], a["shw"][:, SC_D:3 * SHF * KD]).then_inc(ld_c, 16)
                def load_pair(n, q):
                    wrow, srow = (n * 2 * P, n * P) if isinstance(n, int) else (e.snap(n * 2 * P), e.snap(n * P))
                    if not (isinstance(n, int) and n < 2):
                        W(we_used, n - 1)
                    e.dma_start(wE[:, q, :, :], a["wexp"][bass.ds(wrow, 2 * P), :]
                                .rearrange("(e p) n -> p e n", p=P)).then_inc(we_ld[q], 16)
                    e.dma_start(xgE[:, q, :], d_xg[bass.ds(srow, P), :]).then_inc(xe_ld[q], 16)
                    e.dma_start(xm[:, q, :], d_meta[bass.ds(srow, P), :]).then_inc(xe_ld[q], 16)

                load_pair(0, 0)
                load_pair(1, 1)
                with e.Fori(0, (NPAIR - 2) // 2) as j:
                    for q in range(2):
                        load_pair(2 * j + 2 + q, q)
                barrier(e, 5)
                with e.Fori(0, B // 2) as j:
                    offs = [e.snap((2 * j + q) * P) for q in range(2)]
                    for q in range(2):
                        W(ya_used, 2 * j + q + 1)
                        for o in range(2):
                            e.dma_start(ya[:, q, o, :], d_acc[bass.ds(e.snap(offs[q] + o * ACC), P), :]).then_inc(ya_ld[q], 16)
                e.wait_ge(ac_out, 16 * B + 1)
            else:
                e.dma_start(out.rearrange("b t d -> t b d"), hres[:]).then_inc(ac_out, 16)
                e.wait_ge(ac_out, 17)

        @block.gpsimd
        def _(e):
            W = lambda s, v: wait(e, idle["pool"], s, v)
            st = Steps(pool_step)
            nr = [0]

            def rsqrt(src, k, scale, eps, src_sem, src_val):
                W(src_sem, src_val)
                st.up(e.tensor_scalar(veps[:, k:k + 1], src, scale, eps, ALU.mult, ALU.add))
                W(pool_step, st.now())
                e.tensor_tensor(rstd[:, k:k + 1], veps[:, k:k + 1], mhalf[:], ALU.pow).then_inc(rstd_ready, 1)

            def gather(dst, tab, ix, s):
                e.indirect_dma_start(dst, None, tab, bass.IndirectOffsetOnAxis(ap=ix, axis=0)).then_inc(s, 16)

            e.memset(zrow[:], 0.0).then_inc(zrow_ready, 1)
            e.memset(mhalf[:], -0.5).then_inc(mhalf_ready, 1)
            e.wait_ge(mhalf_ready, 1)
            rsqrt(ssq[:, 0:1], 0, 1.0 / D, EPS_RMS, ms_ready, 1)
            rsqrt(ssq[:, 1:2], 1, 1.0 / D, EPS_RMS, ms_ready, 2)
            rsqrt(mv[:, 0, 1:2], 2, 1.0, EPS_LN, var_ready, 1)
            e.wait_ge(ld_a, 16 * NLD_A)
            e.wait_ge(tab_stored, 48)
            for i in range(B):
                gather(small[:, i, :], d_s, tokix[:, i:i + 1], small_in)
            e.wait_ge(small_in, 16 * B)
            barrier(e, 1)
            def gather_rows(m, half, q, dst, tab, k, landed):
                ix = at(e, m)
                s = Steps(pool_step, 3 + 2 * m + k)
                s.up(e.tensor_copy(ixb[:, q, k:k + 1], tokix[:, bass.ds(ix, 1)]))
                W(pool_step, s.now())
                gather(dst[:, q, :], tab, ixb[:, q, k:k + 1], landed[q])

            def spans(m, g):
                ix = at(e, m)
                if not (isinstance(m, int) and m == 0 and g < 4):
                    W(g_ready, NG * m + g - 3)
                e.tensor_tensor(segr[:, g % 4, :, :],
                                small[:, bass.ds(ix, 1), H0 + HG * g:H0 + HG * g + HG].rearrange("p a h -> p (a h)").unsqueeze(2).to_broadcast([P, HG, P]),
                                cst[:, C_TRI:C_TRI + P].unsqueeze(1).to_broadcast([P, HG, P]),
                                ALU.mult).then_inc(segr_ready, 1)

            def by_head(x):
                return x.rearrange("p (h w) -> p h w", w=HP)

            def scale_x(m, half, q):
                ix = at(e, m)
                W(xg_ld[q], 16 * half + 16)
                e.tensor_tensor(by_head(xD[:, q, :]), by_head(xg[:, q, :]),
                                dskip[:].unsqueeze(2).to_broadcast([P, H0, HP]), ALU.mult)
                e.tensor_tensor(by_head(xdt[:, q, :]), by_head(xg[:, q, :]),
                                small[:, bass.ds(ix, 1), 0:H0].rearrange("p a h -> p (a h)").unsqueeze(2).to_broadcast([P, H0, HP]),
                                ALU.mult).then_inc(xd_ready, 1)

            gather_rows(0, 0, 0, xg, d_x, 0, xg_ld)
            gather_rows(0, 0, 0, hg, d_h, 1, hg_ld)
            for g in range(3):
                spans(0, g)
            scale_x(0, 0, 0)

            def step(j, odd, first, last):
                i = 2 * j + odd
                q, half = 1 - odd, j + odd
                if not last:
                    if not first:
                        W(xd_ready, i)
                    gather_rows(i + 1, half, q, xg, d_x, 0, xg_ld)
                for g in range(3, NG):
                    spans(i, g)
                if not last:
                    if not first:
                        W(xh_used, i)
                    scale_x(i + 1, half, q)
                    gather_rows(i + 1, half, q, hg, d_h, 1, hg_ld)
                    for g in range(3):
                        spans(i + 1, g)

            each_sequence(e, step)
            barrier(e, 2)
            if stop == "B":
                return
            base = 3 + 2 * B
            done = 3

            def ln_pairs(base, seen, n_pairs):
                with e.Fori(0, n_pairs) as j:
                    s = Steps(pool_step, j * 2 + base)
                    for p in range(2):
                        W(var_ready, seen + 1 + 2 * j + p)
                        s.up(e.tensor_scalar(veps[:, p:p + 1], mv[:, p, 1:2], 1.0, EPS_LN, ALU.mult, ALU.add))
                        W(pool_step, s.now())
                        e.tensor_tensor(rstd[:, p:p + 1], veps[:, p:p + 1], mhalf[:], ALU.pow).then_inc(rstd_ready, 1)

            def low_parts(lo, a0, a1, hi, n0):
                for c in range(a0, a1, 1024):
                    n0 += 1
                    z = slice(c, min(c + 1024, a1))
                    e.wait_ge(whi_ready, n0)
                    e.tensor_tensor(lo[:, z], wreg[:, z], hi[:, z], ALU.subtract).then_inc(wlo_pool, 1)

            low_parts(wlo, 2 * KD * INTER, LUT_COLS, whi, NSPLIT_C)
            ln_pairs(base, 1, B // 2)
            base += B
            barrier(e, 3)
            if stop == "C":
                return
            def powers(s, out, k, src, sem_in, v, sem_out, eps):
                W(sem_in, v)
                s.up(e.tensor_scalar(k, src, 1.0, eps, ALU.mult, ALU.add))
                W(pool_step, s.now())
                e.tensor_tensor(out, k, mhalf[:].to_broadcast([P, out.shape[-1]]), ALU.pow).then_inc(sem_out, 1)

            def scatter_pair(i):
                for p in range(2):
                    W(slot_ready, i + 1)
                    for k in range(TOPK):
                        for dst, src in ((d_xg, xr[:, p, :]), (d_meta, meta[:, p, k, :])):
                            e.indirect_dma_start(dst, bass.IndirectOffsetOnAxis(ap=islot[:, p, k:k + 1], axis=0),
                                                 src, None, bounds_check=E * CAP - 1,
                                                 oob_is_err=False).then_inc(scattered, 16)
                W(scattered, 32 * 2 * TOPK * (i + 1))
                e.sem_inc(xr_free, 1)

            def powers_x(s, n):
                for p in range(2):
                    powers(s, rstd[:, p:p + 1], veps[:, p:p + 1], mv[:, p, 1:2], var_ready,
                           1 + B + 2 * n + p + 1, rstd_ready, EPS_LN)

            def powers_latents(s, n):
                for p in range(2):
                    powers(s, rr[:, p, :], rv2[:, p, :], ssd2[:, p, :], ms_ready,
                           2 + 2 * n + p + 1, rstd_ready, EPS_RMS)

            NP = B // 2

            def attn(j, ahead, route, scatter):
                if isinstance(j, int):
                    first = {0: 4, NP: 6 * NP - 2}.get(j, 6 * j + 2)
                else:
                    first = 6 * j + 2
                s = Steps(pool_step, base + first)
                if ahead:
                    powers_x(s, j + 1)
                if route:
                    for p in (2, 3):
                        powers(s, rstd[:, p:p + 1], veps[:, p:p + 1], mv[:, p, 1:2], var3_ready,
                               2 * (j - 1) + p - 1, rstd3_ready, EPS_LN)
                if scatter:
                    scatter_pair(j - 2)
                if ahead:
                    powers_latents(s, j + 1)

            s = Steps(pool_step, base)
            powers_x(s, 0)
            powers_latents(s, 0)
            attn(0, True, False, False)
            attn(1, True, True, False)
            with e.Fori(2, NP - 1) as j:
                attn(j, True, True, True)
            attn(NP - 1, False, True, True)
            attn(NP, False, True, True)
            if stop != "D":
                scatter_pair(NP - 1)
            base += 3 * B
            barrier(e, 4)
            if stop == "D":
                return
            low_parts(slo, SC_D, 3 * KD * SHF, shi, NSPLIT_C + NSPLIT_CD + NSPLIT_S)
            with e.Fori(0, 4) as g:
                s = Steps(pool_step, g * 4 + base)
                for q in range(4):
                    p = q % 2
                    W(var_ready, 1 + 2 * B + 1 + 4 * g + q)
                    s.up(e.tensor_scalar(veps[:, p:p + 1], mv[:, p, 1:2], 1.0, EPS_LN, ALU.mult, ALU.add))
                    W(pool_step, s.now())
                    e.tensor_tensor(rstd[:, p:p + 1], veps[:, p:p + 1], mhalf[:], ALU.pow).then_inc(rstd_ready, 1)
                for f in range(NSH):
                    W(ye_ready, NSH * g + f + 1)
                    e.indirect_dma_start(d_acc, bass.IndirectOffsetOnAxis(ap=xix[:, f % 2:f % 2 + 1], axis=0),
                                         yE[:, f % 2, :], None, compute_op=ALU.add).then_inc(acc_added, 16)
                    W(acc_added, 16 * (NSH * g + f + 1))
                    e.sem_inc(ye_free, 1)
            barrier(e, 5)

        @block.tensor
        def _(e):
            W = lambda s, v: wait(e, idle["pe"], s, v)

            def fill(ring, free, depth):
                n, b = ring.take()
                W(free, n - depth + 1 + CREDIT)
                return n, psum[:, b, :]

            def turn(dst, src, w=P):
                return e.transpose(dst, src, ident[0:w, 0:w])

            ra, rv = Ring(A_AB), Ring(V_AB)
            e.wait_ge(ld_a, 16 * NLD_A)
            e.wait_ge(x_ready, 1)
            n, ps = fill(ra, act_free, 4)
            for k in range(KD):
                t = turn(ps[:, k * P:(k + 1) * P], e1[:, k * P:(k + 1) * P])
            t.then_inc(act_full, 1)
            e.wait_ge(act_free, n + 1 + CREDIT)
            n, ps = fill(rv, dve_free, 4)
            for k in range(KD):
                t = e.matmul(ps, eT[:, k, :], projT[:, k, :], start=k == 0, stop=k == KD - 1)
            t.then_inc(dve_full, 1)
            e.wait_ge(x_ready, 2)
            n, ps = fill(ra, act_free, 4)
            for k in range(KD):
                t = turn(ps[:, k * P:(k + 1) * P], xtab[:, k * P:(k + 1) * P])
            t.then_inc(act_full, 1)
            e.wait_ge(act_free, n + 1 + CREDIT)
            n, ps = fill(rv, dve_free, 4)
            for k in range(KD):
                t = e.matmul(ps[:, 0:160], xtT[:, k, :], bcdtT[:, k, :], start=k == 0, stop=k == KD - 1)
            t.then_inc(dve_full, 1)
            barrier(e, 1)

            e.wait_ge(hot_ready, 1)
            def sums(ra, m, g):
                W(segr_ready, NG * m + g + 1)
                n, ps = fill(ra, act_free, 4)
                e.matmul(ps, cst[:, C_GT:C_GT + P], segr[:, g % 4, :, :].rearrange("p a b -> p (a b)"),
                         start=True, stop=True).then_inc(act_full, 1)

            def b_and_c(ra, m):
                col = at(e, m * P)
                n, ps = fill(ra, act_free, 4)
                for c in range(2):
                    t = e.matmul(ps[0:N0, c * P:(c + 1) * P], bc[:, N0 * c:N0 * c + N0], onehot[:, bass.ds(col, P)],
                                 start=True, stop=True)
                t.then_inc(act_full, 1)
                return n

            def b_by_c(rv, q, copied):
                W(act_free, copied + 1 + CREDIT)
                n, ps = fill(rv, dve_free, 2)
                e.matmul(ps[:, 0:P], bct[:, q, 0:P], bct[:, q, P:2 * P], start=True, stop=True).then_inc(dve_full, 1)

            def turn_y(ra, i, q):
                W(y_ready, i + 1)
                n, ps = fill(ra, act_free, 4)
                for k in range(KD):
                    t = turn(ps[:, k * P:(k + 1) * P], xD[:, q, k * P:(k + 1) * P])
                t.then_inc(act_full, 1)
                return n

            def project_y(rv, q, copied):
                W(act_free, copied + 1 + CREDIT)
                n, ps = fill(rv, dve_free, 2)
                for k in range(KD):
                    t = e.matmul(ps, yT[:, q, k, :], owT[:, k, :], start=k == 0, stop=k == KD - 1)
                t.then_inc(dve_full, 1)

            ra = Ring(A_AB, A_B)
            n = b_and_c(ra, 0)
            sums(ra, 0, 0)
            sums(ra, 0, 1)
            b_by_c(Ring([4, 5], V_B), 0, n)

            def step(j, odd, first, last):
                i = 2 * j + odd
                ra, rv = ssd_rings(i, odd)
                for g in range(NG):
                    if g + 2 < NG:
                        sums(ra, i, g + 2)
                    elif not last:
                        sums(ra, i + 1, g + 2 - NG)
                    if g == 1 and not first:
                        turned = turn_y(ra, i - 1, 1 - odd)
                    if g == 2 and not first:
                        project_y(rv, 1 - odd, turned)
                    if g == 3 and not last:
                        copied = b_and_c(ra, i + 1)
                    if g == 5 and not last:
                        b_by_c(rv, 1 - odd, copied)
                    if g == 0:
                        W(xd_ready, i + 1)
                    W(g_ready, NG * i + g + 1)
                    for h in range(HG):
                        c = (HG * g + h) * HP
                        t = e.matmul(psum[:, 6 + odd, c:c + HP], lg[:, g % 4, h, :], xdt[:, odd, c:c + HP],
                                     start=True, stop=True)
                    t.then_inc(y_done, 1)

            each_sequence(e, step)
            turned = turn_y(Ring(A_AB, A_B + B * A_BN - 1, 3), B - 1, 1)
            project_y(Ring([4, 5], V_B + B * V_BN - 1, 1), 1, turned)
            barrier(e, 2)
            if stop == "B":
                return

            def split_product(out, lhs, rhs, first, last):
                for n, (x, y) in enumerate(((0, 0), (0, 1), (1, 0))):
                    t = e.matmul(out, lhs[x], rhs[y], start=first and n == 0, stop=last and n == 2)
                return t

            def ffn(base_a, base_v, na, nv, nf, seen, w, cols, rows, groups_before, xh, experts):
                c_up, c_down, width = cols
                with e.Fori(0, 4) as g:
                    ra, rv = Ring([0, 1], base_a + g * na), Ring([2, 3], base_v + g * nv)
                    got = {}
                    for q in range(4):
                        W(x_ready, seen + g * 4 + q + 1)
                        n, ps = fill(rv, dve_free, 2)
                        for k in range(KD):
                            t = turn(ps[:, k * P:(k + 1) * P], xn[:, q % 2, k * P:(k + 1) * P])
                        t.then_inc(dve_full, 1)
                    W(dve_free, n + 1 + CREDIT)
                    for f in range(nf + 1):
                        if f < nf:
                            m = rows(f)
                            for ring, free, full, c0 in ((ra, act_free, act_full, 0), (rv, dve_free, dve_full, c_up)):
                                n, ps = fill(ring, free, 2)
                                for k in range(KD):
                                    c = c0 + k * width + f * P
                                    t = split_product(ps[0:m, :], [x[:, c:c + m] for x in w],
                                                      (xh[:, k, :], xlo[:, k, :]), k == 0, k == KD - 1)
                                t.then_inc(full, 1)
                        if experts and f < nf:
                            W(xe_ld[f % 2], 32 * (4 * g + f // 2 + 1))
                            got["T"], ps = fill(ra, act_free, 2)
                            for k in range(KD):
                                t = turn(ps[:, k * P:(k + 1) * P], xgE[:, f % 2, k * P:(k + 1) * P])
                            t.then_inc(act_full, 1)
                        if experts and f:
                            W(he_ready, nf * g + f)
                            n, ps = fill(rv, dve_free, 2)
                            for x in range(2):
                                r = slice(CAP * x, CAP * x + CAP)
                                t = e.matmul(ps[r, :], hE[:, (f - 1) % 2, r], wE[:, (f - 1) % 2, x, 2 * D:3 * D],
                                             start=True, stop=True)
                            t.then_inc(dve_full, 1)
                        if f:
                            m = rows(f - 1)
                            if f == 1:
                                W(down_free, (groups_before + g) * 4 + CREDIT)
                            W(hT_ready, groups_before * NF + g * nf + f)
                            c = c_down + (f - 1) * D
                            for q in range(4):
                                z = slice(q * P, (q + 1) * P)
                                t = split_product(psum[:, 4 + q, :], [h[0:m, (f - 1) % 2, z] for h in (hhi, hlo)],
                                                  [x[0:m, c:c + D] for x in w], f == 1, f == nf)
                            t.then_inc(hT_used, 1)
                        if experts and f < nf:
                            W(we_ld[f % 2], 16 * (4 * g + f // 2 + 1))
                            W(act_free, got["T"] + 1 + CREDIT)
                            for c, (ring, free, full) in enumerate(((ra, act_free, act_full), (rv, dve_free, dve_full))):
                                n, ps = fill(ring, free, 2)
                                for x in range(2):
                                    for k in range(KD):
                                        t = e.matmul(ps[:, CAP * x:CAP * x + CAP],
                                                     wE[:, f % 2, x, c * D + k * P:c * D + (k + 1) * P],
                                                     xgT[:, f % 2, k, CAP * x:CAP * x + CAP], start=k == 0, stop=k == KD - 1)
                                t.then_inc(full, 1)
                    e.drain().then_inc(down_full, 1)
                    if not experts:
                        ra.take(), rv.take()
                        e.drain().then_inc(act_full, 1)
                        e.drain().then_inc(dve_full, 1)
                    assert ra.k == na and rv.k == nv, (ra.k, rv.k)

            e.wait_ge(wlo_ready, NSPLIT_C)
            e.wait_ge(wlo_pool, NSPLIT_CD)
            ffn(A_C, V_C, A_CN, V_CN, NF, 2, (whi, wlo), (KD * INTER, 2 * KD * INTER, INTER), rows0, 0, xhi, False)
            barrier(e, 3)
            if stop == "C":
                return

            e.wait_ge(ld_d, 16 * 7)
            e.wait_ge(ld_r, 32)

            def turn_x(ra, n, got):
                for p in range(2):
                    W(x_ready, 2 + B + 2 * n + p + 1)
                    got["x", p], ps = fill(ra, act_free, 4)
                    for k in range(KD):
                        t = turn(ps[:, k * P:(k + 1) * P], xa[:, p, k * P:(k + 1) * P])
                    t.then_inc(act_full, 1)

            def latents(rv, got):
                for p in range(2):
                    W(act_free, got["x", p] + 1 + CREDIT)
                    n, ps = fill(rv, dve_free, 4)
                    for k in range(KD):
                        t = e.matmul(ps[:, 0:384], xT1[:, p, k, :], wq3[:, k, :], start=k == 0, stop=k == KD - 1)
                    t.then_inc(dve_full, 1)

            def turn_latents(ra, n):
                for p in range(2):
                    W(lat_ready, 2 * n + p + 1)
                    m, ps = fill(ra, act_free, 4)
                    turn(ps[:, 0:P], lat[:, p, 0:P])
                    turn(ps[0:QL - P, P:2 * P], lat[:, p, P:QL])
                    turn(ps[:, 2 * P:3 * P], lat[:, p, QL:QL + KVL]).then_inc(act_full, 1)

            def attn(j, route, last):
                ra, rv = attention_rings(j)
                got = {}
                for p in range(2):
                    if isinstance(j, int) and j == 0:
                        W(act_free, A_D + 2 + p + 1 + CREDIT)
                    elif p == 0:
                        W(act_free, ra.base + CREDIT)
                    for g in range(4):
                        n, ps = fill(rv, dve_free, 4)
                        e.matmul(ps[:, 0:384], qct[:, p, 0:P], wdq[:, 0, g * 384:(g + 1) * 384], start=True, stop=False)
                        e.matmul(ps[:, 0:384], qct[0:QL - P, p, P:2 * P], wdq[0:QL - P, 1, g * 384:(g + 1) * 384],
                                 start=False, stop=True).then_inc(dve_full, 1)
                    n, ps = fill(rv, dve_free, 4)
                    e.matmul(ps, qct[:, p, 2 * P:3 * P], wdkv[:, 0:D], start=True, stop=True).then_inc(dve_full, 1)
                    n, ps = fill(ra, act_free, 4)
                    e.matmul(ps, qct[:, p, 2 * P:3 * P], wdkv[:, D:2 * D], start=True, stop=True).then_inc(act_full, 1)
                for p in range(2):
                    for src, w in ((qa, 0), (ka, 1)):
                        for g in range(4):
                            if g == 0 or not w:
                                W(rope_ready, 5 * (2 * j + p) + (5 if w else g + 1))
                            n, ps = fill(ra, act_free, 4)
                            for h in range(4):
                                t = turn(ps[0:HQ, h * P:(h + 1) * P], src[:, p, 4 * g + h, :])
                            t.then_inc(act_full, 1)
                    got["kT", p] = n
                if route:
                    route_turn(rv, j - 1, got)
                ob_ps = {}
                for what, g in HEAD_STEPS:
                    if what in "XCL":
                        if not last:
                            if what == "X":
                                turn_x(ra, j + 1, got)
                            elif what == "C":
                                latents(rv, got)
                            else:
                                turn_latents(ra, j + 1)
                        continue
                    if route and (what, g) == ("T", 0):
                        route_logits(rv, got)
                    for p in range(2):
                        if what == "S":
                            if g == 0:
                                W(act_free, got["kT", p] + 1 + CREDIT)
                            got["S", p, g], ps = fill(ra, act_free, 4)
                            for h in range(4):
                                t = e.matmul(ps[:, h * P:(h + 1) * P], qT[:, p, 4 * g + h, :], kT[:, p, 4 * g + h, :],
                                             start=True, stop=True)
                            t.then_inc(act_full, 1)
                        elif what == "T":
                            W(act_free, got["S", p, g] + 1 + CREDIT)
                            got["T", p, g], ps = fill(ra, act_free, 4)
                            for h in range(4):
                                t = turn(ps[:, h * P:(h + 1) * P], pb[:, p, g % 2, h * P:(h + 1) * P])
                            t.then_inc(act_full, 1)
                        else:
                            W(act_free, got["T", p, g] + 1 + CREDIT)
                            if g == 0:
                                n, ob_ps[p] = fill(rv, dve_free, 4)
                            for h in range(4):
                                c = (4 * g + h) * HD
                                t = e.matmul(ob_ps[p][:, c:c + HD], pT[:, p, g % 2, h * P:(h + 1) * P],
                                             va[:, p, c:c + HD], start=True, stop=True)
                            if g == 3:
                                t.then_inc(dve_full, 1)
                if route:
                    route_places(rv, j - 1)
                for p in range(2):
                    W(o_ready, 2 * j + p + 1)
                    got["o", p], ps = fill(ra, act_free, 4)
                    for k in range(KD):
                        t = turn(ps[:, k * P:(k + 1) * P], ob[:, p, k * P:(k + 1) * P])
                    t.then_inc(act_full, 1)
                for p in range(2):
                    W(act_free, got["o", p] + 1 + CREDIT)
                    n, ps = fill(rv, dve_free, 4)
                    for k in range(KD):
                        t = e.matmul(ps, oT[:, p, k, :], wo[:, k, :], start=k == 0, stop=k == KD - 1)
                    t.then_inc(dve_full, 1)
                assert ra.k == 2 * A_DN - 4 * last, ra.k
                assert rv.k == 2 * V_DN - 2 * last + 2 * V_RN * route, rv.k

            def route_turn(rv, i, got):
                for p in range(2):
                    W(x3_ready, 2 * i + p + 1)
                    got["x3"], ps = fill(rv, dve_free, 4)
                    for k in range(KD):
                        t = turn(ps[:, k * P:(k + 1) * P], xr[:, p, k * P:(k + 1) * P])
                    t.then_inc(dve_full, 1)

            def route_logits(rv, got):
                W(dve_free, got["x3"] + 1 + CREDIT)
                n, ps = fill(rv, dve_free, 4)
                for p in range(2):
                    for k in range(KD):
                        t = e.matmul(ps[:, p * E:(p + 1) * E], x3T[:, p, k, :], rwT[:, k, :], start=k == 0, stop=k == KD - 1)
                t.then_inc(dve_full, 1)

            def route_places(rv, i):
                W(msk_ready, i + 1)
                n, ps = fill(rv, dve_free, 4)
                for p in range(2):
                    e.matmul(ps[:, p * E:(p + 1) * E], cst[:, C_STR:C_STR + P], msk[:, p, :], start=True, stop=False)
                    t = e.matmul(ps[:, p * E:(p + 1) * E], cst[:, C_ONE:C_ONE + P], cum[:, p, :], start=False, stop=True)
                t.then_inc(dve_full, 1)

            got = {}
            ra = Ring(A_AB, A_D)
            turn_x(ra, 0, got)
            latents(Ring(V_AB, V_D), got)
            turn_latents(ra, 0)
            attn(0, False, False)
            with e.Fori(1, B // 2 - 1) as j:
                attn(j, True, False)
            attn(B // 2 - 1, True, True)
            rv, got = attention_rings(B // 2)[1], {}
            route_turn(rv, B // 2 - 1, got)
            route_logits(rv, got)
            route_places(rv, B // 2 - 1)
            barrier(e, 4)
            if stop == "D":
                return

            e.wait_ge(wlo_ready, NSPLIT_C + NSPLIT_S)
            e.wait_ge(wlo_pool, NSPLIT_CD + NSPLIT_SD)
            ffn(A_S, V_S, A_SN, V_SN, NSH, 2 + 2 * B, (shi, slo), (SC_G, SC_D, SHF), lambda f: P, 4, xhiS, True)
            barrier(e, 5)

        @block.scalar
        def _(e):
            W = lambda s, v: wait(e, idle["act"], s, v)

            def drawn(ring):
                n, b = ring.take()
                W(act_full, n + 1)
                return psum[:, b, :]

            def give(ins):
                ins.then_inc(act_free, 1)

            def copy(dst, src):
                return e.activation(dst, src, ACT.Copy)

            e.sem_inc(act_free, CREDIT)
            e.wait_ge(ld_a, 16 * NLD_A)
            ra = Ring(A_AB)
            e.activation(junk[:], emb[:], ACT.Square, accum_out=ssq[:, 0:1]).then_inc(ms_ready, 1)
            give(copy(eT[:].rearrange("p a b -> p (a b)"), drawn(ra)))
            e.wait_ge(hraw_ready, 1)
            e.wait_ge(ms_ready, 1)
            e.activation(junk[:], hraw[:], ACT.Square, accum_out=ssq[:, 1:2]).then_inc(ms_ready, 1)
            give(copy(xtT[:].rearrange("p a b -> p (a b)"), drawn(ra)))
            e.wait_ge(dtin_ready, 1)
            e.activation(sp4[:, 1, :], sp4[:, 0, :], ACT.Exp).then_inc(act_step, 1)
            e.wait_ge(act_step, 1)
            e.activation(sp4[:, 2, :], sp4[:, 1, :], ACT.Ln, bias=1.0).then_inc(sp_ready, 1)
            e.activation(alog[:], alog[:], ACT.Exp).then_inc(sp_ready, 1)
            barrier(e, 1)

            def look(n, half, c, ts_, wait_stored):
                if ts_[0] == 0:
                    W(qm_ready, n + 1)
                    if wait_stored:
                        W(qw_stored[c], 16 * half)
                for t in ts_:
                    e.activation(qt[:, c, t, :], qm0[:, c, :], ACT.Identity, scale=lutd[:, t:t + 1],
                                 bias=lutb[:, 2 * t:2 * t + 1]).then_inc(qt_ready, 1)

            def decays(ra, g):
                give(e.activation(lg[:, g % 4, :, :].rearrange("p a b -> p (a b)"), drawn(ra), ACT.Exp))

            def copy_bc(ra, q):
                give(copy(bct[:, q, :], drawn(ra)[0:N0, 0:2 * P]))

            ra = Ring(A_AB, A_B)
            copy_bc(ra, 0)
            decays(ra, 0)
            decays(ra, 1)
            look(0, 0, 0, range(8), False)

            def step(j, odd, first, last):
                i = 2 * j + odd
                ra = ssd_rings(i, odd)[0]
                for g in range(NG):
                    if g + 2 < NG or not last:
                        decays(ra, (g + 2) % NG)
                    if g == 1 and not first:
                        give(copy(xdt[:, 1 - odd, :], drawn(ra)))
                    if g == 3 and not last:
                        copy_bc(ra, 1 - odd)
                    if g < 4:
                        look(2 * i + 1, i, 1, range(2 * g, 2 * g + 2), not first)
                    elif not last:
                        look(2 * i + 2, i + 1, 0, range(2 * g - 8, 2 * g - 6), True)

            each_sequence(e, step)
            give(copy(xdt[:, 1, :], drawn(Ring(A_AB, A_B + B * A_BN - 1, 3))))
            barrier(e, 2)
            if stop == "B":
                return

            def high_parts(hi, pieces):
                for z in pieces:
                    copy(hi[:, z], wreg[:, z]).then_inc(whi_ready, 1)

            def ffn(base_a, base_v, na, nv, nf, rows, groups_before, xh, experts):
                with e.Fori(0, 4) as g:
                    ra, rv = Ring([0, 1], base_a + g * na), Ring([2, 3], base_v + g * nv)
                    for q in range(4):
                        n, b = rv.take()
                        W(dve_full, n + 1)
                        copy(xh[:, :, q * P:(q + 1) * P], psum[:, b, :].rearrange("p (a b) -> p a b", a=KD)).then_inc(xhi_ready, 1)
                    for f in range(nf):
                        m = rows(f)
                        done = groups_before * NF + g * nf
                        ps = drawn(ra)
                        if f >= 2:
                            W(hT_ready, done + f - 1)
                        e.activation(sg[0:m, f % 2, :], ps[0:m, :], ACT.Silu).then_inc(act_free, 1)
                        if experts:
                            give(copy(xgT[:, f % 2, :, :].rearrange("p a b -> p (a b)"), drawn(ra)))
                        W(h_ready, done + f + 1)
                        if f >= 2:
                            W(hT_used, done + f - 1)
                        copy(hhi[0:m, f % 2, :], sg[0:m, f % 2, :]).then_inc(hi_ready, 1)
                        if experts:
                            e.activation(sgE[:, f % 2, :], drawn(ra)[:, 0:P], ACT.Silu).then_inc(act_free, 1)
                    if not experts:
                        ra.take()
                        e.drain().then_inc(act_free, 1)

            high_parts(whi, CUT_C)
            ffn(A_C, V_C, A_CN, V_CN, NF, rows0, 0, xhi, False)
            barrier(e, 3)
            if stop == "C":
                return

            SC = float(HQ) ** -0.5

            def copy_x(ra):
                for p in range(2):
                    give(copy(xT1[:, p, :, :].rearrange("p a b -> p (a b)"), drawn(ra)))

            def mean_squares(n):
                for p in range(2):
                    W(lat_in, 2 * n + p + 1)
                    e.activation(scratch[:, p, 0:QL], lat[:, p, 0:QL], ACT.Square, scale=float(QL) ** -0.5,
                                 accum_out=ssd2[:, p, 0:1])
                    e.activation(scratch[:, p, QL:QL + KVL], lat[:, p, QL:QL + KVL], ACT.Square, scale=float(KVL) ** -0.5,
                                 accum_out=ssd2[:, p, 1:2]).then_inc(ms_ready, 1)

            def copy_latents(ra):
                for p in range(2):
                    ps = drawn(ra)
                    copy(qct[:, p, 0:P], ps[:, 0:P])
                    copy(qct[0:QL - P, p, P:2 * P], ps[0:QL - P, P:2 * P])
                    give(copy(qct[:, p, 2 * P:3 * P], ps[:, 2 * P:3 * P]))

            def attn(j, route, last):
                ra = attention_rings(j)[0]
                for p in range(2):
                    give(copy(va[:, p, :], drawn(ra)))
                for p in range(2):
                    for dst in (qT, kT):
                        for g in range(4):
                            give(copy(dst[:, p, 4 * g:4 * g + 4, :].rearrange("p a b -> p (a b)"), drawn(ra)[0:HQ, :]))
                for what, g in HEAD_STEPS:
                    if what in "XL" and not last:
                        (copy_x if what == "X" else copy_latents)(ra)
                    if (what, g) == ("T", 2) and not last:
                        mean_squares(j + 1)
                    if what not in "ST":
                        continue
                    for p in range(2):
                        ps = drawn(ra)
                        if what == "S":
                            W(mx_ready, (2 * j) * 4 + 2 * g + p + 1)
                            for h in range(4):
                                hh = 4 * g + h
                                t = e.activation(pb[:, p, g % 2, h * P:(h + 1) * P], ps[:, h * P:(h + 1) * P], ACT.Exp,
                                                 bias=nmx[:, p, hh:hh + 1], scale=SC, accum_out=rs[:, p, hh:hh + 1])
                            give(t)
                        else:
                            give(copy(pT[:, p, g % 2, :], ps))
                if route:
                    route_exp(j - 1)
                for p in range(2):
                    give(copy(oT[:, p, :, :].rearrange("p a b -> p (a b)"), drawn(ra)))

            def route_exp(i):
                W(nlm_ready, i + 1)
                for p in range(2):
                    e.activation(ex[:, p, :], lgt[:, p, :], ACT.Exp, bias=nlm[:, p:p + 1]).then_inc(ex_ready, 1)

            ra = Ring(A_AB, A_D)
            copy_x(ra)
            mean_squares(0)
            copy_latents(ra)
            attn(0, False, False)
            with e.Fori(1, B // 2 - 1) as j:
                attn(j, True, False)
            attn(B // 2 - 1, True, True)
            route_exp(B // 2 - 1)
            barrier(e, 4)
            if stop == "D":
                return

            e.wait_ge(ld_c, 16)
            high_parts(shi, CUT_S[:NSPLIT_S])
            e.wait_ge(ld_c, 32)
            high_parts(shi, CUT_S[NSPLIT_S:])
            ffn(A_S, V_S, A_SN, V_SN, NSH, lambda f: P, 4, xhiS, True)
            barrier(e, 5)
            out_v = out.rearrange("b t d -> (b t) d")
            with e.Fori(0, B // 2) as j:
                for q in range(2):
                    row = e.snap((2 * j + q) * P)
                    W(ac_ready, 2 * j + q + 1)
                    e.dma_start(out_v[bass.ds(row, P), :], ac[:, q, :]).then_inc(ac_out, 16)
            e.wait_ge(ac_out, 16 * B + 1)

        @block.vector
        def _(e):
            W = lambda s, v: wait(e, idle["dve"], s, v)
            tt, ts, stt_ = e.tensor_tensor, e.tensor_scalar, e.scalar_tensor_tensor
            st = Steps(dve_step)

            def link(ins):
                v = st.up(ins)
                W(dve_step, v)

            def drawn(ring):
                n, b = ring.take()
                W(dve_full, n + 1)
                return psum[:, b, :]

            def give(ins):
                ins.then_inc(dve_free, 1)

            def spread(x, h, w):
                return x.unsqueeze(2).to_broadcast([x.shape[0], h, w])

            def stats(src, k):
                link(e.bn_stats(stat[:, k, 0:6], src))
                e.bn_aggr(mv[:, k, :], stat[:, k, 0:6]).then_inc(var_ready, 1)

            e.sem_inc(dve_free, CREDIT)
            e.sem_inc(down_free, CREDIT)
            for s in (ac_out, xr_free):
                e.sem_inc(s, 1)
            e.wait_ge(ld_a, 16 * NLD_A)
            rv = Ring(V_AB)
            e.wait_ge(rstd_ready, 1)
            stt_(e1[:], emb[:], rstd[:, 0:1], nw[:], ALU.mult, ALU.mult).then_inc(x_ready, 1)
            tt(lutd[:], lutb[:].rearrange("p (a b) -> p a b", b=2)[:, :, 1], lutb[:].rearrange("p (a b) -> p a b", b=2)[:, :, 0],
               ALU.subtract)
            ts(onehot[:], xtok[:], cst[:, C_P:C_P + 1], None, ALU.is_equal).then_inc(hot_ready, 1)
            ps = drawn(rv)
            t = e.tensor_copy(hraw[:], ps)
            t.then_inc(hraw_ready, 1)
            e.wait_ge(hraw_ready, 1)
            e.sem_inc(dve_free, 1)
            e.wait_ge(rstd_ready, 2)
            link(ts(htab[:], hraw[:], rstd[:, 1:2], None, ALU.mult))
            tt(htabb[:], htab[:], outb[:], ALU.add).then_inc(tab_ready, 1)
            stats(htab[:], 0)
            e.wait_ge(var_ready, 1)
            e.wait_ge(rstd_ready, 3)
            t = ts(xtab[:], htab[:], mv[:, 0, 0:1], rstd[:, 2:3], ALU.subtract, ALU.mult)
            t.then_inc(x_ready, 1)
            e.wait_ge(x_ready, 2)
            ps = drawn(rv)
            link(tt(bc[:], ps[:, 0:160], bcb[:], ALU.add))
            e.sem_inc(dve_free, 1)
            link(ts(sp4[:, 3, :], bc[:, 128:160], -1.0, None, ALU.mult))
            tt(sp4[:, 0, :], sp4[:, 3, :], bc[:, 128:160], ALU.min).then_inc(dtin_ready, 1)
            e.wait_ge(sp_ready, 2)
            link(stt_(stab[:, 0:H0], bc[:, 128:160], 0.0, sp4[:, 2, :], ALU.max, ALU.add))
            link(stt_(stab[:, H0:2 * H0], stab[:, 0:H0], -1.0, alog[:], ALU.mult, ALU.mult))
            e.drain().then_inc(tab_ready, 2)
            barrier(e, 1)
            base = st.now()
            stc = [st]

            def link(ins):
                v = stc[0].up(ins)
                W(dve_step, v)

            def low_bit(n, half, c):
                W(qi_ld[c], 16 * half + 16)
                ts(qm0[:, c, :], qi[:, c, :], 1, None, ALU.bitwise_and).then_inc(qm_ready, 1)

            def high_bits(c):
                for b in (3, 2, 1):
                    t = ts(qm[:, b - 1, :], qi[:, c, :], 1 << b, None, ALU.bitwise_and)
                link(t)
                e.sem_inc(qi_used, 1)

            def pick(n, c, part):
                if part == 0:
                    W(qt_ready, 8 * n + 8)
                for lv, w, ts_ in (((1, 1, (0, 2)),), ((1, 1, (4, 6)),), ((2, 2, (0, 4)), (3, 4, (0,))))[part]:
                    for t in ts_:
                        x = e.copy_predicated(qt[:, c, t, :], qm[:, lv - 1, :], qt[:, c, t + w, :])
                    if part:
                        link(x)
                if part == 2:
                    e.sem_inc(qw_ready, 1)

            def mask_bc(rv, q):
                link(tt(mm[:, q, :], drawn(rv)[:, 0:P], cst[:, C_TRI:C_TRI + P], ALU.mult))
                e.sem_inc(dve_free, 1)

            def add_y(i, q):
                W(y_done, NG * (i + 1))
                tt(xD[:, q, :], xD[:, q, :], psum[:, 6 + q, :], ALU.add).then_inc(y_ready, 1)

            def add_h(rv, i, half, q):
                ii = at(e, i)
                ps = drawn(rv)
                W(hg_ld[q], 16 * half + 16)
                link(tt(hres[:, bass.ds(ii, 1), :].rearrange("p a d -> p (a d)"), ps, hg[:, q, :], ALU.add))
                e.sem_inc(dve_free, 1)
                e.sem_inc(xh_used, 1)

            stc[0] = Steps(dve_step, base)
            low_bit(0, 0, 0)
            high_bits(0)
            mask_bc(Ring([4, 5], V_B), 0)

            def step(j, odd, first, last):
                i = 2 * j + odd
                stc[0] = Steps(dve_step, base + (2 if first else SSD_LINKS * i + 1))
                ra, rv = ssd_rings(i, odd)
                place = {0: -2, 1: -1}
                for g in range(2, NG):
                    place[g] = g - 2 + (g > 3 and not first) + (g > 5 and not last)
                for g in range(NG):
                    W(act_free, ra.base + place[g] + 1 + CREDIT)
                    tt(lg[:, g % 4, :, :], lg[:, g % 4, :, :], mm[:, odd, :].unsqueeze(1).to_broadcast([P, HG, P]),
                       ALU.mult).then_inc(g_ready, 1)
                    if g == 0:
                        if not first:
                            add_y(i - 1, 1 - odd)
                        low_bit(2 * i + 1, i, 1)
                    if g in (1, 2, 3):
                        pick(2 * i, 0, g - 1)
                    if g == 4:
                        if not first:
                            add_h(rv, i - 1, j + odd - 1, 1 - odd)
                        high_bits(1)
                        if not last:
                            low_bit(2 * i + 2, i + 1, 0)
                    if g in (5, 6, 7):
                        pick(2 * i + 1, 1, g - 5)
                    if g == 6 and not last:
                        mask_bc(rv, 1 - odd)
                    if g == 7 and not last:
                        high_bits(0)
                assert stc[0].k == SSD_LINKS - first - 2 * last, stc[0].k

            each_sequence(e, step)
            stc[0] = Steps(dve_step, base + B * SSD_LINKS - 1)
            add_y(B - 1, 1)
            add_h(Ring([4, 5], V_B + B * V_BN - 1, 1), B - 1, B // 2 - 1, 1)
            base += B * SSD_LINKS
            barrier(e, 2)
            if stop == "B":
                return

            def low_parts(lo, hi, pieces, n0):
                for n, z in enumerate(pieces):
                    e.wait_ge(whi_ready, n0 + n + 1)
                    tt(lo[:, z], wreg[:, z], hi[:, z], ALU.subtract).then_inc(wlo_ready, 1)

            def ffn(base, base_v, nv, nf, seen_x, seen_r, rows, groups_before, base_a, na, xh, experts, links):
                with e.Fori(0, 4) as g:
                    stc[0] = Steps(dve_step, base + g * links)
                    rv = Ring([2, 3], base_v + g * nv)
                    for q in range(4):
                        ii = e.snap(g * 4 + q)
                        hrow = hres[:, bass.ds(ii, 1), :].rearrange("p a d -> p (a d)")
                        link(e.bn_stats(stat[:, q % 2, 0:6], hrow))
                        e.bn_aggr(mv[:, q % 2, :], stat[:, q % 2, 0:6]).then_inc(var_ready, 1)
                        W(rstd_ready, seen_r + g * 4 + q + 1)
                        W(var_ready, seen_x - 1 + g * 4 + q + 1)
                        if q >= 2:
                            W(dve_full, base_v + g * nv + q - 1)
                        ts(xn[:, q % 2, :], hrow, mv[:, q % 2, 0:1], rstd[:, q % 2:q % 2 + 1],
                           ALU.subtract, ALU.mult).then_inc(x_ready, 1)
                        if q:
                            lower_x(rv, g, q - 1, groups_before, xh)
                    lower_x(rv, g, 3, groups_before, xh)

                    def results(f):
                        n = nf * g + f
                        ps = drawn(rv)
                        W(ye_free, n + 1)
                        ts(xix[:, f % 2:f % 2 + 1], xm[:, f % 2, 1:2], cst[:, C_ODD:C_ODD + 1], None, ALU.add)
                        link(ts(yE[:, f % 2, :], ps, xm[:, f % 2, 0:1], None, ALU.mult))
                        e.sem_inc(dve_free, 1)
                        e.sem_inc(ye_ready, 1)
                        e.sem_inc(we_used, 1)

                    for f in range(nf):
                        m = rows(f)
                        done = groups_before * NF + g * nf
                        ps = drawn(rv)
                        W(act_free, base_a + g * na + (3 * f if experts else f) + 1 + CREDIT)
                        tt(sg[0:m, f % 2, :], sg[0:m, f % 2, :], ps[0:m, :], ALU.mult).then_inc(h_ready, 1)
                        W(h_ready, done + f + 1)
                        e.sem_inc(dve_free, 1)
                        if experts and f:
                            results(f - 1)
                        W(hi_ready, done + f + 1)
                        tt(hlo[0:m, f % 2, :], sg[0:m, f % 2, :], hhi[0:m, f % 2, :], ALU.subtract).then_inc(hT_ready, 1)
                        if experts:
                            ps = drawn(rv)
                            W(act_free, base_a + g * na + 3 * f + 2 + 1 + CREDIT)
                            link(tt(hE[:, f % 2, :], sgE[:, f % 2, :], ps[:, 0:P], ALU.mult))
                            e.sem_inc(dve_free, 1)
                            e.sem_inc(he_ready, 1)
                    if experts:
                        results(nf - 1)
                    else:
                        rv.take()
                        e.drain().then_inc(dve_free, 1)
                    W(down_full, groups_before + g + 1)
                    for q in range(4):
                        ii = e.snap(g * 4 + q)
                        hrow = hres[:, bass.ds(ii, 1), :].rearrange("p a d -> p (a d)")
                        link(tt(hrow, psum[:, 4 + q, :], hrow, ALU.add))
                        e.sem_inc(down_free, 1)
                    assert stc[0].k == links, stc[0].k
                    assert rv.k == nv

            def lower_x(rv, g, q, groups_before, xh):
                ps = drawn(rv)
                W(xhi_ready, (groups_before + g) * 4 + q + 1)
                give(tt(xlo[:, :, q * P:(q + 1) * P], ps.rearrange("p (a b) -> p a b", a=KD),
                        xh[:, :, q * P:(q + 1) * P], ALU.subtract))

            low_parts(wlo, whi, CUT_C[:NSPLIT_C], 0)
            ffn(base, V_C, V_CN, NF, 2, 3, rows0, 0, A_C, A_CN, xhi, False, FFN_LINKS)
            base += 4 * FFN_LINKS
            barrier(e, 3)
            if stop == "C":
                return
            e.wait_ge(ld_d, 16 * 7)
            e.wait_ge(ld_r, 32)
            stc[0] = Steps(dve_step, base)
            link(e.memset(cum[:, 0, :], 0.0))
            base += 1
            iota = cst[:, C_IOTA:C_IOTA + E]
            cos = cst[:, C_COS:C_COS + RD]
            sin = cst[:, C_SIN:C_SIN + RD]
            HR = RD // 2

            RB = 3 + B

            def norm_stats(n):
                for p in range(2):
                    ii = at(e, 2 * n + p)
                    hrow = hres[:, bass.ds(ii, 1), :].rearrange("p a d -> p (a d)")
                    link(e.bn_stats(stat[:, p, 0:6], hrow))
                    e.bn_aggr(mv[:, p, :], stat[:, p, 0:6]).then_inc(var_ready, 1)

            def norm_x(n):
                for p in range(2):
                    ii = at(e, 2 * n + p)
                    hrow = hres[:, bass.ds(ii, 1), :].rearrange("p a d -> p (a d)")
                    W(rstd_ready, RB + 4 * n + p + 1)
                    W(var_ready, 1 + B + 2 * n + p + 1)
                    ts(xa[:, p, :], hrow, mv[:, p, 0:1], rstd[:, p:p + 1], ALU.subtract, ALU.mult).then_inc(x_ready, 1)

            def latents(rv):
                for p in range(2):
                    ps = drawn(rv)
                    link(e.tensor_copy(lat[:, p, :], ps[:, 0:384]))
                    e.sem_inc(lat_in, 1)
                    e.sem_inc(dve_free, 1)
                for p in range(2):
                    tt(rt1[:, p, :], lat[:, p, 320:384], cos, ALU.mult)
                    tt(rt2[:, p, 0:HR], lat[:, p, 320 + HR:384], sin[:, 0:HR], ALU.mult)
                    t = tt(rt2[:, p, HR:RD], lat[:, p, 320:320 + HR], sin[:, HR:RD], ALU.mult)
                link(t)
                link(tt(rt1[:, 0:2, :], rt1[:, 0:2, :], rt2[:, 0:2, :], ALU.add))
                for p in range(2):
                    t = e.tensor_copy(ka[:, p, :, HD:HQ], rt1[:, p, :].unsqueeze(1).to_broadcast([P, H1, RD]))
                link(t)

            def norm_latents(n):
                for p in range(2):
                    W(rstd_ready, RB + 4 * n + 2 + p + 1)
                    stt_(lat[:, p, 0:QL], lat[:, p, 0:QL], rr[:, p, 0:1], gqb[:], ALU.mult, ALU.mult)
                    stt_(lat[:, p, QL:QL + KVL], lat[:, p, QL:QL + KVL], rr[:, p, 1:2], gkb[:],
                         ALU.mult, ALU.mult).then_inc(lat_ready, 1)

            def attn(j, route, last):
                first = isinstance(j, int) and j == 0
                stc[0] = Steps(dve_step, base + (D_AHEAD if first else D_AHEAD + D_PERIOD + (j - 1) * (D_PERIOD + R_PERIOD)))
                ra, rv = attention_rings(j)
                i = j - 1
                if not last:
                    norm_stats(j + 1)
                if route:
                    route_stats(i)
                for p in range(2):
                    for g in range(4):
                        ps = drawn(rv)[:, 0:384].rearrange("p (h w) -> p h w", w=HQ)
                        e.tensor_copy(qa[:, p, 4 * g:4 * g + 4, 0:HD], ps[:, :, 0:HD])
                        tt(rt1[:], ps[:, :, HD:HQ], cos.unsqueeze(1).to_broadcast([P, 4, RD]), ALU.mult)
                        tt(rt2[:, :, 0:HR], ps[:, :, HD + HR:HQ], sin[:, 0:HR].unsqueeze(1).to_broadcast([P, 4, HR]), ALU.mult)
                        link(tt(rt2[:, :, HR:RD], ps[:, :, HD:HD + HR], sin[:, HR:RD].unsqueeze(1).to_broadcast([P, 4, HR]), ALU.mult))
                        e.sem_inc(dve_free, 1)
                        link(tt(qa[:, p, 4 * g:4 * g + 4, HD:HQ], rt1[:], rt2[:], ALU.add))
                        e.sem_inc(rope_ready, 1)
                    ps = drawn(rv)
                    link(e.tensor_copy(ka[:, p, :, 0:HD], ps.rearrange("p (h w) -> p h w", w=HD)))
                    e.sem_inc(dve_free, 1)
                    e.sem_inc(rope_ready, 1)
                if not last:
                    W(act_full, ra.base + 2)
                    norm_x(j + 1)
                if route:
                    route_x(i)
                s_at = score_places(last)
                for g in range(4):
                    for p in range(2):
                        k = s_at[g] + p
                        W(act_full, ra.base + k + 1)
                        ps = psum[:, A_AB[k % 4], :]
                        link(e.tensor_reduce(mx[:, p, 4 * g:4 * g + 4], ps.rearrange("p (h w) -> p h w", w=P), AX.X, ALU.max))
                        ts(nmx[:, p, 4 * g:4 * g + 4], mx[:, p, 4 * g:4 * g + 4], -float(HQ) ** -0.5, None, ALU.mult).then_inc(mx_ready, 1)
                    if route:
                        if g == 0:
                            route_turned(rv)
                        else:
                            route_choose(rv, g - 1)
                    if g == 1 and not last:
                        latents(rv)
                    if g == 3 and not last:
                        norm_latents(j + 1)
                for p in range(2):
                    W(act_free, ra.base + s_at[3] + p + 1 + CREDIT)
                    link(e.reciprocal(ri[:, p, :], rs[:, p, :]))
                    ps = drawn(rv)
                    link(tt(ob[:, p, :].rearrange("p (h w) -> p h w", w=HD), ps.rearrange("p (h w) -> p h w", w=HD),
                            spread(ri[:, p, :], H1, HD), ALU.mult))
                    e.sem_inc(dve_free, 1)
                    e.sem_inc(o_ready, 1)
                if route:
                    route_slots(rv, i)
                for p in range(2):
                    ii = at(e, 2 * j + p)
                    hrow = hres[:, bass.ds(ii, 1), :].rearrange("p a d -> p (a d)")
                    ps = drawn(rv)
                    link(tt(hrow, ps, hrow, ALU.add))
                    e.sem_inc(dve_free, 1)
                assert stc[0].k == D_PERIOD + (R_PERIOD if route else 0) - (D_AHEAD if last else 0), (stc[0].k, route)

            def route_stats(i):
                for p in range(2):
                    ii = at(e, 2 * i + p)
                    hrow = hres[:, bass.ds(ii, 1), :].rearrange("p a d -> p (a d)")
                    link(e.bn_stats(stat[:, 2 + p, 0:6], hrow))
                    e.bn_aggr(mv[:, 2 + p, :], stat[:, 2 + p, 0:6]).then_inc(var3_ready, 1)

            def route_x(i):
                W(xr_free, i + 1)
                for p in range(2):
                    ii = at(e, 2 * i + p)
                    hrow = hres[:, bass.ds(ii, 1), :].rearrange("p a d -> p (a d)")
                    W(rstd3_ready, 2 * i + p + 1)
                    W(var3_ready, 2 * i + p + 1)
                    ts(xr[:, p, :], hrow, mv[:, 2 + p, 0:1], rstd[:, 2 + p:3 + p], ALU.subtract, ALU.mult).then_inc(x3_ready, 1)

            def route_turned(rv):
                for p in range(2):
                    ps = drawn(rv)
                    give(e.tensor_copy(x3T[:, p, :, :].rearrange("p a b -> p (a b)"), ps))

            def route_choose(rv, part):
                if part == 0:
                    ps = drawn(rv)[:, 0:2 * E].rearrange("p (s e) -> p s e", s=2)
                    e.tensor_copy(lgt[:], ps)
                    link(tt(bia[:], ps, rb[:].unsqueeze(1).to_broadcast([P, 2, E]), ALU.add))
                    e.sem_inc(dve_free, 1)
                    link(e.tensor_reduce(nlm[:], lgt[:], AX.X, ALU.max, negate=True))
                    e.sem_inc(nlm_ready, 1)
                    e.max(top[:, 0, :], bia[:, 0, :])
                    link(e.max(top[:, 1, :], bia[:, 1, :]))
                elif part == 1:
                    e.max_index(topi[:, 0, :], top[:, 0, :], bia[:, 0, :])
                    link(e.max_index(topi[:, 1, :], top[:, 1, :], bia[:, 1, :]))
                    link(e.tensor_copy(topf[:], topi[:, :, 0:TOPK]))
                    for p in range(2):
                        t = tt(hot[:, p, :, :], iota.unsqueeze(1).to_broadcast([P, TOPK, E]), spread(topf[:, p, :], TOPK, E), ALU.is_equal)
                    link(t)
                else:
                    for p in range(2):
                        t = e.tensor_reduce(msk[:, p, :], hot[:, p, :, :].rearrange("p k e -> p e k"), AX.X, ALU.add)
                    link(t)
                    link(tt(cum[:, 1, :], cum[:, 0, :], msk[:, 0, :], ALU.add))
                    e.sem_inc(msk_ready, 1)
                    link(tt(cum[:, 2, :], cum[:, 1, :], msk[:, 1, :], ALU.add))

            def route_slots(rv, i):
                ti = at(e, 2 * i + C_TOK)
                W(ex_ready, 2 * i + 2)
                for p in range(2):
                    t = tt(hw[:, p, :, :], hot[:, p, :, :], ex[:, p, :].unsqueeze(1).to_broadcast([P, TOPK, E]), ALU.mult)
                ps = drawn(rv)
                for p in range(2):
                    t = tt(hp[:, p, :, :], hot[:, p, :, :], ps[:, p * E:(p + 1) * E].unsqueeze(1).to_broadcast([P, TOPK, E]), ALU.mult)
                link(t)
                e.sem_inc(dve_free, 1)
                e.tensor_copy(cum[:, 0, :], cum[:, 2, :])
                e.tensor_reduce(tk[:, 0, :, :], hw[:], AX.X, ALU.add)
                link(e.tensor_reduce(tk[:, 1, :, :], hp[:], AX.X, ALU.add))
                e.tensor_reduce(tsum[:, :, 0], tk[:, 0, :, :], AX.X, ALU.add)
                ts(tk[:, 2, :, :], tk[:, 1, :, :], float(CAP), None, ALU.is_lt)
                link(stt_(tk[:, 3, :, :], topf[:], float(CAP), tk[:, 1, :, :], ALU.mult, ALU.add))
                e.reciprocal(tsum[:, :, 1], tsum[:, :, 0])
                tt(tk[:, 4, :, :], tk[:, 3, :, :], tk[:, 2, :, :], ALU.mult)
                link(ts(tk[:, 5, :, :], tk[:, 2, :, :], -2.0 * E * CAP, 2.0 * E * CAP, ALU.mult, ALU.add))
                tt(meta[:, :, :, 0], tk[:, 0, :, :], spread(tsum[:, :, 1], 2, TOPK), ALU.mult)
                e.tensor_copy(meta[:, :, :, 1], spread(cst[:, bass.ds(ti, 2)], 2, TOPK))
                link(tt(islot[:], tk[:, 4, :, :], tk[:, 5, :, :], ALU.add))
                e.sem_inc(slot_ready, 1)

            stc[0] = Steps(dve_step, base)
            norm_stats(0)
            norm_x(0)
            latents(Ring(V_AB, V_D))
            norm_latents(0)
            assert stc[0].k == D_AHEAD, stc[0].k
            attn(0, False, False)
            with e.Fori(1, B // 2 - 1) as j:
                attn(j, True, False)
            attn(B // 2 - 1, True, True)
            base += B // 2 * (D_PERIOD + R_PERIOD) - R_PERIOD
            stc[0] = Steps(dve_step, base)
            i, rv = B // 2 - 1, attention_rings(B // 2)[1]
            route_stats(i)
            route_x(i)
            route_turned(rv)
            for part in range(3):
                route_choose(rv, part)
            route_slots(rv, i)
            assert stc[0].k == R_PERIOD, stc[0].k
            base += R_PERIOD
            barrier(e, 4)
            if stop == "D":
                return

            low_parts(slo, shi, CUT_S[:NSPLIT_S], NSPLIT_C + NSPLIT_CD)
            e.sem_inc(ye_free, 2)
            ffn(base, V_S, V_SN, NSH, 2 + 2 * B, 3 + 3 * B, lambda f: P, 4, A_S, A_SN, xhiS, True, FFN_LINKS + 2 * NSH)
            base += 4 * (FFN_LINKS + 2 * NSH)
            e.sem_inc(ya_used, 2)
            barrier(e, 5)
            with e.Fori(0, B // 2) as j:
                stc[0] = Steps(dve_step, base + j * 2)
                for p in range(2):
                    ii = e.snap(2 * j + p)
                    W(ac_out, 32 * j + 1)
                    W(ya_ld[p], 32 * j + 32)
                    link(tt(ac[:, p, :], ya[:, p, 0, :], ya[:, p, 1, :], ALU.add))
                    tt(ac[:, p, :], ac[:, p, :], hres[:, bass.ds(ii, 1), :].rearrange("p a d -> p (a d)"), ALU.add).then_inc(ac_ready, 1)
                    W(ac_ready, 2 * j + p + 1)
                    e.sem_inc(ya_used, 1)


def rows0(f):
    return P if f < NF - 1 else INTER - (NF - 1) * P


def pieces(a0, a1, n):
    return [slice(c, min(c + n, a1)) for c in range(a0, a1, n)]


CUT_C = pieces(0, 2 * KD * INTER, INTER) + pieces(2 * KD * INTER, LUT_COLS, 1024)
CUT_S = pieces(0, 2 * KD * SHF, SHF) + pieces(2 * KD * SHF, 3 * KD * SHF, 1024)
NSPLIT_C = NSPLIT_S = 2 * KD
NSPLIT_CD, NSPLIT_SD = len(CUT_C) - NSPLIT_C, len(CUT_S) - NSPLIT_S
SSD_LINKS = 10
FFN_LINKS = 8
D_AHEAD = 7
D_PERIOD = 39
R_PERIOD = 16


def constants():
    import numpy as np
    c = np.zeros((P, C_N), np.float32)
    k, m = np.arange(P)[:, None], np.arange(P)[None, :]
    c[:, C_ID:C_ID + P] = k == m
    c[:, C_GT:C_GT + P] = k > m
    c[:, C_STR:C_STR + P] = k < m
    c[:, C_ONE:C_ONE + P] = 1.0
    c[:, C_TRI:C_TRI + P] = k <= m
    c[:, C_IOTA:C_IOTA + E] = m[:, :E]
    inv = np.float32(1.0) / np.float32(10000.0) ** (np.arange(0, RD, 2, dtype=np.float32) / np.float32(RD))
    ang = np.arange(P, dtype=np.float32)[:, None] * inv[None, :]
    c[:, C_COS:C_COS + RD] = np.concatenate([np.cos(ang)] * 2, 1)
    c[:, C_SIN:C_SIN + RD] = np.concatenate([-np.sin(ang), np.sin(ang)], 1)
    c[:, C_P] = np.arange(P)
    c[:, C_TOK:C_TOK + B] = np.arange(B)[None, :] * P + k
    c[:, C_ODD] = np.arange(P) // CAP * ACC
    c[:, C_META + 1::2] = B * P + k % CAP
    return c


def arrange(x):
    import numpy as np
    x = {k: np.asarray(v) for k, v in x.items()}

    def tiles(w):
        return np.ascontiguousarray(w.reshape(-1, P, w.shape[1]).transpose(1, 0, 2))

    o = {"consts": constants()}
    tok = x["x"]
    o["tokix"], o["xtok"] = np.ascontiguousarray(tok.T), tok.reshape(-1)
    o["emb"], o["nw"] = x["L0_tok_emb_table"], x["L0_tok_norm_weight"]
    o["projT"] = tiles(x["L0_tok_proj_weight"].T)
    o["bcdtT"] = tiles(np.concatenate([x["L0_attn_B_w"], x["L0_attn_C_w"], x["L0_attn_dt_w"]], 0).T)
    o["bcb"] = np.concatenate([x["L0_attn_B_b"], x["L0_attn_C_b"], x["L0_attn_dt_b"]])
    o["alog"], o["dskip"] = x["L0_attn_A_log"], x["L0_attn_D"]
    o["owT"], o["outb"] = tiles(x["L0_attn_out_w"].T), x["L0_attn_out_b"]
    o["lut"] = x["L0_ffn_lut"]
    down = np.zeros((NF * P, D), np.int32)
    down[:INTER] = x["L0_ffn_down_idx"].T
    o["lutidx"] = np.concatenate([tiles(w).reshape(P, -1) for w in
                                  (x["L0_ffn_gate_idx"].T, x["L0_ffn_up_idx"].T, down)], 1)
    o["wq3"] = tiles(np.concatenate([x["L1_attn_Wcq"], x["L1_attn_Wckv"], x["L1_attn_Wkr"]], 1))
    o["wdq"] = np.concatenate([x["L1_attn_Wdq"].reshape(QL, H1, HD), x["L1_attn_Wdqr"].reshape(QL, H1, RD)],
                              2).reshape(QL, H1 * HQ)
    o["wdkv"] = np.concatenate([x["L1_attn_Wdk"], x["L1_attn_Wdv"]], 1)
    o["wo"] = tiles(x["L1_attn_Wo"])
    o["gq"], o["gkv"] = x["L1_attn_g_q"], x["L1_attn_g_kv"]
    o["rwT"], o["rb"] = tiles(x["L1_ffn_router_w"].T), x["L1_ffn_router_bias"]
    sg, su, sd = x["L1_ffn_sh_gate_w"], x["L1_ffn_sh_up_w"], x["L1_ffn_sh_down_w"]
    o["shw"] = np.concatenate([tiles(w).reshape(P, -1) for w in
                               (sg.reshape(SHF, D).T, su.reshape(SHF, D).T, sd.transpose(0, 2, 1).reshape(SHF, D))], 1)

    def expert(w):
        return w.transpose(0, 2, 1).reshape(E, KD, P, F).transpose(0, 2, 1, 3).reshape(E, P, KD * F)

    o["wexp"] = np.concatenate([expert(x["L1_ffn_gate_w"]), expert(x["L1_ffn_up_w"]),
                                x["L1_ffn_down_w"].transpose(0, 2, 1)], 2).reshape(E * P, 3 * D)
    return {k: np.ascontiguousarray(v) for k, v in o.items()}


def kernel(**inputs):
    import concourse.bacc as bacc
    from concourse.bass_utils import run_bass_kernel_spmd

    arrays = arrange(inputs)
    nc = bacc.Bacc("TRN2", target_bir_lowering=False, num_devices=1)
    a = {k: nc.dram_tensor(f"in_{k}", v.shape, mybir.dt.from_np(v.dtype), kind="ExternalInput").ap()
         for k, v in arrays.items()}
    out = nc.dram_tensor("out_h", (B, P, D), F32, kind="ExternalOutput").ap()
    tower(nc, a, out)
    r = run_bass_kernel_spmd(nc, [{f"in_{k}": v for k, v in arrays.items()}], core_ids=[0])
    return r.results[0]["out_h"]
```

```python
from contextlib import ExitStack

import concourse.bass as bass
from concourse import mybir

F32 = mybir.dt.float32
F32R = mybir.dt.float32r
I32 = mybir.dt.int32
U32 = mybir.dt.uint32
ALU = mybir.AluOpType
ACT = mybir.ActivationFunctionType
AX = mybir.AxisListType

P = 128
B = 16
D = 512
KD = D // P
V = 128
H0, HP, N0 = 32, 16, 64
HG = 4
NG = H0 // HG
INTER = 1376
NF = 11
H1, HD, RD = 16, 32, 64
HQ = HD + RD
QL, KVL = 192, 128
E, TOPK, F, CAP = 64, 4, 128, 64
SHF = 1024
EPS_RMS, EPS_LN = 1e-6, 1e-5
CREDIT = 4
LUTN = 520
LUT_COLS = 2 * KD * INTER + NF * D
NCHUNK = LUT_COLS // LUTN
G4 = 4

C_ID, C_GT, C_TRI, C_STR, C_ONE, C_IOTA, C_COS, C_SIN, C_P = 0, 128, 256, 384, 512, 640, 704, 768, 832
C_TOK = C_P + 1
C_ODD = C_TOK + B
C_META = C_ODD + 1
C_N = C_META + 2 * E * CAP // P
ACC = B * P + CAP


class Steps:

    def __init__(self, sem, base=0):
        self.sem, self.base, self.k = sem, base, 0

    def up(self, ins):
        ins.then_inc(self.sem, 1)
        self.k += 1
        return self.base + self.k

    def now(self):
        return self.base + self.k


class Ring:

    def __init__(self, banks, base=0, shift=0):
        self.banks, self.base, self.shift, self.k = banks, base, shift, 0

    def take(self):
        n, bank = self.base + self.k, self.banks[(self.k + self.shift) % len(self.banks)]
        self.k += 1
        return n, bank


def at(e, x):
    return x if isinstance(x, int) else e.snap(x)


def wait(e, idle, sem, value):
    e.wait_ge(sem, value)
    if not isinstance(value, int):
        e.sem_inc(idle, 1)


def tower(nc, a, out, stop=None):
    with ExitStack() as ctx:
        def sem(name):
            return ctx.enter_context(nc.semaphore(name))

        def sbuf(scope, name, shape, dt=F32):
            return scope.enter_context(nc.sbuf_tensor(name, shape, dt))

        hres = sbuf(ctx, "hres", [P, B, D])
        cst = sbuf(ctx, "cst", [P, C_N])
        stat = sbuf(ctx, "stat", [P, 4, 8])
        mv = sbuf(ctx, "mv", [P, 4, 2])
        rstd = sbuf(ctx, "rstd", [P, 4])
        veps = sbuf(ctx, "veps", [P, 4])
        mhalf = sbuf(ctx, "mhalf", [P, 1])
        ident = cst[:, C_ID:C_ID + P]
        psum = ctx.enter_context(nc.psum_tensor("psum", [P, 8, 512], F32))

        sw = ExitStack()
        wreg = sbuf(sw, "wreg", [P, LUT_COLS])
        sw.close()
        sw = ExitStack()
        wlo = sbuf(sw, "wlo", [P, LUT_COLS], F32R)
        sw.close()
        sw = ExitStack()
        slo = sbuf(sw, "slo", [P, 3 * SHF * KD], F32R)
        xhiS = sbuf(sw, "xhiS", [P, KD, G4 * P], F32R)
        xgT = sbuf(sw, "xgT", [P, 2, KD, P])
        yE = sbuf(sw, "yE", [P, 2, D])
        sw.close()
        sw = ctx.enter_context(ExitStack())
        sbuf(sw, "w_region", [P, LUT_COLS])

        s1 = ctx.enter_context(ExitStack())
        zrow = sbuf(s1, "zrow", [P, D])
        onehot = sbuf(s1, "onehot", [P, B * P])
        owT = sbuf(s1, "owT", [P, KD, D])
        small = sbuf(s1, "small", [P, B, 2 * H0])
        bc = sbuf(s1, "bc", [P, 160])
        tokix = sbuf(s1, "tokix", [P, B], I32)
        dskip = sbuf(s1, "dskip", [P, H0])
        lutb = sbuf(s1, "lutb", [P, 16])
        lutd = sbuf(s1, "lutd", [P, 8])
        qi = sbuf(s1, "qi", [P, 2, LUTN], I32)
        qm = sbuf(s1, "qm", [P, 3, LUTN], I32)
        qm0 = sbuf(s1, "qm0", [P, 2, LUTN], I32)
        qt = sbuf(s1, "qt", [P, 2, 8, LUTN])
        sa = ExitStack()
        xtok = sbuf(sa, "xtok", [P, B * P], I32)
        projT = wreg[:, 0:KD * D].rearrange("p (k n) -> p k n", k=KD)
        emb = sbuf(sa, "emb", [P, D])
        nw = sbuf(sa, "nw", [P, D])
        outb = sbuf(sa, "outb", [P, D])
        junk = sbuf(sa, "junk", [P, D])
        e1 = sbuf(sa, "e1", [P, D])
        hraw = sbuf(sa, "hraw", [P, D])
        htab = sbuf(sa, "htab", [P, D])
        xtab = sbuf(sa, "xtab", [P, D])
        htabb = sbuf(sa, "htabb", [P, D])
        eT = sbuf(sa, "eT", [P, KD, V])
        xtT = sbuf(sa, "xtT", [P, KD, V])
        bcdtT = sbuf(sa, "bcdtT", [P, KD, 160])
        bcb = sbuf(sa, "bcb", [P, 160])
        alog = sbuf(sa, "alog", [P, H0])
        sp4 = sbuf(sa, "sp4", [P, 4, H0])
        stab = sbuf(sa, "stab", [P, 2 * H0])
        ssq = sbuf(sa, "ssq", [P, 2])
        sa.close()
        xg = sbuf(s1, "xg", [P, 2, D])
        hg = sbuf(s1, "hg", [P, 2, D])
        ixb = sbuf(s1, "ixb", [P, 2, 2], I32)
        segr = sbuf(s1, "segr", [P, 4, HG, P])
        lg = sbuf(s1, "lg", [P, 4, HG, P])
        mm = sbuf(s1, "mm", [P, 2, P])
        bct = sbuf(s1, "bct", [N0, 2, 2 * P])
        xdt = sbuf(s1, "xdt", [P, 2, D])
        xD = sbuf(s1, "xD", [P, 2, D])
        yT = xdt[:].rearrange("p s (a b) -> p s a b", a=KD)
        s1.close()

        sf = ExitStack()
        sx = ExitStack()
        wE = sbuf(sx, "wE", [P, 2, 2, 3 * D])
        ya = wE[:].rearrange("p q x n -> p (q x n)")[:, 0:4 * 2 * D].rearrange("p (s o d) -> p s o d", s=4, o=2)
        xgE = sbuf(sx, "xgE", [P, 2, D])
        shi = sbuf(sx, "shi", [P, 3 * SHF * KD], F32R)
        xm = sbuf(sx, "xm", [P, 2, 2])
        xix = sbuf(sx, "xix", [P, 2], I32)
        sgE = sbuf(sx, "sgE", [P, 2, P])
        hE = sbuf(sx, "hE", [P, 2, P])
        sx.close()
        sx = ExitStack()
        xhi = sbuf(sx, "xhi", [P, KD, G4 * P], F32R)
        whi = sbuf(sx, "whi", [P, LUT_COLS], F32R)
        sx.close()
        sbuf(sf, "ffn_weights", [P, max(2 * 2 * 3 * D + 2 * D + 3 * SHF * KD + 4 * P + 64, KD * G4 * P + LUT_COLS)])
        xn = sbuf(sf, "xn", [P, G4, D])
        sg = sbuf(sf, "sg", [P, 2, D])
        hhi = sbuf(sf, "hhi", [P, 2, D], F32R)
        hlo = sbuf(sf, "hlo", [P, 2, D], F32R)
        xlo = sbuf(sf, "xlo", [P, KD, G4 * P], F32R)
        sf.close()

        s2 = ctx.enter_context(ExitStack())
        xr = sbuf(s2, "xr", [P, 2, D])
        xr_last = sbuf(s2, "xr_last", [P, 2, D])
        islot = sbuf(s2, "islot", [P, 2, TOPK], I32)
        meta = sbuf(s2, "meta", [P, 2, TOPK, 2])
        xa = sbuf(s2, "xa", [P, 2, D])
        wq3 = sbuf(s2, "wq3", [P, KD, 384])
        wdq = sbuf(s2, "wdq", [P, 2, H1 * HQ])
        wdkv = sbuf(s2, "wdkv", [P, 2 * D])
        wo = sbuf(s2, "wo", [P, KD, D])
        gqb = sbuf(s2, "gqb", [P, QL])
        gkb = sbuf(s2, "gkb", [P, KVL])
        sd = ExitStack()
        xT1 = sbuf(sd, "xT1", [P, 2, KD, P])
        lat = sbuf(sd, "lat", [P, 2, 384])
        qct = xa
        qa = sbuf(sd, "qa", [P, 2, H1, HQ])
        ka = sbuf(sd, "ka", [P, 2, H1, HQ])
        rt1 = sbuf(sd, "rt1", [P, 8, RD])
        rt2 = sbuf(sd, "rt2", [P, 8, RD])
        va = sbuf(sd, "va", [P, 2, D])
        qT, kT = (wreg[0:HQ, c:c + 2 * H1 * P].rearrange("p (s h t) -> p s h t", s=2, h=H1)
                  for c in (2 * KD * SHF, 2 * KD * SHF + 2 * H1 * P))
        mx = sbuf(sd, "mx", [P, 2, H1])
        nmx = sbuf(sd, "nmx", [P, 2, H1])
        rs = sbuf(sd, "rs", [P, 2, H1])
        ri = sbuf(sd, "ri", [P, 2, H1])
        pb = sbuf(sd, "pb", [P, 2, 2, D])
        pT = sbuf(sd, "pT", [P, 2, 2, D])
        qa_rows = qa[:].rearrange("p s h w -> p s (h w)")
        ob, oT, scratch = (qa_rows[:, :, c * D:(c + 1) * D] for c in range(3))
        oT = oT.rearrange("p s (a b) -> p s a b", a=KD)
        ssd2 = sbuf(sd, "ssd2", [P, 2, 2])
        rr = sbuf(sd, "rr", [P, 2, 2])
        rv2 = sbuf(sd, "rv2", [P, 2, 2])
        sr = sd
        rwT = wreg[:, 2 * KD * SHF + 4 * H1 * P:2 * KD * SHF + 4 * H1 * P + KD * E].rearrange("p (k e) -> p k e", k=KD)
        rb = sbuf(sr, "rb", [P, E])
        x3T = sbuf(sr, "x3T", [P, 2, KD, P])
        lgt = sbuf(sr, "lgt", [P, 2, E])
        bia = sbuf(sr, "bia", [P, 2, E])
        ex = sbuf(sr, "ex", [P, 2, E])
        nlm = sbuf(sr, "nlm", [P, 2])
        top = sbuf(sr, "top", [P, 2, 8])
        topi = sbuf(sr, "topi", [P, 2, 8], U32)
        topf = sbuf(sr, "topf", [P, 2, TOPK])
        hot = rt2[:].rearrange("p (s k) e -> p s k e", s=2)
        hw, hp = (x3T[:].rearrange("p s k t -> p (s k t)")[:, c * 2 * TOPK * E:(c + 1) * 2 * TOPK * E]
                  .rearrange("p (s k e) -> p s k e", s=2, k=TOPK) for c in range(2))
        msk = sbuf(sr, "msk", [P, 2, E])
        cum = sbuf(sr, "cum", [P, 3, E])
        tk = sbuf(sr, "tk", [P, 6, 2, TOPK])
        tsum = sbuf(sr, "tsum", [P, 2, 2])
        sr.close()
        d_h = nc.dram_tensor("tab_h", [V, D], F32).ap()
        d_x = nc.dram_tensor("tab_x", [V, D], F32).ap()
        d_xg = nc.dram_tensor("slots_x", [E * CAP, D], F32).ap()
        d_meta = nc.dram_tensor("slots_meta", [E * CAP, 2], F32).ap()
        d_acc = nc.dram_tensor("acc", [2 * ACC, D], F32).ap()

        act_full, act_free = sem("act_full"), sem("act_free")
        dve_full, dve_free = sem("dve_full"), sem("dve_free")
        idle = {k: sem(f"idle_{k}") for k in ("pe", "act", "dve", "pool", "sp")}
        dve_step, act_step, pool_step = sem("dve_step"), sem("act_step"), sem("pool_step")
        phase_end = sem("phase_end")
        ld_0, ld_a, ld_b, ld_c, ld_d, ld_q, ld_r = (sem(f"ld_{x}") for x in "0abcdqr")
        var_ready, rstd_ready = sem("var_ready"), sem("rstd_ready")
        ms_ready = sem("ms_ready")
        x_ready = sem("x_ready")
        hraw_ready, dtin_ready, sp_ready, tab_ready, tab_stored = (
            sem(x) for x in ("hraw_ready", "dtin_ready", "sp_ready", "tab_ready", "tab_stored"))
        mhalf_ready, stab_ready = sem("mhalf_ready"), sem("stab_ready")
        xh_used = sem("xh_used")
        segr_ready = sem("segr_ready")
        g_ready, xd_ready, y_ready = sem("g_ready"), sem("xd_ready"), sem("y_ready")
        y_done = sem("y_done")
        qi_ld, xg_ld, hg_ld, qw_stored, we_ld, xe_ld, ya_ld = (
            [sem(f"{x}_{p}") for p in range(4 if x == "ya_in" else 2)]
            for x in ("qi_in", "xg_in", "hg_in", "qw_stored", "we_in", "xe_in", "ya_in"))
        wd_ld, xm_ld = ([sem(f"{x}_{p}") for p in range(2)] for x in ("wd_in", "xm_in"))
        qi_used, qm_ready, qt_ready, qw_ready = (
            sem(x) for x in ("qi_used", "qm_ready", "qt_ready", "qw_ready"))
        xhi_ready, h_ready, hi_ready, hT_ready, hT_used, down_full, down_free = (
            sem(x) for x in ("xhi_ready", "h_ready", "hi_ready", "hT_ready", "hT_used", "down_full", "down_free"))
        whi_ready, wlo_ready, dhi_ready, dlo_ready = (
            sem(x) for x in ("whi_ready", "wlo_ready", "dhi_ready", "dlo_ready"))
        zrow_ready, dram_init = sem("zrow_ready"), sem("dram_init")
        lat_in, lat_ready, rope_ready, mx_ready, o_ready = (
            sem(x) for x in ("lat_in", "lat_ready", "rope_ready", "mx_ready", "o_ready"))
        var3_ready, rstd3_ready, x3_ready, xr_free = (
            sem(x) for x in ("var3_ready", "rstd3_ready", "x3_ready", "xr_free"))
        nlm_ready, ex_ready, msk_ready, slot_ready, scattered = (
            sem(x) for x in ("nlm_ready", "ex_ready", "msk_ready", "slot_ready", "scattered"))
        we_used, he_ready, ye_ready, ye_free, acc_added = (
            sem(x) for x in ("we_used", "he_ready", "ye_ready", "ye_free", "acc_added"))
        fin_ready, out_stored = sem("fin_ready"), sem("out_stored")

        NLD_A = 9

        def bank(n):
            return psum[:, n, :]

        A_AB, V_AB = [0, 1, 2, 3], [4, 5, 6, 7]

        def barrier(e, k):
            e.drain().then_inc(phase_end, 1)
            e.wait_ge(phase_end, 5 * k)

        block = ctx.enter_context(nc.Block())

        A_B, V_B = 4, 2
        A_BN, V_BN = NG + 2, 2

        def ssd_rings(i, odd):
            if isinstance(i, int) and i == 0:
                a, v = 3, 1
                sa_, sv = 3, 1
            else:
                a, v = A_BN * i + 2, V_BN * i
                sa_, sv = 0 if odd else 2, 0
            return Ring(A_AB, A_B + a, sa_), Ring([4, 5], V_B + v, sv)

        def each_sequence(e, body):
            body(0, 0, True, False)
            with e.Fori(0, B // 2 - 1) as j:
                body(j, 1, False, False)
                body(j + 1, 0, False, False)
            body(B // 2 - 1, 1, False, True)
        A_C, V_C = A_B + B * A_BN, V_B + B * V_BN
        A_CN, V_CN = NF + 1, 4 + NF + 1
        A_D, V_D = A_C + 4 * A_CN, V_C + 4 * V_CN
        A_DN, V_DN, V_RN = 22, 6, 2
        A_S, V_S = A_D + B * A_DN, V_D + B * (V_DN + V_RN)

        def attention_rings(j):
            routed = 0 if isinstance(j, int) and j == 0 else j - 1
            early = 0 if isinstance(j, int) and j == B // 2 else 2
            return (Ring(A_AB, A_D + 3 * early + j * 2 * A_DN, early),
                    Ring(V_AB, V_D + early + j * 2 * V_DN + routed * 2 * V_RN, early))

        HEAD_STEPS = (("X", 0), ("S", 0), ("S", 1), ("C", 0), ("T", 0), ("S", 2), ("T", 1), ("V", 0), ("S", 3),
                      ("T", 2), ("V", 1), ("T", 3), ("V", 2), ("L", 0), ("V", 3))

        def ffn_base(g, n, experts, extra=4 * SHF // P):
            inner = min(max(g - 1, 0), 2) if isinstance(g, int) else g - 1
            return n * g + (extra * inner if experts else 0)

        def each_group(e, body):
            body(0, True, False)
            with e.Fori(1, 3) as g:
                body(g, False, False)
            body(3, False, True)

        def gate_and_up(x, width, f, m):
            for c in range(2):
                yield x[:, c * KD * width:(c + 1) * KD * width].rearrange("p (k n) -> p k n", k=KD)[:, :, f * P:f * P + m]

        def score_places(last):
            k, places = 4 + 16, {}
            for what, g in HEAD_STEPS:
                if what == "S":
                    places[g] = k
                if what in "ST" or what == "X" and not last:
                    k += 2
                elif what == "L" and not last:
                    k += 4
            return places
        NSH = SHF // P
        A_SN, V_SN = NSH, 4 + NSH
        NPG = 2 * NSH
        SC_G, SC_D = KD * SHF, 2 * KD * SHF
        NPAIR = E // 2
        @block.sync
        def _(e):
            W = lambda s, v: wait(e, idle["sp"], s, v)
            for dst, src in ((emb[:], a["emb"]), (cst[:], a["consts"]), (nw[:], a["nw"].partition_broadcast(P))):
                e.dma_start(dst, src).then_inc(ld_0, 16)
            e.dma_start(projT, a["projT"]).then_inc(ld_b, 16)
            for dst, src in ((outb[:], a["outb"].partition_broadcast(P)),
                             (bcdtT[:], a["bcdtT"]), (bcb[:], a["bcb"].partition_broadcast(P)),
                             (alog[:], a["alog"].partition_broadcast(P)),
                             (dskip[:], a["dskip"].partition_broadcast(P)),
                             (lutb[:], a["lut"].partition_broadcast(P)), (tokix[:], a["tokix"]),
                             (xtok[:], a["xtok"].partition_broadcast(P)), (owT[:], a["owT"])):
                e.dma_start(dst, src).then_inc(ld_a, 16)
            e.wait_ge(tab_ready, 2)
            e.dma_start(d_h, htabb[:]).then_inc(tab_stored, 16)
            e.dma_start(d_x, xtab[:]).then_inc(tab_stored, 16)
            barrier(e, 1)
            e.wait_ge(zrow_ready, 1)
            e.wait_ge(ld_a, 16 * NLD_A)
            def load(n, c):
                off = at(e, n * LUTN)
                if not (isinstance(n, int) and n < 2):
                    W(qi_used, n - 1)
                e.dma_start(qi[:, c, :], a["lutidx"][:, bass.ds(off, LUTN)]).then_inc(qi_ld[c], 16)

            def store(n, c):
                off, row = at(e, n * LUTN), at(e, n * P)
                e.dma_start(d_xg[bass.ds(row, P), :], zrow[:]).then_inc(dram_init, 16)
                e.dma_start(d_acc[bass.ds(row, P), :], zrow[:]).then_inc(dram_init, 16)
                W(qw_ready, n + 1)
                e.dma_start(wreg[:, bass.ds(off, LUTN)], qt[:, c, 0, :]).then_inc(qw_stored[c], 16)

            load(0, 0)
            load(1, 1)
            with e.Fori(0, NCHUNK // 2 - 1) as j:
                for c in range(2):
                    load(2 * j + 2 + c, c)
                    store(2 * j + c, c)
            store(NCHUNK - 2, 0)
            store(NCHUNK - 1, 1)
            e.dma_start(d_acc[NCHUNK * P:2 * ACC, :], zrow[:]).then_inc(dram_init, 16)
            e.dma_start(d_meta.rearrange("(n p) c -> p n c", p=P),
                        cst[:, C_META:C_N].rearrange("p (n c) -> p n c", c=2)).then_inc(dram_init, 16)
            e.wait_ge(dram_init, 16 * (2 * NCHUNK + 2))
            for c in range(2):
                e.wait_ge(qw_stored[c], 16 * NCHUNK // 2)
            barrier(e, 2)
            if stop != "B":
                barrier(e, 3)
                e.dma_start(wq3[:], a["wq3"]).then_inc(ld_q, 16)
                for dst, src in ((gqb[:], a["gq"].partition_broadcast(P)), (gkb[:], a["gkv"].partition_broadcast(P)),
                                 (wdq[:, 0, :], a["wdq"][0:P]), (wdq[0:QL - P, 1, :], a["wdq"][P:QL]),
                                 (wdkv[:], a["wdkv"]), (wo[:], a["wo"])):
                    e.dma_start(dst, src).then_inc(ld_d, 16)
                e.dma_start(rwT, a["rwT"]).then_inc(ld_r, 16)
                e.dma_start(rb[:], a["rb"].partition_broadcast(P)).then_inc(ld_r, 16)
                e.wait_ge(ld_d, 16 * 6)
                e.dma_start(wreg[:, 0:SC_D], a["shw"][:, 0:SC_D]).then_inc(ld_c, 16)
                e.wait_ge(ld_c, 16)
                e.wait_ge(ld_r, 32)
            if stop not in ("B", "C"):
                barrier(e, 4)
            if stop not in ("B", "C", "D"):
                e.dma_start(wreg[:, SC_D:3 * SHF * KD], a["shw"][:, SC_D:3 * SHF * KD]).then_inc(ld_c, 16)
                e.wait_ge(scattered, 32 * TOPK * B)
                def load_pair(n, q):
                    wrow, srow = (n * 2 * P, n * P) if isinstance(n, int) else (e.snap(n * 2 * P), e.snap(n * P))
                    w = a["wexp"][bass.ds(wrow, 2 * P), :].rearrange("(e p) n -> p e n", p=P)
                    later = not (isinstance(n, int) and n < 2)
                    if later:
                        W(he_ready, n - 1)
                    e.dma_start(xgE[:, q, :], d_xg[bass.ds(srow, P), :]).then_inc(xe_ld[q], 16)
                    e.dma_start(wE[:, q, :, 0:2 * D], w[:, :, 0:2 * D]).then_inc(we_ld[q], 16)
                    if later:
                        W(we_used, n - 1)
                    e.dma_start(wE[:, q, :, 2 * D:3 * D], w[:, :, 2 * D:3 * D]).then_inc(wd_ld[q], 16)
                    e.dma_start(xm[:, q, :], d_meta[bass.ds(srow, P), :]).then_inc(xm_ld[q], 16)

                load_pair(0, 0)
                load_pair(1, 1)
                with e.Fori(0, (NPAIR - 2) // 2) as j:
                    for q in range(2):
                        load_pair(2 * j + 2 + q, q)
                e.wait_ge(ye_free, 2 + NPAIR)
                out_v = out.rearrange("b t d -> (b t) d")

                def load_sums(n, c):
                    rows = [at(e, n * P + o * ACC) for o in range(2)]
                    for o in range(2):
                        e.dma_start(ya[:, c, o, :], d_acc[bass.ds(rows[o], P), :]).then_inc(ya_ld[c], 16)

                def store_sequence(n, ready):
                    i, row = at(e, n), at(e, n * P)
                    W(fin_ready, ready)
                    e.dma_start(out_v[bass.ds(row, P), :], hres[:, bass.ds(i, 1), :].rearrange("p a d -> p (a d)")).then_inc(out_stored, 16)

                for c in range(4):
                    load_sums(c, c)
                with e.Fori(0, 3) as j:
                    for c in range(4):
                        store_sequence(4 * j + c, 4 * j + c + 1)
                        load_sums(4 * j + 4 + c, c)
                for c in range(4):
                    store_sequence(B - 4 + c, B + c + 1)
                e.wait_ge(out_stored, 16 * B)
            else:
                e.dma_start(out.rearrange("b t d -> t b d"), hres[:]).then_inc(out_stored, 16)
                e.wait_ge(out_stored, 16)

        @block.gpsimd
        def _(e):
            W = lambda s, v: wait(e, idle["pool"], s, v)
            st = Steps(pool_step)

            def rsqrt(src, k, scale, eps, src_sem, src_val):
                W(src_sem, src_val)
                st.up(e.tensor_scalar(veps[:, k:k + 1], src, scale, eps, ALU.mult, ALU.add))
                W(pool_step, st.now())
                e.tensor_tensor(rstd[:, k:k + 1], veps[:, k:k + 1], mhalf[:], ALU.pow).then_inc(rstd_ready, 1)

            def gather(dst, tab, ix, s):
                e.indirect_dma_start(dst, None, tab, bass.IndirectOffsetOnAxis(ap=ix, axis=0)).then_inc(s, 16)

            e.memset(zrow[:], 0.0).then_inc(zrow_ready, 1)
            e.memset(mhalf[:], -0.5).then_inc(mhalf_ready, 1)
            e.wait_ge(mhalf_ready, 1)
            rsqrt(ssq[:, 0:1], 0, 1.0 / D, EPS_RMS, ms_ready, 1)
            rsqrt(ssq[:, 1:2], 1, 1.0 / D, EPS_RMS, ms_ready, 2)
            rsqrt(mv[:, 0, 1:2], 2, 1.0, EPS_LN, var_ready, 1)
            e.wait_ge(ld_a, 16 * NLD_A)
            e.wait_ge(tab_stored, 32)
            barrier(e, 1)
            def gather_rows(m, half, q, dst, tab, k, landed):
                ix = at(e, m)
                s = Steps(pool_step, 3 + 2 * m + k)
                s.up(e.tensor_copy(ixb[:, q, k:k + 1], tokix[:, bass.ds(ix, 1)]))
                W(pool_step, s.now())
                gather(dst[:, q, :], tab, ixb[:, q, k:k + 1], landed[q])

            def spans(m, g):
                ix = at(e, m)
                if not (isinstance(m, int) and m == 0 and g < 4):
                    W(g_ready, NG * m + g - 3)
                e.tensor_tensor(segr[:, g % 4, :, :],
                                small[:, bass.ds(ix, 1), H0 + HG * g:H0 + HG * g + HG].rearrange("p a h -> p (a h)").unsqueeze(2).to_broadcast([P, HG, P]),
                                cst[:, C_TRI:C_TRI + P].unsqueeze(1).to_broadcast([P, HG, P]),
                                ALU.mult).then_inc(segr_ready, 1)

            def by_head(x):
                return x.rearrange("p (h w) -> p h w", w=HP)

            def scale_x(m, half, q):
                ix = at(e, m)
                W(xg_ld[q], 16 * half + 16)
                e.tensor_tensor(by_head(xD[:, q, :]), by_head(xg[:, q, :]),
                                dskip[:].unsqueeze(2).to_broadcast([P, H0, HP]), ALU.mult)
                e.tensor_tensor(by_head(xdt[:, q, :]), by_head(xg[:, q, :]),
                                small[:, bass.ds(ix, 1), 0:H0].rearrange("p a h -> p (a h)").unsqueeze(2).to_broadcast([P, H0, HP]),
                                ALU.mult).then_inc(xd_ready, 1)

            gather_rows(0, 0, 0, xg, d_x, 0, xg_ld)
            gather_rows(0, 0, 0, hg, d_h, 1, hg_ld)
            for g in range(3):
                spans(0, g)
            scale_x(0, 0, 0)

            def step(j, odd, first, last):
                i = 2 * j + odd
                q, half = 1 - odd, j + odd
                if not last:
                    if not first:
                        W(xd_ready, i)
                    gather_rows(i + 1, half, q, xg, d_x, 0, xg_ld)
                for g in range(3, NG):
                    spans(i, g)
                if not last:
                    if not first:
                        W(xh_used, i)
                    scale_x(i + 1, half, q)
                    gather_rows(i + 1, half, q, hg, d_h, 1, hg_ld)
                    for g in range(3):
                        spans(i + 1, g)

            each_sequence(e, step)
            barrier(e, 2)
            if stop == "B":
                return
            base = 3 + 2 * B
            done = 3

            def ffn(base, seen_x, nf, experts):
                def powers_x(n, q):
                    s = Steps(pool_step, base + n)
                    W(var_ready, seen_x + n + 1)
                    s.up(e.tensor_scalar(veps[:, q:q + 1], mv[:, q, 1:2], 1.0, EPS_LN, ALU.mult, ALU.add))
                    W(pool_step, s.now())
                    e.tensor_tensor(rstd[:, q:q + 1], veps[:, q:q + 1], mhalf[:], ALU.pow).then_inc(rstd_ready, 1)

                for q in range(G4):
                    powers_x(q, q)
                if experts:
                    scatter_pair(B // 2 - 1, xr_last)

                def group(g, first, last):
                    for f in range(nf):
                        if f < G4 and not last:
                            powers_x(G4 * (g + 1) + f, f)
                        if experts and not first and not last:
                            for h in range(2):
                                n = NPG * (g - 1) + 2 * f + h
                                W(ye_ready, n + 1)
                                e.indirect_dma_start(d_acc, bass.IndirectOffsetOnAxis(ap=xix[:, h:h + 1], axis=0),
                                                     yE[:, h, :], None, compute_op=ALU.add).then_inc(acc_added, 16)
                                W(acc_added, 16 * (n + 1))
                                e.sem_inc(ye_free, 1)

                each_group(e, group)

            ffn(base, 1, NF, False)
            base += B
            barrier(e, 3)
            if stop == "C":
                return
            def powers(s, out, k, src, sem_in, v, sem_out, eps):
                W(sem_in, v)
                s.up(e.tensor_scalar(k, src, 1.0, eps, ALU.mult, ALU.add))
                W(pool_step, s.now())
                e.tensor_tensor(out, k, mhalf[:].to_broadcast([P, out.shape[-1]]), ALU.pow).then_inc(sem_out, 1)

            def scatter_pair(i, xr=xr):
                for p in range(2):
                    W(slot_ready, i + 1)
                    for k in range(TOPK):
                        for dst, src in ((d_xg, xr[:, p, :]), (d_meta, meta[:, p, k, :])):
                            e.indirect_dma_start(dst, bass.IndirectOffsetOnAxis(ap=islot[:, p, k:k + 1], axis=0),
                                                 src, None, bounds_check=E * CAP - 1,
                                                 oob_is_err=False).then_inc(scattered, 16)
                W(scattered, 32 * 2 * TOPK * (i + 1))
                e.sem_inc(xr_free, 1)

            def powers_x(s, n):
                for p in range(2):
                    powers(s, rstd[:, p:p + 1], veps[:, p:p + 1], mv[:, p, 1:2], var_ready,
                           1 + B + 2 * n + p + 1, rstd_ready, EPS_LN)

            def powers_latents(s, n):
                for p in range(2):
                    powers(s, rr[:, p, :], rv2[:, p, :], ssd2[:, p, :], ms_ready,
                           2 + 2 * n + p + 1, rstd_ready, EPS_RMS)

            NP = B // 2

            def attn(j, ahead, route, scatter):
                if isinstance(j, int):
                    first = {0: 4, NP: 6 * NP - 2}.get(j, 6 * j + 2)
                else:
                    first = 6 * j + 2
                s = Steps(pool_step, base + first)
                if ahead:
                    powers_x(s, j + 1)
                if route:
                    for p in (2, 3):
                        powers(s, rstd[:, p:p + 1], veps[:, p:p + 1], mv[:, p, 1:2], var3_ready,
                               2 * (j - 1) + p - 1, rstd3_ready, EPS_LN)
                if scatter:
                    scatter_pair(j - 2)
                if ahead:
                    powers_latents(s, j + 1)

            s = Steps(pool_step, base)
            powers_x(s, 0)
            powers_latents(s, 0)
            attn(0, True, False, False)
            attn(1, True, True, False)
            with e.Fori(2, NP - 1) as j:
                attn(j, True, True, True)
            attn(NP - 1, False, True, True)
            attn(NP, False, True, True)
            base += 3 * B
            barrier(e, 4)
            if stop == "D":
                return
            ffn(base, 1 + 2 * B, NSH, True)

        @block.tensor
        def _(e):
            W = lambda s, v: wait(e, idle["pe"], s, v)

            def fill(ring, free, depth):
                n, b = ring.take()
                W(free, n - depth + 1 + CREDIT)
                return n, psum[:, b, :]

            def turn(dst, src, w=P):
                return e.transpose(dst, src, ident[0:w, 0:w])

            ra, rv = Ring(A_AB), Ring(V_AB)
            e.wait_ge(ld_0, 48)
            e.wait_ge(x_ready, 1)
            n, ps = fill(ra, act_free, 4)
            for k in range(KD):
                t = turn(ps[:, k * P:(k + 1) * P], e1[:, k * P:(k + 1) * P])
            t.then_inc(act_full, 1)
            e.wait_ge(act_free, n + 1 + CREDIT)
            e.wait_ge(ld_b, 16)
            n, ps = fill(rv, dve_free, 4)
            for k in range(KD):
                t = e.matmul(ps, eT[:, k, :], projT[:, k, :], start=k == 0, stop=k == KD - 1)
            t.then_inc(dve_full, 1)
            e.wait_ge(x_ready, 2)
            n, ps = fill(ra, act_free, 4)
            for k in range(KD):
                t = turn(ps[:, k * P:(k + 1) * P], xtab[:, k * P:(k + 1) * P])
            t.then_inc(act_full, 1)
            e.wait_ge(act_free, n + 1 + CREDIT)
            e.wait_ge(ld_a, 16 * NLD_A)
            n, ps = fill(rv, dve_free, 4)
            for k in range(KD):
                t = e.matmul(ps[:, 0:160], xtT[:, k, :], bcdtT[:, k, :], start=k == 0, stop=k == KD - 1)
            t.then_inc(dve_full, 1)
            e.wait_ge(stab_ready, 1)
            for c in range(2):
                n, ps = fill(ra, act_free, 4)
                for i in range(B // 2):
                    m = c * B // 2 + i
                    t = e.matmul(ps[:, 2 * H0 * i:2 * H0 * (i + 1)], onehot[:, m * P:(m + 1) * P], stab[:], start=True, stop=True)
                t.then_inc(act_full, 1)
            barrier(e, 1)

            def sums(ra, m, g):
                W(segr_ready, NG * m + g + 1)
                n, ps = fill(ra, act_free, 4)
                e.matmul(ps, cst[:, C_GT:C_GT + P], segr[:, g % 4, :, :].rearrange("p a b -> p (a b)"),
                         start=True, stop=True).then_inc(act_full, 1)

            def b_and_c(ra, m):
                col = at(e, m * P)
                n, ps = fill(ra, act_free, 4)
                for c in range(2):
                    t = e.matmul(ps[0:N0, c * P:(c + 1) * P], bc[:, N0 * c:N0 * c + N0], onehot[:, bass.ds(col, P)],
                                 start=True, stop=True)
                t.then_inc(act_full, 1)
                return n

            def b_by_c(rv, q, copied):
                W(act_free, copied + 1 + CREDIT)
                n, ps = fill(rv, dve_free, 2)
                e.matmul(ps[:, 0:P], bct[:, q, 0:P], bct[:, q, P:2 * P], start=True, stop=True).then_inc(dve_full, 1)

            def turn_y(ra, i, q):
                W(y_ready, i + 1)
                n, ps = fill(ra, act_free, 4)
                for k in range(KD):
                    t = turn(ps[:, k * P:(k + 1) * P], xD[:, q, k * P:(k + 1) * P])
                t.then_inc(act_full, 1)
                return n

            def project_y(rv, q, copied):
                W(act_free, copied + 1 + CREDIT)
                n, ps = fill(rv, dve_free, 2)
                for k in range(KD):
                    t = e.matmul(ps, yT[:, q, k, :], owT[:, k, :], start=k == 0, stop=k == KD - 1)
                t.then_inc(dve_full, 1)

            ra = Ring(A_AB, A_B)
            n = b_and_c(ra, 0)
            sums(ra, 0, 0)
            sums(ra, 0, 1)
            b_by_c(Ring([4, 5], V_B), 0, n)

            def step(j, odd, first, last):
                i = 2 * j + odd
                ra, rv = ssd_rings(i, odd)
                for g in range(NG):
                    if g + 2 < NG:
                        sums(ra, i, g + 2)
                    elif not last:
                        sums(ra, i + 1, g + 2 - NG)
                    if g == 1 and not first:
                        turned = turn_y(ra, i - 1, 1 - odd)
                    if g == 2 and not first:
                        project_y(rv, 1 - odd, turned)
                    if g == 3 and not last:
                        copied = b_and_c(ra, i + 1)
                    if g == 5 and not last:
                        b_by_c(rv, 1 - odd, copied)
                    if g == 0:
                        W(xd_ready, i + 1)
                    W(g_ready, NG * i + g + 1)
                    for h in range(HG):
                        c = (HG * g + h) * HP
                        t = e.matmul(psum[:, 6 + odd, c:c + HP], lg[:, g % 4, h, :], xdt[:, odd, c:c + HP],
                                     start=True, stop=True)
                    t.then_inc(y_done, 1)

            each_sequence(e, step)
            turned = turn_y(Ring(A_AB, A_B + B * A_BN - 1, 3), B - 1, 1)
            project_y(Ring([4, 5], V_B + B * V_BN - 1, 1), 1, turned)
            barrier(e, 2)
            if stop == "B":
                return

            def split_product(out, lhs, rhs, first, last):
                for n, (x, y) in enumerate(((0, 0), (0, 1), (1, 0))):
                    t = e.matmul(out, lhs[x], rhs[y], start=first and n == 0, stop=last and n == 2)
                return t

            def ffn(base_a, base_v, na, nv, nf, seen, w, cols, rows, groups_before, xh, experts):
                c_up, c_down, width = cols
                split0 = NF if groups_before else 0

                def group(g, first, last):
                    ra = Ring([0, 1], base_a + ffn_base(g, na, experts))
                    rv = Ring([2, 3], base_v + ffn_base(g, nv, experts))
                    for q in range(G4):
                        W(x_ready, seen + g * G4 + q + 1)
                        n, ps = fill(rv, dve_free, 2)
                        for k in range(KD):
                            t = turn(ps[:, k * P:(k + 1) * P], xn[:, q, k * P:(k + 1) * P])
                        t.then_inc(dve_full, 1)
                    W(dve_free, n + 1 + CREDIT)
                    pairs = experts and not first and not last

                    def pair_turn(f, h):
                        W(xe_ld[h], 16 * (NSH * (g - 1) + f + 1))
                        n, ps = fill(ra, act_free, 2)
                        for k in range(KD):
                            t = turn(ps[:, k * P:(k + 1) * P], xgE[:, h, k * P:(k + 1) * P])
                        t.then_inc(act_full, 1)
                        return n

                    def pair_in(f, h, turned):
                        W(we_ld[h], 16 * (NSH * (g - 1) + f + 1))
                        W(act_free, turned + 1 + CREDIT)
                        for c, (ring, free, full) in enumerate(((ra, act_free, act_full), (rv, dve_free, dve_full))):
                            n, ps = fill(ring, free, 2)
                            for x in range(2):
                                for k in range(KD):
                                    t = e.matmul(ps[:, CAP * x:CAP * x + CAP],
                                                 wE[:, h, x, c * D + k * P:c * D + (k + 1) * P],
                                                 xgT[:, h, k, CAP * x:CAP * x + CAP], start=k == 0, stop=k == KD - 1)
                            t.then_inc(full, 1)

                    def pair_out(f, h):
                        W(wd_ld[h], 16 * (NSH * (g - 1) + f + 1))
                        W(he_ready, NPG * (g - 1) + 2 * f + h + 1)
                        n, ps = fill(rv, dve_free, 2)
                        for x in range(2):
                            r = slice(CAP * x, CAP * x + CAP)
                            t = e.matmul(ps[r, :], hE[:, h, r], wE[:, h, x, 2 * D:3 * D], start=True, stop=True)
                        t.then_inc(dve_full, 1)

                    def product_in(f, u):
                        m = rows(f)
                        if first:
                            e.wait_ge(wlo_ready, 2 * (split0 + f) + u + 1)
                        ring, free, full, c0 = ((ra, act_free, act_full, 0), (rv, dve_free, dve_full, c_up))[u]
                        n, ps = fill(ring, free, 2)
                        for k in range(KD):
                            c = c0 + k * width + f * P
                            t = split_product(ps[0:m, :], [x[:, c:c + m] for x in w],
                                              (xh[:, k, :], xlo[:, k, :]), k == 0, k == KD - 1)
                        t.then_inc(full, 1)

                    def product_out(f):
                        m = rows(f)
                        if f == 0:
                            W(down_free, (groups_before + g) * 4 + CREDIT)
                        if first:
                            e.wait_ge(dlo_ready, split0 + f + 1)
                        W(hT_ready, groups_before * NF + g * nf + f + 1)
                        c = c_down + f * D
                        for q in range(4):
                            z = slice(q * P, (q + 1) * P)
                            t = split_product(psum[:, 4 + q, :], [h[0:m, f % 2, z] for h in (hhi, hlo)],
                                              [x[0:m, c:c + D] for x in w], f == 0, f == nf - 1)
                        t.then_inc(hT_used, 1)

                    for f in range(nf):
                        product_in(f, 0)
                        if pairs:
                            turned = pair_turn(f, 0)
                        product_in(f, 1)
                        if pairs:
                            if f:
                                pair_out(f - 1, 1)
                            pair_in(f, 0, turned)
                            turned = pair_turn(f, 1)
                        if f:
                            product_out(f - 1)
                        if pairs:
                            pair_out(f, 0)
                            pair_in(f, 1, turned)
                    product_out(nf - 1)
                    e.drain().then_inc(down_full, 1)
                    if pairs:
                        pair_out(nf - 1, 1)
                    if not experts:
                        ra.take(), rv.take()
                        e.drain().then_inc(act_full, 1)
                        e.drain().then_inc(dve_full, 1)

                each_group(e, group)

            ffn(A_C, V_C, A_CN, V_CN, NF, 2, (whi, wlo), (KD * INTER, 2 * KD * INTER, INTER), rows0, 0, xhi, False)
            barrier(e, 3)
            if stop == "C":
                return


            def turn_x(ra, n, got):
                for p in range(2):
                    W(x_ready, 2 + B + 2 * n + p + 1)
                    got["x", p], ps = fill(ra, act_free, 4)
                    for k in range(KD):
                        t = turn(ps[:, k * P:(k + 1) * P], xa[:, p, k * P:(k + 1) * P])
                    t.then_inc(act_full, 1)

            def latents(rv, got):
                for p in range(2):
                    W(act_free, got["x", p] + 1 + CREDIT)
                    n, ps = fill(rv, dve_free, 4)
                    for k in range(KD):
                        t = e.matmul(ps[:, 0:384], xT1[:, p, k, :], wq3[:, k, :], start=k == 0, stop=k == KD - 1)
                    t.then_inc(dve_full, 1)

            def turn_latents(ra, n):
                for p in range(2):
                    W(lat_ready, 2 * n + p + 1)
                    m, ps = fill(ra, act_free, 4)
                    turn(ps[:, 0:P], lat[:, p, 0:P])
                    turn(ps[0:QL - P, P:2 * P], lat[:, p, P:QL]).then_inc(act_full, 1)
                    m, ps = fill(ra, act_free, 4)
                    turn(ps[:, 0:P], lat[:, p, QL:QL + KVL]).then_inc(act_full, 1)

            def attn(j, route, last):
                ra, rv = attention_rings(j)
                got = {}
                for p in range(2):
                    if p == 0:
                        W(act_free, ra.base + CREDIT)
                    for c, (ring, free, full) in enumerate(((ra, act_free, act_full), (rv, dve_free, dve_full),
                                                            (rv, dve_free, dve_full))):
                        n, ps = fill(ring, free, 4)
                        if c == 0:
                            got["qn", p] = n
                        z = slice(c * D, (c + 1) * D)
                        e.matmul(ps, qct[:, p, 0:P], wdq[:, 0, z], start=True, stop=False)
                        e.matmul(ps, qct[0:QL - P, p, P:2 * P], wdq[0:QL - P, 1, z],
                                 start=False, stop=True).then_inc(full, 1)
                    n, ps = fill(rv, dve_free, 4)
                    e.matmul(ps, qct[:, p, 2 * P:3 * P], wdkv[:, 0:D], start=True, stop=True).then_inc(dve_full, 1)
                    n, ps = fill(ra, act_free, 4)
                    e.matmul(ps, qct[:, p, 2 * P:3 * P], wdkv[:, D:2 * D], start=True, stop=True).then_inc(act_full, 1)
                for p in range(2):
                    for src, w in ((qa, 0), (ka, 1)):
                        for g in range(4):
                            if g == 0 and not w:
                                W(act_free, got["qn", p] + 1 + CREDIT)
                            if g == 0 or g == 2 and not w:
                                W(rope_ready, 3 * (2 * j + p) + (3 if w else g // 2 + 1))
                            n, ps = fill(ra, act_free, 4)
                            for h in range(4):
                                t = turn(ps[0:HQ, h * P:(h + 1) * P], src[:, p, 4 * g + h, :])
                            t.then_inc(act_full, 1)
                    got["kT", p] = n
                ob_ps = {}
                for what, g in HEAD_STEPS:
                    if what in "XCL":
                        if not last:
                            if what == "X":
                                turn_x(ra, j + 1, got)
                            elif what == "C":
                                latents(rv, got)
                            else:
                                turn_latents(ra, j + 1)
                        continue
                    if route and (what, g) == ("S", 2):
                        route_turn(rv, j - 1, got)
                    if route and (what, g) == ("V", 0):
                        route_logits(rv, got)
                    for p in range(2):
                        if what == "S":
                            if g == 0:
                                W(act_free, got["kT", p] + 1 + CREDIT)
                            got["S", p, g], ps = fill(ra, act_free, 4)
                            for h in range(4):
                                t = e.matmul(ps[:, h * P:(h + 1) * P], qT[:, p, 4 * g + h, :], kT[:, p, 4 * g + h, :],
                                             start=True, stop=True)
                            t.then_inc(act_full, 1)
                        elif what == "T":
                            W(act_free, got["S", p, g] + 1 + CREDIT)
                            got["T", p, g], ps = fill(ra, act_free, 4)
                            for h in range(4):
                                t = turn(ps[:, h * P:(h + 1) * P], pb[:, p, g % 2, h * P:(h + 1) * P])
                            t.then_inc(act_full, 1)
                        else:
                            W(act_free, got["T", p, g] + 1 + CREDIT)
                            if g == 0:
                                n, ob_ps[p] = fill(rv, dve_free, 4)
                            for h in range(4):
                                c = (4 * g + h) * HD
                                t = e.matmul(ob_ps[p][:, c:c + HD], pT[:, p, g % 2, h * P:(h + 1) * P],
                                             va[:, p, c:c + HD], start=True, stop=True)
                            if g == 3:
                                t.then_inc(dve_full, 1)
                if route:
                    route_places(rv, j - 1)
                for p in range(2):
                    W(o_ready, 2 * j + p + 1)
                    got["o", p], ps = fill(ra, act_free, 4)
                    for k in range(KD):
                        t = turn(ps[:, k * P:(k + 1) * P], ob[:, p, k * P:(k + 1) * P])
                    t.then_inc(act_full, 1)
                for p in range(2):
                    W(act_free, got["o", p] + 1 + CREDIT)
                    n, ps = fill(rv, dve_free, 4)
                    for k in range(KD):
                        t = e.matmul(ps, oT[:, p, k, :], wo[:, k, :], start=k == 0, stop=k == KD - 1)
                    t.then_inc(dve_full, 1)
                assert ra.k == 2 * A_DN - 6 * last, ra.k
                assert rv.k == 2 * V_DN - 2 * last + 2 * V_RN * route, rv.k

            def route_turn(rv, i, got, xr=xr):
                for p in range(2):
                    W(x3_ready, 2 * i + p + 1)
                    got["x3"], ps = fill(rv, dve_free, 4)
                    for k in range(KD):
                        t = turn(ps[:, k * P:(k + 1) * P], xr[:, p, k * P:(k + 1) * P])
                    t.then_inc(dve_full, 1)

            def route_logits(rv, got):
                W(dve_free, got["x3"] + 1 + CREDIT)
                n, ps = fill(rv, dve_free, 4)
                for p in range(2):
                    for k in range(KD):
                        t = e.matmul(ps[:, p * E:(p + 1) * E], x3T[:, p, k, :], rwT[:, k, :], start=k == 0, stop=k == KD - 1)
                t.then_inc(dve_full, 1)

            def route_places(rv, i):
                W(msk_ready, i + 1)
                n, ps = fill(rv, dve_free, 4)
                for p in range(2):
                    e.matmul(ps[:, p * E:(p + 1) * E], cst[:, C_STR:C_STR + P], msk[:, p, :], start=True, stop=False)
                    t = e.matmul(ps[:, p * E:(p + 1) * E], cst[:, C_ONE:C_ONE + P], cum[:, p, :], start=False, stop=True)
                t.then_inc(dve_full, 1)

            got = {}
            ra = Ring(A_AB, A_D)
            turn_x(ra, 0, got)
            e.wait_ge(ld_q, 16)
            latents(Ring(V_AB, V_D), got)
            turn_latents(ra, 0)
            e.wait_ge(ld_d, 16 * 6)
            e.wait_ge(ld_r, 32)
            attn(0, False, False)
            with e.Fori(1, B // 2 - 1) as j:
                attn(j, True, False)
            attn(B // 2 - 1, True, True)
            rv, got = attention_rings(B // 2)[1], {}
            route_turn(rv, B // 2 - 1, got, xr_last)
            route_logits(rv, got)
            route_places(rv, B // 2 - 1)
            barrier(e, 4)
            if stop == "D":
                return

            ffn(A_S, V_S, A_SN, V_SN, NSH, 2 + 2 * B, (shi, slo), (SC_G, SC_D, SHF), lambda f: P, 4, xhiS, True)

        @block.scalar
        def _(e):
            W = lambda s, v: wait(e, idle["act"], s, v)

            def drawn(ring):
                n, b = ring.take()
                W(act_full, n + 1)
                return psum[:, b, :]

            def give(ins):
                ins.then_inc(act_free, 1)

            def copy(dst, src):
                return e.activation(dst, src, ACT.Copy)

            e.sem_inc(act_free, CREDIT)
            e.wait_ge(ld_0, 48)
            ra = Ring(A_AB)
            e.activation(junk[:], emb[:], ACT.Square, accum_out=ssq[:, 0:1]).then_inc(ms_ready, 1)
            give(copy(eT[:].rearrange("p a b -> p (a b)"), drawn(ra)))
            e.wait_ge(hraw_ready, 1)
            e.wait_ge(ms_ready, 1)
            e.activation(junk[:], hraw[:], ACT.Square, accum_out=ssq[:, 1:2]).then_inc(ms_ready, 1)
            give(copy(xtT[:].rearrange("p a b -> p (a b)"), drawn(ra)))
            e.wait_ge(dtin_ready, 1)
            e.wait_ge(ld_a, 16 * NLD_A)
            e.activation(sp4[:, 1, :], sp4[:, 0, :], ACT.Exp).then_inc(act_step, 1)
            e.wait_ge(act_step, 1)
            e.activation(sp4[:, 2, :], sp4[:, 1, :], ACT.Ln, bias=1.0).then_inc(sp_ready, 1)
            e.activation(alog[:], alog[:], ACT.Exp).then_inc(sp_ready, 1)
            for c in range(2):
                give(copy(small[:, c * B // 2:(c + 1) * B // 2, :].rearrange("p a b -> p (a b)"), drawn(ra)))
            barrier(e, 1)

            def look(n, half, c, ts_, wait_stored):
                if ts_[0] == 0:
                    W(qm_ready, n + 1)
                    if wait_stored:
                        W(qw_stored[c], 16 * half)
                for t in ts_:
                    e.activation(qt[:, c, t, :], qm0[:, c, :], ACT.Identity, scale=lutd[:, t:t + 1],
                                 bias=lutb[:, 2 * t:2 * t + 1]).then_inc(qt_ready, 1)

            def decays(ra, g):
                give(e.activation(lg[:, g % 4, :, :].rearrange("p a b -> p (a b)"), drawn(ra), ACT.Exp))

            def copy_bc(ra, q):
                give(copy(bct[:, q, :], drawn(ra)[0:N0, 0:2 * P]))

            ra = Ring(A_AB, A_B)
            copy_bc(ra, 0)
            decays(ra, 0)
            decays(ra, 1)
            look(0, 0, 0, range(8), False)

            def step(j, odd, first, last):
                i = 2 * j + odd
                ra = ssd_rings(i, odd)[0]
                for g in range(NG):
                    if g + 2 < NG or not last:
                        decays(ra, (g + 2) % NG)
                    if g == 1 and not first:
                        give(copy(xdt[:, 1 - odd, :], drawn(ra)))
                    if g == 3 and not last:
                        copy_bc(ra, 1 - odd)
                    if g < 4:
                        look(2 * i + 1, i, 1, range(2 * g, 2 * g + 2), not first)
                    elif not last:
                        look(2 * i + 2, i + 1, 0, range(2 * g - 8, 2 * g - 6), True)

            each_sequence(e, step)
            give(copy(xdt[:, 1, :], drawn(Ring(A_AB, A_B + B * A_BN - 1, 3))))
            barrier(e, 2)
            if stop == "B":
                return

            def ffn(base_a, base_v, na, nv, nf, rows, width, groups_before, hi, xh, experts):
                def high(f):
                    for x, y in zip(gate_and_up(hi, width, f, rows(f)), gate_and_up(wreg, width, f, rows(f))):
                        copy(x, y).then_inc(whi_ready, 1)

                def high_down(f):
                    z = slice(2 * KD * width + f * D, 2 * KD * width + (f + 1) * D)
                    copy(hi[:, z], wreg[:, z]).then_inc(dhi_ready, 1)

                def group(g, first, last):
                    ra = Ring([0, 1], base_a + ffn_base(g, na, experts))
                    rv = Ring([2, 3], base_v + ffn_base(g, nv, experts))
                    if first:
                        high(0)
                        high(1)
                    for q in range(G4):
                        n, b = rv.take()
                        W(dve_full, n + 1)
                        copy(xh[:, :, q * P:(q + 1) * P], psum[:, b, :].rearrange("p (a b) -> p a b", a=KD)).then_inc(xhi_ready, 1)
                    done = groups_before * NF + g * nf
                    pairs = experts and not first and not last
                    for f in range(nf):
                        m = rows(f)
                        ps = drawn(ra)
                        if f >= 2:
                            W(hT_ready, done + f - 1)
                        e.activation(sg[0:m, f % 2, :], ps[0:m, :], ACT.Silu).then_inc(act_free, 1)
                        if pairs:
                            give(copy(xgT[:, 0, :, :].rearrange("p a b -> p (a b)"), drawn(ra)))
                        if first:
                            if experts and f == 0:
                                e.wait_ge(ld_c, 32)
                            high_down(f)
                            if f + 2 < nf:
                                high(f + 2)
                        W(h_ready, done + f + 1)
                        if f >= 2:
                            W(hT_used, done + f - 1)
                        copy(hhi[0:m, f % 2, :], sg[0:m, f % 2, :]).then_inc(hi_ready, 1)
                        if pairs:
                            e.activation(sgE[:, 0, :], drawn(ra)[:, 0:P], ACT.Silu).then_inc(act_free, 1)
                            give(copy(xgT[:, 1, :, :].rearrange("p a b -> p (a b)"), drawn(ra)))
                            e.activation(sgE[:, 1, :], drawn(ra)[:, 0:P], ACT.Silu).then_inc(act_free, 1)
                    if not experts:
                        e.drain().then_inc(act_free, 1)

                each_group(e, group)

            ffn(A_C, V_C, A_CN, V_CN, NF, rows0, INTER, 0, whi, xhi, False)
            barrier(e, 3)
            if stop == "C":
                return

            SC = float(HQ) ** -0.5

            def copy_x(ra):
                for p in range(2):
                    give(copy(xT1[:, p, :, :].rearrange("p a b -> p (a b)"), drawn(ra)))

            def mean_squares(n):
                for p in range(2):
                    W(lat_in, 2 * n + p + 1)
                    e.activation(scratch[:, p, 0:QL], lat[:, p, 0:QL], ACT.Square, scale=float(QL) ** -0.5,
                                 accum_out=ssd2[:, p, 0:1])
                    e.activation(scratch[:, p, QL:QL + KVL], lat[:, p, QL:QL + KVL], ACT.Square, scale=float(KVL) ** -0.5,
                                 accum_out=ssd2[:, p, 1:2]).then_inc(ms_ready, 1)

            def copy_latents(ra):
                for p in range(2):
                    ps = drawn(ra)
                    copy(qct[:, p, 0:P], ps[:, 0:P])
                    give(copy(qct[0:QL - P, p, P:2 * P], ps[0:QL - P, P:2 * P]))
                    give(copy(qct[:, p, 2 * P:3 * P], drawn(ra)[:, 0:P]))

            def attn(j, route, last):
                ra = attention_rings(j)[0]
                for p in range(2):
                    give(copy(qa[:, p, :, 0:HD], drawn(ra).rearrange("p (h w) -> p h w", w=HD)))
                    give(copy(va[:, p, :], drawn(ra)))
                for p in range(2):
                    for dst in (qT, kT):
                        for g in range(4):
                            give(copy(dst[:, p, 4 * g:4 * g + 4, :].rearrange("p a b -> p (a b)"), drawn(ra)[0:HQ, :]))
                for what, g in HEAD_STEPS:
                    if what in "XL" and not last:
                        (copy_x if what == "X" else copy_latents)(ra)
                    if (what, g) == ("S", 3) and not last:
                        mean_squares(j + 1)
                    if what not in "ST":
                        continue
                    for p in range(2):
                        ps = drawn(ra)
                        if what == "S":
                            W(mx_ready, (2 * j) * 4 + 2 * g + p + 1)
                            for h in range(4):
                                hh = 4 * g + h
                                t = e.activation(pb[:, p, g % 2, h * P:(h + 1) * P], ps[:, h * P:(h + 1) * P], ACT.Exp,
                                                 bias=nmx[:, p, hh:hh + 1], scale=SC, accum_out=rs[:, p, hh:hh + 1])
                            give(t)
                        else:
                            give(copy(pT[:, p, g % 2, :], ps))
                if route:
                    route_exp(j - 1)
                for p in range(2):
                    give(copy(oT[:, p, :, :].rearrange("p a b -> p (a b)"), drawn(ra)))

            def route_exp(i):
                W(nlm_ready, i + 1)
                for p in range(2):
                    e.activation(ex[:, p, :], lgt[:, p, :], ACT.Exp, bias=nlm[:, p:p + 1]).then_inc(ex_ready, 1)

            ra = Ring(A_AB, A_D)
            copy_x(ra)
            mean_squares(0)
            copy_latents(ra)
            attn(0, False, False)
            with e.Fori(1, B // 2 - 1) as j:
                attn(j, True, False)
            attn(B // 2 - 1, True, True)
            route_exp(B // 2 - 1)
            barrier(e, 4)
            if stop == "D":
                return

            e.wait_ge(ld_c, 16)
            ffn(A_S, V_S, A_SN, V_SN, NSH, lambda f: P, SHF, 4, shi, xhiS, True)

        @block.vector
        def _(e):
            W = lambda s, v: wait(e, idle["dve"], s, v)
            tt, ts, stt_ = e.tensor_tensor, e.tensor_scalar, e.scalar_tensor_tensor
            st = Steps(dve_step)

            def link(ins):
                v = st.up(ins)
                W(dve_step, v)

            def drawn(ring):
                n, b = ring.take()
                W(dve_full, n + 1)
                return psum[:, b, :]

            def give(ins):
                ins.then_inc(dve_free, 1)

            def spread(x, h, w):
                return x.unsqueeze(2).to_broadcast([x.shape[0], h, w])

            def stats(src, k):
                link(e.bn_stats(stat[:, k, 0:6], src))
                e.bn_aggr(mv[:, k, :], stat[:, k, 0:6]).then_inc(var_ready, 1)

            e.sem_inc(dve_free, CREDIT)
            e.sem_inc(down_free, CREDIT)
            e.sem_inc(xr_free, 1)
            e.wait_ge(ld_0, 48)
            rv = Ring(V_AB)
            e.wait_ge(rstd_ready, 1)
            stt_(e1[:], emb[:], rstd[:, 0:1], nw[:], ALU.mult, ALU.mult).then_inc(x_ready, 1)
            e.wait_ge(ld_a, 16 * NLD_A)
            tt(lutd[:], lutb[:].rearrange("p (a b) -> p a b", b=2)[:, :, 1], lutb[:].rearrange("p (a b) -> p a b", b=2)[:, :, 0],
               ALU.subtract)
            ts(onehot[:], xtok[:], cst[:, C_P:C_P + 1], None, ALU.is_equal)
            ps = drawn(rv)
            t = e.tensor_copy(hraw[:], ps)
            t.then_inc(hraw_ready, 1)
            e.wait_ge(hraw_ready, 1)
            e.sem_inc(dve_free, 1)
            e.wait_ge(rstd_ready, 2)
            link(ts(htab[:], hraw[:], rstd[:, 1:2], None, ALU.mult))
            tt(htabb[:], htab[:], outb[:], ALU.add).then_inc(tab_ready, 1)
            stats(htab[:], 0)
            e.wait_ge(var_ready, 1)
            e.wait_ge(rstd_ready, 3)
            t = ts(xtab[:], htab[:], mv[:, 0, 0:1], rstd[:, 2:3], ALU.subtract, ALU.mult)
            t.then_inc(x_ready, 1)
            e.wait_ge(x_ready, 2)
            e.drain().then_inc(tab_ready, 1)
            ps = drawn(rv)
            link(tt(bc[:], ps[:, 0:160], bcb[:], ALU.add))
            e.sem_inc(dve_free, 1)
            link(ts(sp4[:, 3, :], bc[:, 128:160], -1.0, None, ALU.mult))
            tt(sp4[:, 0, :], sp4[:, 3, :], bc[:, 128:160], ALU.min).then_inc(dtin_ready, 1)
            e.wait_ge(sp_ready, 2)
            link(stt_(stab[:, 0:H0], bc[:, 128:160], 0.0, sp4[:, 2, :], ALU.max, ALU.add))
            link(stt_(stab[:, H0:2 * H0], stab[:, 0:H0], -1.0, alog[:], ALU.mult, ALU.mult))
            e.sem_inc(stab_ready, 1)
            barrier(e, 1)
            base = st.now()
            stc = [st]

            def link(ins):
                v = stc[0].up(ins)
                W(dve_step, v)

            def low_bit(n, half, c):
                W(qi_ld[c], 16 * half + 16)
                ts(qm0[:, c, :], qi[:, c, :], 1, None, ALU.bitwise_and).then_inc(qm_ready, 1)

            def high_bits(c):
                for b in (3, 2, 1):
                    t = ts(qm[:, b - 1, :], qi[:, c, :], 1 << b, None, ALU.bitwise_and)
                link(t)
                e.sem_inc(qi_used, 1)

            def pick(n, c, part):
                if part == 0:
                    W(qt_ready, 8 * n + 8)
                for lv, w, ts_ in (((1, 1, (0, 2)),), ((1, 1, (4, 6)),), ((2, 2, (0, 4)), (3, 4, (0,))))[part]:
                    for t in ts_:
                        x = e.copy_predicated(qt[:, c, t, :], qm[:, lv - 1, :], qt[:, c, t + w, :])
                    if part:
                        link(x)
                if part == 2:
                    e.sem_inc(qw_ready, 1)

            def mask_bc(rv, q):
                link(tt(mm[:, q, :], drawn(rv)[:, 0:P], cst[:, C_TRI:C_TRI + P], ALU.mult))
                e.sem_inc(dve_free, 1)

            def add_y(i, q):
                W(y_done, NG * (i + 1))
                tt(xD[:, q, :], xD[:, q, :], psum[:, 6 + q, :], ALU.add).then_inc(y_ready, 1)

            def add_h(rv, i, half, q):
                ii = at(e, i)
                ps = drawn(rv)
                W(hg_ld[q], 16 * half + 16)
                link(tt(hres[:, bass.ds(ii, 1), :].rearrange("p a d -> p (a d)"), ps, hg[:, q, :], ALU.add))
                e.sem_inc(dve_free, 1)
                e.sem_inc(xh_used, 1)

            stc[0] = Steps(dve_step, base)
            low_bit(0, 0, 0)
            high_bits(0)
            mask_bc(Ring([4, 5], V_B), 0)

            def step(j, odd, first, last):
                i = 2 * j + odd
                stc[0] = Steps(dve_step, base + (2 if first else SSD_LINKS * i + 1))
                ra, rv = ssd_rings(i, odd)
                place = {0: -2, 1: -1}
                for g in range(2, NG):
                    place[g] = g - 2 + (g > 3 and not first) + (g > 5 and not last)
                for g in range(NG):
                    W(act_free, ra.base + place[g] + 1 + CREDIT)
                    tt(lg[:, g % 4, :, :], lg[:, g % 4, :, :], mm[:, odd, :].unsqueeze(1).to_broadcast([P, HG, P]),
                       ALU.mult).then_inc(g_ready, 1)
                    if g == 0:
                        if not first:
                            add_y(i - 1, 1 - odd)
                        low_bit(2 * i + 1, i, 1)
                    if g in (1, 2, 3):
                        pick(2 * i, 0, g - 1)
                    if g == 4:
                        if not first:
                            add_h(rv, i - 1, j + odd - 1, 1 - odd)
                        high_bits(1)
                        if not last:
                            low_bit(2 * i + 2, i + 1, 0)
                    if g in (5, 6, 7):
                        pick(2 * i + 1, 1, g - 5)
                    if g == 6 and not last:
                        mask_bc(rv, 1 - odd)
                    if g == 7 and not last:
                        high_bits(0)
                assert stc[0].k == SSD_LINKS - first - 2 * last, stc[0].k

            each_sequence(e, step)
            stc[0] = Steps(dve_step, base + B * SSD_LINKS - 1)
            add_y(B - 1, 1)
            add_h(Ring([4, 5], V_B + B * V_BN - 1, 1), B - 1, B // 2 - 1, 1)
            base += B * SSD_LINKS
            barrier(e, 2)
            if stop == "B":
                return

            def ffn(base, base_v, nv, nf, seen_x, seen_r, rows, width, groups_before, base_a, na, hi, lo, xh, experts, links):
                split0 = NF if groups_before else 0

                def low(f):
                    parts = zip(*(gate_and_up(x, width, f, rows(f)) for x in (lo, wreg, hi)))
                    for c, (x, y, z) in enumerate(parts):
                        e.wait_ge(whi_ready, 2 * (split0 + f) + c + 1)
                        tt(x, y, z, ALU.subtract).then_inc(wlo_ready, 1)

                def low_down(f):
                    z = slice(2 * KD * width + f * D, 2 * KD * width + (f + 1) * D)
                    e.wait_ge(dhi_ready, split0 + f + 1)
                    tt(lo[:, z], wreg[:, z], hi[:, z], ALU.subtract).then_inc(dlo_ready, 1)

                def row(g, q):
                    return hres[:, bass.ds(at(e, g * G4 + q), 1), :].rearrange("p a d -> p (a d)")

                def norm_stats(g, q):
                    link(e.bn_stats(stat[:, q, 0:6], row(g, q)))
                    e.bn_aggr(mv[:, q, :], stat[:, q, 0:6]).then_inc(var_ready, 1)

                def norm_x(g, q):
                    W(rstd_ready, seen_r + g * G4 + q + 1)
                    W(var_ready, seen_x + g * G4 + q + 1)
                    ts(xn[:, q, :], row(g, q), mv[:, q, 0:1], rstd[:, q:q + 1],
                       ALU.subtract, ALU.mult).then_inc(x_ready, 1)

                def add_down(g):
                    W(down_full, groups_before + g + 1)
                    for q in range(G4):
                        link(tt(row(g, q), psum[:, 4 + q, :], row(g, q), ALU.add))
                        e.sem_inc(down_free, 1)
                        if experts and isinstance(g, int) and g == 3:
                            e.sem_inc(fin_ready, 1)

                def results(rv, h, n, round_):
                    ps = drawn(rv)
                    W(ye_free, n + 1)
                    W(xm_ld[h], 16 * round_ + 16)
                    ts(xix[:, h:h + 1], xm[:, h, 1:2], cst[:, C_ODD:C_ODD + 1], None, ALU.add)
                    link(ts(yE[:, h, :], ps, xm[:, h, 0:1], None, ALU.mult))
                    e.sem_inc(dve_free, 1)
                    e.sem_inc(ye_ready, 1)
                    e.sem_inc(we_used, 1)

                stc[0] = Steps(dve_step, base)
                for q in range(G4):
                    norm_stats(0, q)
                for q in range(G4):
                    norm_x(0, q)

                def group(g, first, last):
                    stc[0] = Steps(dve_step, base + (G4 if first else ffn_base(g, links, experts, 2 * NPG)))
                    rv = Ring([2, 3], base_v + ffn_base(g, nv, experts))
                    if first:
                        low(0)
                        low(1)
                    for q in range(G4):
                        lower_x(rv, g, q, groups_before, xh)
                    if not first:
                        add_down(g - 1)
                    done = groups_before * NF + g * nf
                    pairs = experts and not first and not last
                    a0 = base_a + ffn_base(g, na, experts)
                    per = 5 if pairs else 1

                    def n_pair(f, h):
                        return NPG * (g - 1) + 2 * f + h

                    def pair_h(f, h):
                        ps = drawn(rv)
                        W(act_free, a0 + per * f + 2 * h + 2 + 1 + CREDIT)
                        link(tt(hE[:, h, :], sgE[:, h, :], ps[:, 0:P], ALU.mult))
                        e.sem_inc(dve_free, 1)
                        e.sem_inc(he_ready, 1)

                    for f in range(nf):
                        m = rows(f)
                        ps = drawn(rv)
                        W(act_free, a0 + per * f + 1 + CREDIT)
                        tt(sg[0:m, f % 2, :], sg[0:m, f % 2, :], ps[0:m, :], ALU.mult).then_inc(h_ready, 1)
                        W(h_ready, done + f + 1)
                        e.sem_inc(dve_free, 1)
                        if pairs and f:
                            results(rv, 1, n_pair(f - 1, 1), NSH * (g - 1) + f - 1)
                        W(hi_ready, done + f + 1)
                        tt(hlo[0:m, f % 2, :], sg[0:m, f % 2, :], hhi[0:m, f % 2, :], ALU.subtract).then_inc(hT_ready, 1)
                        if first:
                            low_down(f)
                            if f + 2 < nf:
                                low(f + 2)
                        if pairs:
                            pair_h(f, 0)
                            results(rv, 0, n_pair(f, 0), NSH * (g - 1) + f)
                            pair_h(f, 1)
                        if not last and f < G4:
                            norm_stats(g + 1, f)
                        if not last and 1 <= f <= G4:
                            norm_x(g + 1, f - 1)
                        if experts and last:
                            for n in (2 * f, 2 * f + 1):
                                e.wait_ge(ya_ld[n % 4], 32 * (n // 4 + 1))
                                x = row(0, n)
                                link(tt(x, x, ya[:, n % 4, 0, :], ALU.add))
                                link(tt(x, x, ya[:, n % 4, 1, :], ALU.add))
                                e.sem_inc(fin_ready, 1)
                    if pairs:
                        results(rv, 1, n_pair(nf - 1, 1), NSH * (g - 1) + nf - 1)
                    if not experts:
                        e.drain().then_inc(dve_free, 1)
                    if last:
                        add_down(g)

                each_group(e, group)

            def lower_x(rv, g, q, groups_before, xh):
                ps = drawn(rv)
                W(xhi_ready, (groups_before + g) * 4 + q + 1)
                give(tt(xlo[:, :, q * P:(q + 1) * P], ps.rearrange("p (a b) -> p a b", a=KD),
                        xh[:, :, q * P:(q + 1) * P], ALU.subtract))

            ffn(base, V_C, V_CN, NF, 1, 3, rows0, INTER, 0, A_C, A_CN, whi, wlo, xhi, False, FFN_LINKS)
            base += 4 * FFN_LINKS
            barrier(e, 3)
            if stop == "C":
                return
            stc[0] = Steps(dve_step, base)
            link(e.memset(cum[:, 0, :], 0.0))
            base += 1
            iota = cst[:, C_IOTA:C_IOTA + E]
            cos = cst[:, C_COS:C_COS + RD]
            sin = cst[:, C_SIN:C_SIN + RD]
            HR = RD // 2

            RB = 3 + B

            def norm_stats(n):
                for p in range(2):
                    ii = at(e, 2 * n + p)
                    hrow = hres[:, bass.ds(ii, 1), :].rearrange("p a d -> p (a d)")
                    link(e.bn_stats(stat[:, p, 0:6], hrow))
                    e.bn_aggr(mv[:, p, :], stat[:, p, 0:6]).then_inc(var_ready, 1)

            def norm_x(n):
                for p in range(2):
                    ii = at(e, 2 * n + p)
                    hrow = hres[:, bass.ds(ii, 1), :].rearrange("p a d -> p (a d)")
                    W(rstd_ready, RB + 4 * n + p + 1)
                    W(var_ready, 1 + B + 2 * n + p + 1)
                    ts(xa[:, p, :], hrow, mv[:, p, 0:1], rstd[:, p:p + 1], ALU.subtract, ALU.mult).then_inc(x_ready, 1)

            def latents(rv):
                for p in range(2):
                    ps = drawn(rv)
                    link(e.tensor_copy(lat[:, p, :], ps[:, 0:384]))
                    e.sem_inc(lat_in, 1)
                    e.sem_inc(dve_free, 1)
                for p in range(2):
                    tt(rt1[:, p, :], lat[:, p, 320:384], cos, ALU.mult)
                    tt(rt2[:, p, 0:HR], lat[:, p, 320 + HR:384], sin[:, 0:HR], ALU.mult)
                    t = tt(rt2[:, p, HR:RD], lat[:, p, 320:320 + HR], sin[:, HR:RD], ALU.mult)
                link(t)
                link(tt(rt1[:, 0:2, :], rt1[:, 0:2, :], rt2[:, 0:2, :], ALU.add))
                for p in range(2):
                    t = e.tensor_copy(ka[:, p, :, HD:HQ], rt1[:, p, :].unsqueeze(1).to_broadcast([P, H1, RD]))
                link(t)

            def norm_latents(n):
                for p in range(2):
                    W(rstd_ready, RB + 4 * n + 2 + p + 1)
                    stt_(lat[:, p, 0:QL], lat[:, p, 0:QL], rr[:, p, 0:1], gqb[:], ALU.mult, ALU.mult)
                    stt_(lat[:, p, QL:QL + KVL], lat[:, p, QL:QL + KVL], rr[:, p, 1:2], gkb[:],
                         ALU.mult, ALU.mult).then_inc(lat_ready, 1)

            def attn(j, route, last):
                first = isinstance(j, int) and j == 0
                stc[0] = Steps(dve_step, base + (D_AHEAD if first else D_AHEAD + D_PERIOD + (j - 1) * (D_PERIOD + R_PERIOD)))
                ra, rv = attention_rings(j)
                i = j - 1
                if not last:
                    norm_stats(j + 1)
                if route:
                    route_stats(i)
                for p in range(2):
                    for g in range(2):
                        ps = drawn(rv).rearrange("p (h w) -> p h w", w=RD)
                        tt(rt1[:], ps, cos.unsqueeze(1).to_broadcast([P, 8, RD]), ALU.mult)
                        tt(rt2[:, :, 0:HR], ps[:, :, HR:RD], sin[:, 0:HR].unsqueeze(1).to_broadcast([P, 8, HR]), ALU.mult)
                        link(tt(rt2[:, :, HR:RD], ps[:, :, 0:HR], sin[:, HR:RD].unsqueeze(1).to_broadcast([P, 8, HR]), ALU.mult))
                        e.sem_inc(dve_free, 1)
                        link(tt(qa[:, p, 8 * g:8 * g + 8, HD:HQ], rt1[:], rt2[:], ALU.add))
                        e.sem_inc(rope_ready, 1)
                    ps = drawn(rv)
                    link(e.tensor_copy(ka[:, p, :, 0:HD], ps.rearrange("p (h w) -> p h w", w=HD)))
                    e.sem_inc(dve_free, 1)
                    e.sem_inc(rope_ready, 1)
                if not last:
                    W(act_full, ra.base + 4)
                    norm_x(j + 1)
                s_at = score_places(last)
                for g in range(4):
                    for p in range(2):
                        k = s_at[g] + p
                        W(act_full, ra.base + k + 1)
                        ps = psum[:, A_AB[(k + ra.shift) % 4], :]
                        link(e.tensor_reduce(mx[:, p, 4 * g:4 * g + 4], ps.rearrange("p (h w) -> p h w", w=P), AX.X, ALU.max))
                        ts(nmx[:, p, 4 * g:4 * g + 4], mx[:, p, 4 * g:4 * g + 4], -float(HQ) ** -0.5, None, ALU.mult).then_inc(mx_ready, 1)
                    if g == 1:
                        if route:
                            W(xr_free, i + 1)
                            route_x(i)
                        if not last:
                            latents(rv)
                        if route:
                            route_turned(rv)
                    if g == 3 and not last:
                        norm_latents(j + 1)
                    if route and g >= 2:
                        route_choose(rv, g - 2)
                    if route and g == 3:
                        route_choose(rv, 2)
                for p in range(2):
                    W(act_free, ra.base + s_at[3] + p + 1 + CREDIT)
                    link(e.reciprocal(ri[:, p, :], rs[:, p, :]))
                    ps = drawn(rv)
                    link(tt(ob[:, p, :].rearrange("p (h w) -> p h w", w=HD), ps.rearrange("p (h w) -> p h w", w=HD),
                            spread(ri[:, p, :], H1, HD), ALU.mult))
                    e.sem_inc(dve_free, 1)
                    e.sem_inc(o_ready, 1)
                if route:
                    route_slots(rv, i)
                for p in range(2):
                    ii = at(e, 2 * j + p)
                    hrow = hres[:, bass.ds(ii, 1), :].rearrange("p a d -> p (a d)")
                    ps = drawn(rv)
                    link(tt(hrow, ps, hrow, ALU.add))
                    e.sem_inc(dve_free, 1)
                assert stc[0].k == D_PERIOD + (R_PERIOD if route else 0) - (D_AHEAD if last else 0), (stc[0].k, route)

            def route_stats(i):
                for p in range(2):
                    ii = at(e, 2 * i + p)
                    hrow = hres[:, bass.ds(ii, 1), :].rearrange("p a d -> p (a d)")
                    link(e.bn_stats(stat[:, 2 + p, 0:6], hrow))
                    e.bn_aggr(mv[:, 2 + p, :], stat[:, 2 + p, 0:6]).then_inc(var3_ready, 1)

            def route_x(i, xr=xr):
                for p in range(2):
                    ii = at(e, 2 * i + p)
                    hrow = hres[:, bass.ds(ii, 1), :].rearrange("p a d -> p (a d)")
                    W(rstd3_ready, 2 * i + p + 1)
                    W(var3_ready, 2 * i + p + 1)
                    ts(xr[:, p, :], hrow, mv[:, 2 + p, 0:1], rstd[:, 2 + p:3 + p], ALU.subtract, ALU.mult).then_inc(x3_ready, 1)

            def route_turned(rv):
                for p in range(2):
                    ps = drawn(rv)
                    give(e.tensor_copy(x3T[:, p, :, :].rearrange("p a b -> p (a b)"), ps))

            def route_choose(rv, part):
                if part == 0:
                    ps = drawn(rv)[:, 0:2 * E].rearrange("p (s e) -> p s e", s=2)
                    e.tensor_copy(lgt[:], ps)
                    link(tt(bia[:], ps, rb[:].unsqueeze(1).to_broadcast([P, 2, E]), ALU.add))
                    e.sem_inc(dve_free, 1)
                    link(e.tensor_reduce(nlm[:], lgt[:], AX.X, ALU.max, negate=True))
                    e.sem_inc(nlm_ready, 1)
                    e.max(top[:, 0, :], bia[:, 0, :])
                    link(e.max(top[:, 1, :], bia[:, 1, :]))
                elif part == 1:
                    e.max_index(topi[:, 0, :], top[:, 0, :], bia[:, 0, :])
                    link(e.max_index(topi[:, 1, :], top[:, 1, :], bia[:, 1, :]))
                    link(e.tensor_copy(topf[:], topi[:, :, 0:TOPK]))
                    for p in range(2):
                        t = tt(hot[:, p, :, :], iota.unsqueeze(1).to_broadcast([P, TOPK, E]), spread(topf[:, p, :], TOPK, E), ALU.is_equal)
                    link(t)
                else:
                    for p in range(2):
                        t = e.tensor_reduce(msk[:, p, :], hot[:, p, :, :].rearrange("p k e -> p e k"), AX.X, ALU.add)
                    link(t)
                    link(tt(cum[:, 1, :], cum[:, 0, :], msk[:, 0, :], ALU.add))
                    e.sem_inc(msk_ready, 1)
                    link(tt(cum[:, 2, :], cum[:, 1, :], msk[:, 1, :], ALU.add))

            def route_slots(rv, i):
                ti = at(e, 2 * i + C_TOK)
                W(ex_ready, 2 * i + 2)
                for p in range(2):
                    t = tt(hw[:, p, :, :], hot[:, p, :, :], ex[:, p, :].unsqueeze(1).to_broadcast([P, TOPK, E]), ALU.mult)
                ps = drawn(rv)
                for p in range(2):
                    t = tt(hp[:, p, :, :], hot[:, p, :, :], ps[:, p * E:(p + 1) * E].unsqueeze(1).to_broadcast([P, TOPK, E]), ALU.mult)
                link(t)
                e.sem_inc(dve_free, 1)
                e.tensor_copy(cum[:, 0, :], cum[:, 2, :])
                e.tensor_reduce(tk[:, 0, :, :], hw, AX.X, ALU.add)
                link(e.tensor_reduce(tk[:, 1, :, :], hp, AX.X, ALU.add))
                e.tensor_reduce(tsum[:, :, 0], tk[:, 0, :, :], AX.X, ALU.add)
                ts(tk[:, 2, :, :], tk[:, 1, :, :], float(CAP), None, ALU.is_lt)
                link(stt_(tk[:, 3, :, :], topf[:], float(CAP), tk[:, 1, :, :], ALU.mult, ALU.add))
                e.reciprocal(tsum[:, :, 1], tsum[:, :, 0])
                tt(tk[:, 4, :, :], tk[:, 3, :, :], tk[:, 2, :, :], ALU.mult)
                link(ts(tk[:, 5, :, :], tk[:, 2, :, :], -2.0 * E * CAP, 2.0 * E * CAP, ALU.mult, ALU.add))
                tt(meta[:, :, :, 0], tk[:, 0, :, :], spread(tsum[:, :, 1], 2, TOPK), ALU.mult)
                e.tensor_copy(meta[:, :, :, 1], spread(cst[:, bass.ds(ti, 2)], 2, TOPK))
                link(tt(islot[:], tk[:, 4, :, :], tk[:, 5, :, :], ALU.add))
                e.sem_inc(slot_ready, 1)

            stc[0] = Steps(dve_step, base)
            norm_stats(0)
            norm_x(0)
            latents(Ring(V_AB, V_D))
            e.wait_ge(ld_d, 16 * 6)
            e.wait_ge(ld_r, 32)
            norm_latents(0)
            assert stc[0].k == D_AHEAD, stc[0].k
            attn(0, False, False)
            with e.Fori(1, B // 2 - 1) as j:
                attn(j, True, False)
            attn(B // 2 - 1, True, True)
            base += B // 2 * (D_PERIOD + R_PERIOD) - R_PERIOD
            stc[0] = Steps(dve_step, base)
            i, rv = B // 2 - 1, attention_rings(B // 2)[1]
            route_stats(i)
            route_x(i, xr_last)
            route_turned(rv)
            for part in range(3):
                route_choose(rv, part)
            W(xr_free, i + 1)
            route_slots(rv, i)
            assert stc[0].k == R_PERIOD, stc[0].k
            base += R_PERIOD
            barrier(e, 4)
            if stop == "D":
                return

            e.sem_inc(ye_free, 2)
            ffn(base, V_S, V_SN, NSH, 1 + 2 * B, 3 + 3 * B, lambda f: P, SHF, 4, A_S, A_SN, shi, slo, xhiS, True, FFN_LINKS)


def rows0(f):
    return P if f < NF - 1 else INTER - (NF - 1) * P


SSD_LINKS = 10
FFN_LINKS = 8
D_AHEAD = 7
D_PERIOD = 31
R_PERIOD = 16


def constants():
    import numpy as np
    c = np.zeros((P, C_N), np.float32)
    k, m = np.arange(P)[:, None], np.arange(P)[None, :]
    c[:, C_ID:C_ID + P] = k == m
    c[:, C_GT:C_GT + P] = k > m
    c[:, C_STR:C_STR + P] = k < m
    c[:, C_ONE:C_ONE + P] = 1.0
    c[:, C_TRI:C_TRI + P] = k <= m
    c[:, C_IOTA:C_IOTA + E] = m[:, :E]
    inv = np.float32(1.0) / np.float32(10000.0) ** (np.arange(0, RD, 2, dtype=np.float32) / np.float32(RD))
    ang = np.arange(P, dtype=np.float32)[:, None] * inv[None, :]
    c[:, C_COS:C_COS + RD] = np.concatenate([np.cos(ang)] * 2, 1)
    c[:, C_SIN:C_SIN + RD] = np.concatenate([-np.sin(ang), np.sin(ang)], 1)
    c[:, C_P] = np.arange(P)
    c[:, C_TOK:C_TOK + B] = np.arange(B)[None, :] * P + k
    c[:, C_ODD] = np.arange(P) // CAP * ACC
    c[:, C_META + 1::2] = B * P + k % CAP
    return c


def arrange(x):
    import numpy as np
    x = {k: np.asarray(v) for k, v in x.items()}

    def tiles(w):
        return np.ascontiguousarray(w.reshape(-1, P, w.shape[1]).transpose(1, 0, 2))

    o = {"consts": constants()}
    tok = x["x"]
    o["tokix"], o["xtok"] = np.ascontiguousarray(tok.T), tok.reshape(-1)
    o["emb"], o["nw"] = x["L0_tok_emb_table"], x["L0_tok_norm_weight"]
    o["projT"] = tiles(x["L0_tok_proj_weight"].T)
    o["bcdtT"] = tiles(np.concatenate([x["L0_attn_B_w"], x["L0_attn_C_w"], x["L0_attn_dt_w"]], 0).T)
    o["bcb"] = np.concatenate([x["L0_attn_B_b"], x["L0_attn_C_b"], x["L0_attn_dt_b"]])
    o["alog"], o["dskip"] = x["L0_attn_A_log"], x["L0_attn_D"]
    o["owT"], o["outb"] = tiles(x["L0_attn_out_w"].T), x["L0_attn_out_b"]
    o["lut"] = x["L0_ffn_lut"]
    down = np.zeros((NF * P, D), np.int32)
    down[:INTER] = x["L0_ffn_down_idx"].T
    o["lutidx"] = np.concatenate([tiles(w).reshape(P, -1) for w in
                                  (x["L0_ffn_gate_idx"].T, x["L0_ffn_up_idx"].T, down)], 1)
    o["wq3"] = tiles(np.concatenate([x["L1_attn_Wcq"], x["L1_attn_Wckv"], x["L1_attn_Wkr"]], 1))
    o["wdq"] = np.concatenate([x["L1_attn_Wdq"], x["L1_attn_Wdqr"]], 1)
    o["wdkv"] = np.concatenate([x["L1_attn_Wdk"], x["L1_attn_Wdv"]], 1)
    o["wo"] = tiles(x["L1_attn_Wo"])
    o["gq"], o["gkv"] = x["L1_attn_g_q"], x["L1_attn_g_kv"]
    o["rwT"], o["rb"] = tiles(x["L1_ffn_router_w"].T), x["L1_ffn_router_bias"]
    sg, su, sd = x["L1_ffn_sh_gate_w"], x["L1_ffn_sh_up_w"], x["L1_ffn_sh_down_w"]
    o["shw"] = np.concatenate([tiles(w).reshape(P, -1) for w in
                               (sg.reshape(SHF, D).T, su.reshape(SHF, D).T, sd.transpose(0, 2, 1).reshape(SHF, D))], 1)

    def expert(w):
        return w.transpose(0, 2, 1).reshape(E, KD, P, F).transpose(0, 2, 1, 3).reshape(E, P, KD * F)

    o["wexp"] = np.concatenate([expert(x["L1_ffn_gate_w"]), expert(x["L1_ffn_up_w"]),
                                x["L1_ffn_down_w"].transpose(0, 2, 1)], 2).reshape(E * P, 3 * D)
    return {k: np.ascontiguousarray(v) for k, v in o.items()}


def kernel(**inputs):
    import concourse.bacc as bacc
    from concourse.bass_utils import run_bass_kernel_spmd

    arrays = arrange(inputs)
    nc = bacc.Bacc("TRN2", target_bir_lowering=False, num_devices=1)
    a = {k: nc.dram_tensor(f"in_{k}", v.shape, mybir.dt.from_np(v.dtype), kind="ExternalInput").ap()
         for k, v in arrays.items()}
    out = nc.dram_tensor("out_h", (B, P, D), F32, kind="ExternalOutput").ap()
    tower(nc, a, out)
    r = run_bass_kernel_spmd(nc, [{f"in_{k}": v for k, v in arrays.items()}], core_ids=[0])
    return r.results[0]["out_h"]
```
